# Optimizing a Trainium2 kernel written in Bass

```python
import numpy as np
import jax
import jax.numpy as jnp

def _softmax(x, axis=-1):
    return jax.nn.softmax(x, axis=axis)

def _gelu(x):
    return jax.nn.gelu(x, approximate=True)

def _silu(x):
    return jax.nn.silu(x)

def _sigmoid(x):
    return jax.nn.sigmoid(x)

def _layernorm(x, axis=-1, eps=1e-05):
    m = jnp.mean(x, axis=axis, keepdims=True)
    v = jnp.var(x, axis=axis, keepdims=True)
    return (x - m) / jnp.sqrt(v + eps)

def _scatter_add(tgt, idx, src, axis=0):
    return tgt.at[idx].add(src)

def _segment_sum(src, seg, n):
    return jax.ops.segment_sum(src, seg, n)
kernel_name = 'mk_gnn_ffn_d1_gnn_r32_9d902d'

def setup_inputs(seed: int=0):
    np.random.seed(seed)
    _w = jnp.asarray

    def _rec_inputs():
        import jax
        import jax.numpy as jnp
        _gk = jax.random.key(seed)
        x = -0.0006008 + 1.001 * jax.random.normal(jax.random.fold_in(_gk, 1), (3125, 256), jnp.float32)
        src = jax.random.randint(jax.random.fold_in(_gk, 2), (50000,), 0, 3125, jnp.int32)
        dst = jnp.minimum((3125 * jax.random.uniform(jax.random.fold_in(_gk, 3), (50000,)) ** 2.0).astype(jnp.int32), 99999)
        _o = jnp.argsort(dst, stable=True)
        src = src[_o]
        dst = dst[_o]
        edge_attr_16 = 0.000130101 + 1.00012 * jax.random.normal(jax.random.fold_in(_gk, 11), (50000, 16), jnp.float32)
        return (x, src, dst, edge_attr_16)
    x, src, dst, edge_attr_16 = _rec_inputs()

    def _L0_gnn_setup():
        import jax, jax.numpy as jnp
        import numpy as np
        N, NODE_DIM, EDGE_DIM, HIDDEN, E = (10000, 256, 16, 512, 10000)
        key = jax.random.key(seed)
        ks = jax.random.split(key, 12)

        def lin(kw, kb, fan_in, fan_out):
            bound = 1.0 / np.sqrt(fan_in)
            W = jax.random.uniform(kw, (fan_in, fan_out), jnp.float32, -bound, bound)
            b = jax.random.uniform(kb, (fan_out,), jnp.float32, -bound, bound)
            return (W, b)
        node_features = jax.random.normal(ks[0], (N, NODE_DIM), jnp.float32)
        edge_index = jax.random.randint(ks[1], (2, E), 0, N, jnp.int32)
        edge_features = jax.random.normal(ks[2], (E, EDGE_DIM), jnp.float32)
        mW1, mb1 = lin(ks[3], ks[4], 2 * NODE_DIM + EDGE_DIM, HIDDEN)
        mW2, mb2 = lin(ks[5], ks[6], HIDDEN, NODE_DIM)
        uW1, ub1 = lin(ks[7], ks[8], 2 * NODE_DIM, HIDDEN)
        uW2, ub2 = lin(ks[9], ks[10], HIDDEN, NODE_DIM)
        return {'node_features': node_features, 'edge_index': edge_index, 'edge_features': edge_features, 'mW1': mW1, 'mb1': mb1, 'mW2': mW2, 'mb2': mb2, 'uW1': uW1, 'ub1': ub1, 'uW2': uW2, 'ub2': ub2}
    _L0_gnn_all = _L0_gnn_setup()
    _L0_gnn_in = {k: v for k, v in _L0_gnn_all.items() if k in ('mW1', 'mb1', 'mW2', 'mb2', 'uW1', 'ub1', 'uW2', 'ub2')}
    del _L0_gnn_all

    def _L0_ffn_setup():
        import jax, jax.numpy as jnp
        import numpy as np
        E = 8
        K = 2
        D = 256
        H = 512
        DOUT = 256
        EPS = 1e-05
        key = jax.random.key(seed)
        ks = jax.random.split(key, 9)
        s = 0.02
        return {'x': jax.random.normal(ks[0], (4, 256, D), jnp.float32), 'gamma': 1.0 + 0.05 * jax.random.normal(ks[1], (D,), jnp.float32), 'beta': 0.05 * jax.random.normal(ks[2], (D,), jnp.float32), 'Wr': 0.01 * jax.random.normal(ks[3], (D, E), jnp.float32), 'br': jnp.zeros((E,), jnp.float32), 'W1': s * jax.random.normal(ks[4], (E, D, H), jnp.float32), 'b1': s * jax.random.normal(ks[5], (E, H), jnp.float32), 'W2': s * jax.random.normal(ks[6], (E, H, DOUT), jnp.float32), 'b2': s * jax.random.normal(ks[7], (E, DOUT), jnp.float32)}
    _L0_ffn_all = _L0_ffn_setup()
    _L0_ffn_in = {k: v for k, v in _L0_ffn_all.items() if k in ('gamma', 'beta', 'Wr', 'br', 'W1', 'b1', 'W2', 'b2')}
    del _L0_ffn_all
    return {'x': x, 'src': src, 'dst': dst, 'edge_attr_16': edge_attr_16, 'L0_gnn_mW1': _L0_gnn_in['mW1'], 'L0_gnn_mb1': _L0_gnn_in['mb1'], 'L0_gnn_mW2': _L0_gnn_in['mW2'], 'L0_gnn_mb2': _L0_gnn_in['mb2'], 'L0_gnn_uW1': _L0_gnn_in['uW1'], 'L0_gnn_ub1': _L0_gnn_in['ub1'], 'L0_gnn_uW2': _L0_gnn_in['uW2'], 'L0_gnn_ub2': _L0_gnn_in['ub2'], 'L0_ffn_gamma': _L0_ffn_in['gamma'], 'L0_ffn_beta': _L0_ffn_in['beta'], 'L0_ffn_Wr': _L0_ffn_in['Wr'], 'L0_ffn_br': _L0_ffn_in['br'], 'L0_ffn_W1': _L0_ffn_in['W1'], 'L0_ffn_b1': _L0_ffn_in['b1'], 'L0_ffn_W2': _L0_ffn_in['W2'], 'L0_ffn_b2': _L0_ffn_in['b2']}

def reference(x, src, dst, edge_attr_16, L0_gnn_mW1, L0_gnn_mb1, L0_gnn_mW2, L0_gnn_mb2, L0_gnn_uW1, L0_gnn_ub1, L0_gnn_uW2, L0_gnn_ub2, L0_ffn_gamma, L0_ffn_beta, L0_ffn_Wr, L0_ffn_br, L0_ffn_W1, L0_ffn_b1, L0_ffn_W2, L0_ffn_b2):
    import jax
    import jax.numpy as jnp

    def _L0_gnn_ref(node_features, edge_index, edge_features, mW1, mb1, mW2, mb2, uW1, ub1, uW2, ub2):
        import jax, jax.numpy as jnp
        import numpy as np
        N, NODE_DIM, EDGE_DIM, HIDDEN, E = (10000, 256, 16, 512, 10000)
        i_idx = edge_index[0]
        j_idx = edge_index[1]
        node_i = node_features[i_idx]
        node_j = node_features[j_idx]
        msg_input = jnp.concatenate([node_i, node_j, edge_features], axis=-1)
        h = jax.nn.relu(msg_input @ mW1 + mb1)
        messages = h @ mW2 + mb2
        aggregated = jax.ops.segment_sum(messages, i_idx, num_segments=node_features.shape[0])
        update_input = jnp.concatenate([node_features, aggregated], axis=-1)
        u = jax.nn.relu(update_input @ uW1 + ub1)
        updated = u @ uW2 + ub2
        return node_features + updated

    def _L0_ffn_ref(x, gamma, beta, Wr, br, W1, b1, W2, b2):
        import jax, jax.numpy as jnp
        import numpy as np
        E = 8
        K = 2
        D = 256
        H = 512
        DOUT = 256
        EPS = 1e-05
        mu = jnp.mean(x, axis=-1, keepdims=True)
        var = jnp.mean(jnp.square(x - mu), axis=-1, keepdims=True)
        xn = (x - mu) * jax.lax.rsqrt(var + EPS) * gamma + beta
        logits = jnp.einsum('bsd,de->bse', xn, Wr) + br
        top_vals, top_idx = jax.lax.top_k(logits, K)
        w = jax.nn.softmax(top_vals, axis=-1)
        w_full = jnp.einsum('bsk,bske->bse', w, jax.nn.one_hot(top_idx, E, dtype=w.dtype))
        y = jnp.zeros(x.shape[:-1] + (DOUT,), x.dtype)
        for e in range(E):
            h = jax.nn.gelu(jnp.einsum('bsd,dh->bsh', xn, W1[e]) + b1[e], approximate=False)
            y_e = jnp.einsum('bsh,hd->bsd', h, W2[e]) + b2[e]
            y = y + y_e * w_full[..., e, None]
        return y
    edge_index = jnp.stack([src, dst])
    x = x + _L0_gnn_ref(_layernorm(x, axis=-1), edge_index, edge_attr_16, L0_gnn_mW1, L0_gnn_mb1, L0_gnn_mW2, L0_gnn_mb2, L0_gnn_uW1, L0_gnn_ub1, L0_gnn_uW2, L0_gnn_ub2)
    x = x + _L0_ffn_ref(_layernorm(x, axis=-1)[None], L0_ffn_gamma, L0_ffn_beta, L0_ffn_Wr, L0_ffn_br, L0_ffn_W1, L0_ffn_b1, L0_ffn_W2, L0_ffn_b2)[0]
    return x

_drawn_inputs = setup_inputs


def setup_inputs(seed=0):
    import zlib

    import numpy as np

    out = dict(_drawn_inputs(seed))
    spreads = {'L0_ffn_br': (0.0, 0.304)}
    factors = {'edge_attr_16': 4.384,
     'L0_gnn_mb1': 5.464,
     'L0_gnn_ub1': 8.0,
     'L0_gnn_ub2': 4.354,
     'L0_ffn_gamma': 8.0,
     'L0_ffn_beta': 8.0,
     'L0_ffn_Wr': 2.925,
     'L0_ffn_b1': 21.917,
     'L0_ffn_b2': 8.0}
    for name, (base, spread) in spreads.items():
        noise = np.random.default_rng([zlib.crc32(name.encode()), seed]).standard_normal(out[name].shape)
        drawn = base * np.exp(spread * noise) if base else spread * noise
        out[name] = jnp.asarray(drawn.astype(out[name].dtype))
    for name, factor in factors.items():
        out[name] = (out[name] * factor).astype(out[name].dtype)
    return out
```

```python
from contextlib import ExitStack

import concourse.bass as bass
from concourse import mybir


def build_kernel(nc, x, src, dst, edge_attr, mW1, mb1, mW2, mb2, uW1, ub1, uW2, ub2,
                 gamma, beta, Wr, br, W1, b1, W2, b2, out):
    F32, F16, BF16, I32 = mybir.dt.float32, mybir.dt.float16, mybir.dt.bfloat16, mybir.dt.int32
    ALU = mybir.AluOpType
    ACT = mybir.ActivationFunctionType
    AX = mybir.AxisListType
    ds = bass.ds

    N, D = x.shape
    E, EA = edge_attr.shape
    H = mW2.shape[0]
    NX, DM, HE = W1.shape
    EPS = 1e-5
    W = -(-N // 128)
    NP = W * 128
    TAIL = N - (W - 1) * 128
    EP = 125
    EC = E // EP
    PAIRS = (E + W * 255) // 256
    NT = 2 * PAIRS
    CH = EC // W
    REC = 128
    KE = 6 * EA
    NO_NODE = 200.0
    KD, KH = D // 128, H // 128
    assert EP * EC == E and CH * W == EC and NT % 8 == 0 and W % 2 == 1

    recs_d = nc.dram_tensor("recs_d", [128 * NT, REC], BF16, kind="Internal").ap()
    q_d = nc.dram_tensor("q_d", [NP, 2 * H], F16, kind="Internal").ap()

    with ExitStack() as ctx:
        def sb(name, shape, dt=F32):
            return ctx.enter_context(nc.sbuf_tensor("sb_" + name, list(shape), dt))

        def sem(name):
            return ctx.enter_context(nc.semaphore(name))

        r_xs = sb("r_xs", [128, W * D])
        r_xt = sb("r_xt", [128, KD * NP])
        r_p = sb("r_p", [128, W * H])
        r_h = sb("r_h", [128, W * H])
        r_w = sb("r_w", [128, 12288])

        xs = r_xs[:, :].rearrange("p (w d) -> p w d", w=W)
        xnT = r_xt[:, :].rearrange("p (k n) -> p k n", k=KD)
        P12 = r_p[:, :].bitcast(F16).rearrange("p (w s h) -> p w s h", w=W, s=2)
        Hacc = r_h[:, :].rearrange("p (w h) -> p w h", w=W)
        scan = r_p[:, 0:W * EC].rearrange("p (b c) -> p b c", b=W)
        xc = r_h[:, 0:W * D].rearrange("p (w d) -> p w d", w=W)
        ea = r_h[:, W * D:W * D + EC * EA].rearrange("p (c a) -> p c a", c=EC)

        def carve(region, start):
            at = [start]

            def take(shape, dt=F32):
                n = 1
                for s in shape:
                    n *= s
                words = n if dt in (F32, I32) else n // 2
                a = region[:, at[0]:at[0] + words]
                at[0] += words
                assert at[0] <= region.shape[1], (at[0], region.shape)
                if dt != F32:
                    a = a.bitcast(dt)
                if len(shape) == 2:
                    a = a.rearrange("p (a b) -> p a b", a=shape[0])
                if len(shape) == 3:
                    a = a.rearrange("p (a b c) -> p a b c", a=shape[0], b=shape[1])
                return a
            return take

        t1 = carve(r_w, 0)
        hi_b = t1([EC], BF16)
        lo_b = t1([EC], BF16)
        dst_i = t1([EC], I32)
        idx = t1([EC], I32)
        rec = t1([2, CH, REC], BF16)
        idx_s = t1([2, CH], I32)
        oh_lo = t1([CH, 128], BF16)
        oh_hi = t1([CH, W], BF16)
        wAB = t1([4, H])
        b1row = t1([H])
        xstage = t1([D])
        xTst = t1([KD, 128])
        qst = t1([2, 2 * H], F16)
        r1 = t1([CH, EA])
        sq_rows = t1([256])
        pair_no = t1([PAIRS])
        wtab = t1([PAIRS])
        ub2b = t1([D])
        mask = r_h[:, 0:W * EC // 2].bitcast(BF16).rearrange("p (b c) -> p b c", b=W)
        cdup = r_p[0:KE, 11700:11700 + H]
        t3 = carve(r_w, 0)
        recg = t3([2, 4, REC], BF16)
        trs = t3([2, 8 * 128], BF16)
        oh = t3([8, 128], BF16)
        qg = t3([8, 2 * H], F16)
        h1 = t3([4, H], F16)
        h2 = t3([4, H], F16)
        t4 = carve(r_w, 0)
        hst = t4([H])
        HT = t4([KH, H])
        aggT = t4([KD, H])
        uT = t4([KH, H])
        diag = t4([H])
        mb2b = t4([D])
        t4w = carve(r_w, 8192)
        mW2s = t4w([KH, D])
        uW1s = t4w([2 * KD, H])
        uW2s = t4w([KH, D])
        t5 = carve(r_w, 0)
        hT = t5([2, KH, H])
        w2hi = t5([NX // 2 * KH, D])
        zst = t5([D])
        zTst = t5([KD, 128])
        gam = t5([D])
        bet = t5([D])
        b2s = t5([D])
        lg = t5([W, NX])
        rt = t5([4, W, NX])
        wf = t5([W, NX])
        rs = t5([8, W])
        wfT = t5([128])
        W1s = r_p[:, 0:NX * KD * HE].rearrange("p (e k h) -> p e k h", e=NX, k=KD)
        w2lo = r_p[:, NX * KD * HE:NX * KD * HE + NX // 2 * KH * D].rearrange("p (a d) -> p a d", d=D)
        z = r_h[:, 0:W * D].rearrange("p (w d) -> p w d", w=W)
        zsq = r_h[:, W * D:2 * W * D].rearrange("p (w d) -> p w d", w=W)

        C6 = sb("C6", [KE, H], BF16)
        ident = sb("ident", [128, 128])
        identb = sb("identb", [128, 128], BF16)
        before = sb("before", [128, 128])
        iota = sb("iota", [128, 128], BF16)
        iota_w = sb("iota_w", [128, W], BF16)
        ones = sb("ones", [128, 128])
        wtab_i = sb("wtab_i", [128, PAIRS], I32)
        deg_s = sb("deg_s", [128, W])
        ub1c = sb("ub1c", [128, KH])
        Wrs = sb("Wrs", [128, KD, NX])
        brb = sb("brb", [128, NX])
        b1c = sb("b1c", [128, NX, KH])
        epsc = sb("epsc", [128, 1])
        mx = sb("mx", [128, 8])
        mxa = sb("mxa", [128, 8])
        sc = sb("sc", [128, 8])
        sci = sb("sci", [128, 8], I32)
        stat = sb("stat", [128, 6, W])
        riota = sb("riota", [128, NX])
        f_sc, finv = sc[:, 1:2], sc[:, 2:3]

        ps = [ctx.enter_context(nc.psum_tensor(f"ps{i}", [128, 512], F32)) for i in range(8)]

        s_src = sem("src_loaded")
        s_x = sem("x_loaded")
        s_ea = sem("edges_loaded")
        s_w = sem("weights_loaded")
        s_cr = sem("c_replicated")
        s_c6 = sem("c6_placed")
        s_cst = sem("constants_made")
        s_pad = sem("pads_written")
        s_padm = sem("pads_made")
        dv = sem("dve_done")
        s_mx = sem("maxima_made")
        s_all = sem("maxima_reduced")
        s_f = sem("scale_made")
        s_sp = sem("c_split")
        s_cnt = sem("counts_made")
        s_tot = sem("totals_made")
        s_sqr = sem("variance_made")
        s_sd = sem("deviation_made")
        s_chunk = sem("chunk_made")
        s_sc = [sem(f"chunk_scattered{i}") for i in range(2)]
        s_oh = sem("onehots_made")
        s_hist = sem("onehots_counted")
        s_xst = sem("xn_tile_made")
        s_tp = sem("xn_tile_transposed")
        s_xT = sem("xn_tile_evacuated")
        s_pq = sem("pq_made")
        s_pq1 = sem("pq_first_half")
        s_pq2 = sem("pq_second_half")
        s_qst = [sem(f"q_stored{i}") for i in range(2)]
        s_wtab = sem("window_table_made")
        s_deg = sem("degree_made")
        s_ub = sem("ub2_loaded")
        s_wp = sem("small_weights_loaded")
        u_mb = sem("mb2_loaded")
        u_dg = sem("u_diagonal_made")
        z_gb = sem("gamma_beta_b2_loaded")
        s_hz = sem("sums_zeroed")
        e_rec = [sem(f"records_in{i}") for i in range(2)]
        e_oh = sem("tile_onehot_made")
        e_tr = sem("group_transposed")
        e_te = sem("group_evacuated")
        e_q = [sem(f"q_rows_in{i}") for i in range(8)]
        e_s = sem("tile_summed")
        e_h1 = sem("hidden_first_half")
        e_h2 = sem("hidden_second_half")
        e_agg = sem("tile_aggregated")
        e_acc = sem("pair_accumulated")
        u_w = sem("update_weights_loaded")
        u_st = sem("u_sum_staged")
        u_tr = sem("u_sum_transposed")
        u_ht = sem("u_sum_evacuated")
        u_ag = sem("u_agg_made")
        u_ae = sem("u_agg_evacuated")
        u_u = sem("u_hidden_made")
        u_ue = sem("u_hidden_evacuated")
        u_o = sem("u_out_made")
        u_x = sem("u_x_updated")
        f_w1 = sem("w1_loaded")
        f_w2 = sem("w2_loaded")
        z_sq = sem("z_variance_made")
        z_sd = sem("z_deviation_made")
        z_st = sem("z_tile_staged")
        z_tr = sem("z_tile_transposed")
        z_te = sem("z_tile_evacuated")
        z_lg = sem("z_logits_made")
        z_le = sem("z_logits_evacuated")
        z_d = sem("z_gap_made")
        z_ex = sem("z_gap_exp")
        z_wf = sem("z_routes_made")
        b_tr = sem("b_routes_transposed")
        b_te = sem("b_routes_evacuated")
        b_o = sem("b_bias_made")
        b_x = sem("b_bias_added")
        f_h = sem("f_hidden_made")
        f_he = sem("f_hidden_evacuated")
        f_o = sem("f_out_made")
        f_x = sem("f_out_added")
        s_gp, s_gs, s_gd = sem("gates_gpsimd"), sem("gates_sync"), sem("gates_vector")
        s_out = sem("result_stored")

        block = ctx.enter_context(nc.Block())

        def sel(ap, k, n=1):
            return ap[:, k:k + n] if isinstance(k, int) else ap[:, ds(k, n)]

        def gate(eng, passed):
            eng.sem_inc(passed, 1)

        def paired(eng, count, body):
            body(0, 0)
            body(1, 1)
            with eng.Fori(1, count // 2) as i:
                body(2 * i, 0)
                body(2 * i + 1, 1)
            body(count - 1, (count - 1) % 2)

        def static_ge(k, n):
            return (not isinstance(k, int)) or k >= n

        FULL = N - TAIL
        x_full = x[0:FULL, :].rearrange("(w p) d -> p w d", p=128)
        out_full = out[0:FULL, :].rearrange("(w p) d -> p w d", p=128)
        rec_rows = recs_d.rearrange("(q t) r -> q (t r)", q=128)
        row = lambda a: a.rearrange("(o n) -> o n", o=1)
        NCH = W // 4
        CHUNKS = [(c * 4, 4) for c in range(NCH)] + ([(NCH * 4, W - NCH * 4)] if W % 4 else [])
        assert W - NCH * 4 == 1

        src_i = r_p[0:EP, 12250:12250 + EC].bitcast(I32)

        @block.sync
        def _(sp):
            sp.dma_start(src_i, src.rearrange("(p c) -> p c", p=EP)).then_inc(s_src, 16)
            sp.dma_start(ea[0:EP], edge_attr.rearrange("(p c) a -> p c a", p=EP)).then_inc(s_ea, 16)
            sp.dma_start(dst_i[0:EP, :], dst.rearrange("(p c) -> p c", p=EP)).then_inc(s_ea, 16)
            sp.wait_ge(s_padm, 2)
            sp.dma_start(xs[:, 0:W - 1, :], x_full).then_inc(s_x, 16)
            sp.dma_start(xs[0:TAIL, W - 1, :], x[FULL:N, :]).then_inc(s_x, 16)
            sp.dma_start(wAB, mW1[0:2 * D, :].rearrange("(k p) h -> p k h", p=128)).then_inc(s_w, 16)
            sp.dma_start(b1row[0:1, :], row(mb1)).then_inc(s_w, 16)
            for r in range(6):
                sp.dma_start(cdup[r * EA:(r + 1) * EA, :], mW1[2 * D:2 * D + EA, :]).then_inc(s_cr, 16)
            sp.dma_start(ub2b, row(ub2).broadcast_to([128, D])).then_inc(s_ub, 16)
            sp.dma_start(ub1c[:, :], ub1.rearrange("(k p) -> p k", p=128), allow_slow_non_contiguous=True).then_inc(s_wp, 16)
            sp.dma_start(Wrs[:, :, :], Wr.rearrange("(k p) e -> p k e", p=128)).then_inc(s_wp, 16)
            sp.dma_start(brb[:, :], row(br).broadcast_to([128, NX])).then_inc(s_wp, 16)
            sp.dma_start(b1c[:, :, :], b1.rearrange("e (k p) -> p e k", p=128), allow_slow_non_contiguous=True).then_inc(s_wp, 16)
            sp.wait_ge(s_sp, 1)
            for r, part in enumerate((0, 1, 2, 0, 1, 0)):
                sp.dma_start(C6[r * EA:(r + 1) * EA, :], qst[r * EA:(r + 1) * EA, 0, 0:H].bitcast(BF16) if part == 0
                             else qst[r * EA:(r + 1) * EA, 0, H:2 * H].bitcast(BF16) if part == 1
                             else qst[r * EA:(r + 1) * EA, 1, 0:H].bitcast(BF16)).then_inc(s_c6, 16)

            def store_q(k, par):
                sp.wait_ge(s_pq2, 2 * k + 2)
                sp.wait_ge(s_pq1, 2 * k + 2)
                gate(sp, s_gs)
                rows = q_d[k * 128:(k + 1) * 128, :] if isinstance(k, int) else q_d[ds(k * 128, 128), :]
                sp.dma_start(rows, qst[:, par, :]).then_inc(s_qst[par], 16)
            paired(sp, W, store_q)
            for par in range(2):
                sp.wait_ge(s_sc[par], 16 * CH * ((W + 1 - par) // 2))
            sp.wait_ge(s_hz, 1)
            def load_group(g, i, par):
                if static_ge(i, 1):
                    sp.wait_ge(e_tr, g - 1)
                    sp.wait_ge(e_oh, 4 * g - 4)
                    gate(sp, s_gs)
                    for j in range(4):
                        sp.wait_ge(e_q[4 * par + j], 16 * i)
                gate(sp, s_gs)
                cols = (rec_rows[:, g * 4 * REC:(g + 1) * 4 * REC] if isinstance(g, int)
                        else rec_rows[:, ds(g * (4 * REC), 4 * REC)])
                sp.dma_start(recg[:, par, :, :].rearrange("p a b -> p (a b)"), cols).then_inc(e_rec[par], 16)
            load_group(0, 0, 0)
            load_group(1, 0, 1)
            sp.dma_start(mW2s, mW2.rearrange("(k p) d -> p k d", p=128)).then_inc(u_w, 16)
            sp.dma_start(uW1s, uW1.rearrange("(k p) h -> p k h", p=128)).then_inc(u_w, 16)
            sp.dma_start(uW2s, uW2.rearrange("(k p) d -> p k d", p=128)).then_inc(u_w, 16)
            with sp.Fori(1, NT // 8) as i:
                load_group(2 * i, i, 0)
                load_group(2 * i + 1, i, 1)

            sp.wait_ge(e_s, NT)
            sp.dma_start(W1s, W1.rearrange("e (k p) h -> p e k h", p=128)).then_inc(f_w1, 16)
            half = NX // 2
            sp.dma_start(w2lo, W2[0:half].rearrange("e (k p) d -> p (e k) d", p=128)).then_inc(f_w2, 16)
            sp.wait_ge(e_agg, NT)
            sp.dma_start(mb2b, row(mb2).broadcast_to([128, D])).then_inc(u_mb, 16)
            sp.wait_ge(u_o, W)
            sp.wait_ge(u_x, W)
            sp.dma_start(w2hi, W2[half:NX].rearrange("e (k p) d -> p (e k) d", p=128)).then_inc(f_w2, 16)

            sp.dma_start(gam, row(gamma).broadcast_to([128, D])).then_inc(z_gb, 16)
            sp.dma_start(bet, row(beta).broadcast_to([128, D])).then_inc(z_gb, 16)
            sp.dma_start(b2s[0:NX, :], b2).then_inc(z_gb, 16)

            sp.wait_ge(f_x, NX * W)
            sp.dma_start(out_full, xs[:, 0:W - 1, :]).then_inc(s_out, 16)
            sp.dma_start(out[FULL:N, :], xs[0:TAIL, W - 1, :]).then_inc(s_out, 16)
            sp.wait_ge(s_out, 32)

        @block.gpsimd
        def _(pool):
            g = nc.gpsimd
            g.memset(xs[:, W - 1, :], 0.0).then_inc(s_padm, 1)
            g.memset(rec[:, :, :, :].rearrange("p a b c -> p (a b c)"), 0.0).then_inc(s_padm, 1)
            pool.wait_ge(s_padm, 2)
            g.memset(rec[:, :, :, KE + 2:KE + 3].rearrange("p a b c -> p (a b c)"), NO_NODE).then_inc(s_padm, 1)
            pool.wait_ge(s_padm, 3)
            per, left = 2 * CH, NT
            n_pad = 0
            while left:
                m = min(per, left)
                pool.dma_start(rec_rows[:, (NT - left) * REC:(NT - left + m) * REC],
                               rec.rearrange("p a b c -> p (a b c)")[:, 0:m * REC]).then_inc(s_pad, 16)
                left -= m
                n_pad += 1
            g.memset(ident[:, :], 0.0).then_inc(s_cst, 1)
            g.memset(before[:, :], 0.0).then_inc(s_cst, 1)
            g.memset(ones[:, :], 1.0).then_inc(s_cst, 1)
            g.memset(epsc[:, :], EPS).then_inc(s_cst, 1)
            g.memset(mx[:, :], 0.0).then_inc(s_cst, 1)
            g.iota(iota[:, :], [[1, 128]], base=0, channel_multiplier=0, allow_small_or_imprecise_dtypes=True).then_inc(s_cst, 1)
            g.iota(iota_w[:, :], [[1, W]], base=0, channel_multiplier=0, allow_small_or_imprecise_dtypes=True).then_inc(s_cst, 1)
            g.iota(pair_no, [[1, PAIRS]], base=0, channel_multiplier=0, allow_small_or_imprecise_dtypes=True).then_inc(s_cst, 1)
            g.iota(riota[:, :], [[-1, NX]], base=NX, channel_multiplier=0, allow_small_or_imprecise_dtypes=True).then_inc(s_cst, 1)
            pool.wait_ge(s_cst, 9)
            g.affine_select(out=ident[:, :], in_=ident[:, :], compare_op=ALU.not_equal, fill=1.0,
                            base=0, pattern=[[-1, 128]], channel_multiplier=1).then_inc(s_cst, 1)
            g.affine_select(out=before[:, :], in_=before[:, :], compare_op=ALU.is_ge, fill=1.0,
                            base=0, pattern=[[-1, 128]], channel_multiplier=1).then_inc(s_cst, 1)
            pool.wait_ge(s_cst, 11)
            g.tensor_copy(identb[:, :], ident[:, :]).then_inc(s_cst, 1)
            pool.wait_ge(s_mx, 5)
            g.partition_all_reduce(mxa[:, :], mx[:, :], 128, bass.bass_isa.ReduceOp.max).then_inc(s_all, 1)
            pool.wait_ge(s_pad, 16 * n_pad)

            def scatter(k, par):
                pool.wait_ge(s_chunk, k + 1)
                gate(pool, s_gp)
                for c in range(CH):
                    g.indirect_dma_start(recs_d, bass.IndirectOffsetOnAxis(ap=idx_s[0:EP, par, c:c + 1], axis=0),
                                         rec[0:EP, par, c, :], None).then_inc(s_sc[par], 16)
            paired(pool, W, scatter)

            for par in range(2):
                pool.wait_ge(s_qst[par], 16 * ((W + 1 - par) // 2))
            def gather(i):
                for j in range(8):
                    if j % 4 == 0:
                        pool.wait_ge(e_rec[j // 4], 16 * (i + 1))
                    if static_ge(i, 1):
                        pool.wait_ge(e_s, 8 * i + j - 7)
                    gate(pool, s_gp)
                    g.indirect_dma_start(qg[:, j, :], None, q_d, bass.IndirectOffsetOnAxis(
                        ap=recg[:, j // 4, j % 4, KE:KE + 2].bitcast(I32), axis=0)).then_inc(e_q[j], 16)
            gather(0)
            with pool.Fori(1, NT // 8) as i:
                gather(i)

        @block.scalar
        def _(act):
            a = nc.scalar
            act.wait_ge(s_sqr, 1)
            act.wait_ge(s_cst, 4)
            a.activation(stat[:, 2, :], stat[:, 1, :], ACT.Sqrt, bias=epsc[:, :], scale=1.0 / D).then_inc(s_sd, 1)

            def node_tile(k, par):
                act.wait_ge(s_tp, k + 1)
                if static_ge(k, 1):
                    act.wait_ge(s_pq, 2 * k)
                a.activation(xTst.rearrange("p k n -> p (k n)"), ps[0][:, 0:D], ACT.Copy).then_inc(s_xT, 1)
                dst_t = xnT[:, :, k * 128:(k + 1) * 128] if isinstance(k, int) else xnT[:, :, ds(k * 128, 128)]
                a.activation(dst_t, ps[0][:, 0:D].rearrange("p (k n) -> p k n", k=KD), ACT.Copy).then_inc(s_xT, 1)
                act.wait_ge(s_pq, 2 * k + 1)
                pd = P12[:, k, 0, :] if isinstance(k, int) else P12[:, ds(k, 1), 0, :].rearrange("p a h -> p (a h)")
                a.activation(pd, ps[1][:, :], ACT.Copy).then_inc(s_pq1, 1)
                act.wait_ge(s_pq, 2 * k + 2)
                if static_ge(k, 2):
                    act.wait_ge(s_qst[par], 8 * k if par == 0 else 8 * k - 8)
                a.activation(qst[:, par, 0:H], ps[2][:, :], ACT.Copy).then_inc(s_pq1, 1)
            act.wait_ge(s_c6, 96)
            paired(act, W, node_tile)

            def te(g, i):
                act.wait_ge(e_tr, g + 1)
                if static_ge(i, 1):
                    act.wait_ge(e_s, 4 * g - 4)
            def evac(par):
                a.activation(trs[:, par, :], ps[7][:, :].bitcast(BF16), ACT.Copy).then_inc(e_te, 1)

            def edge_body(i, last=False):
                for j in range(8):
                    t = 8 * i + j
                    act.wait_ge(e_s, t + 1)
                    if static_ge(i, 1) or j >= 4:
                        act.wait_ge(e_agg, t - 3)
                    a.activation(h1[:, j % 4, :], ps[j % 4][:, :], ACT.Relu).then_inc(e_h1, 1)
                    if j == 2:
                        te(2 * i + 1, i)
                        evac(1)
                    if j == 6 and not last:
                        g = 2 * i + 2
                        act.wait_ge(e_tr, g + 1)
                        act.wait_ge(e_s, 4 * g - 4)
                        evac(0)
            te(0, 0)
            evac(0)
            edge_body(0)
            with act.Fori(1, NT // 8 - 1) as i:
                edge_body(i)
            edge_body(NT // 8 - 1, last=True)

            def update_chunk(c, n):
                for j in range(n):
                    t = 4 * c + j
                    act.wait_ge(u_tr, t + 1)
                    if j == 0 and static_ge(c, 1):
                        act.wait_ge(u_ag, 2 * c)
                    a.activation(HT[:, :, j * 128:(j + 1) * 128],
                                 ps[0][:, :].rearrange("p (k n) -> p k n", k=KH), ACT.Copy).then_inc(u_ht, 1)
                for m in range(KD):
                    act.wait_ge(u_ag, 2 * c + m + 1)
                    a.activation(aggT[:, m, 0:n * 128], ps[1 + m][:, 0:n * 128], ACT.Copy).then_inc(u_ae, 1)
                for m in range(KH):
                    act.wait_ge(u_u, 4 * c + m + 1)
                    a.activation(uT[:, m, 0:n * 128], ps[3 + m % 2][:, 0:n * 128], ACT.Relu,
                                 bias=ub1c[:, m:m + 1]).then_inc(u_ue, 1)
            update_chunk(0, 4)
            with act.Fori(1, NCH) as c:
                update_chunk(c, 4)
            update_chunk(NCH, 1)

            for r in range(2):
                act.wait_ge(z_sq, r + 1)
                a.activation(stat[:, 2, :], stat[:, 1, :], ACT.Sqrt, bias=epsc[:, :], scale=1.0 / D).then_inc(z_sd, 1)

            def z_tile(k, par):
                act.wait_ge(z_tr, k + 1)
                if static_ge(k, 1):
                    act.wait_ge(z_lg, k)
                a.activation(zTst.rearrange("p k n -> p (k n)"), ps[0][:, 0:D], ACT.Copy).then_inc(z_te, 1)
                dst_t = xnT[:, :, k * 128:(k + 1) * 128] if isinstance(k, int) else xnT[:, :, ds(k * 128, 128)]
                a.activation(dst_t, ps[0][:, 0:D].rearrange("p (k n) -> p k n", k=KD), ACT.Copy).then_inc(z_te, 1)
            paired(act, W, z_tile)
            act.wait_ge(z_d, 1)
            a.activation(rs[:, 3, :], rs[:, 2, :], ACT.Exp).then_inc(z_ex, 1)

            def bias_tile(k, par):
                act.wait_ge(b_tr, k + 1)
                if static_ge(k, 1):
                    act.wait_ge(b_o, k)
                a.activation(wfT[0:NX, :], ps[1][0:NX, 0:128], ACT.Copy).then_inc(b_te, 1)
            paired(act, W, bias_tile)

            def expert_chunk(c, n):
                for e in range(NX):
                    for m in range(KH):
                        q = NX * KH * c + e * KH + m
                        act.wait_ge(f_h, q + 1)
                        if m == 0 and (static_ge(c, 1) or e >= 2):
                            act.wait_ge(f_o, 4 * NX * c + n * (e - 1) if e >= 2 else 4 * NX * c + 4 * (e - 1))
                        a.activation(hT[:, e % 2, m, 0:n * 128], ps[m][:, 0:n * 128], ACT.Gelu,
                                     bias=b1c[:, e, m:m + 1]).then_inc(f_he, 1)
            expert_chunk(0, 4)
            with act.Fori(1, NCH) as c:
                expert_chunk(c, 4)
            expert_chunk(NCH, 1)

        @block.vector
        def _(dve):
            v = nc.vector
            made = [0]

            def own(instruction, also=None):
                instruction.then_inc(dv, 1)
                made[0] += 1
                dve.wait_ge(dv, made[0])

            def small(n):
                return sq_rows[:, n * W:(n + 1) * W]

            tmp_i = r_p[0:EP, 10000:10000 + EC].bitcast(I32)
            tmp_f = r_p[0:EP, 10400:10400 + EC]
            tmp2_i = r_p[0:EP, 10800:10800 + EC].bitcast(I32)
            tmp2_f = r_p[0:EP, 11200:11200 + EC]
            dve.wait_ge(s_src, 16)
            dve.wait_ge(s_cst, 12)
            own(v.tensor_scalar(tmp_i, src_i, 7, None, ALU.logical_shift_right))
            own(v.tensor_scalar(tmp2_i, src_i, 127, None, ALU.bitwise_and))
            own(v.tensor_copy(hi_b[0:EP, :], tmp_i))
            own(v.tensor_copy(lo_b[0:EP, :], tmp2_i))
            m3 = mask[0:EP]
            s3 = scan[0:EP]
            own(v.tensor_tensor(m3, hi_b[0:EP, :].unsqueeze(1).broadcast_to([EP, W, EC]),
                                iota_w[0:EP, :].unsqueeze(2).broadcast_to([EP, W, EC]), ALU.is_equal))
            mflat = m3.rearrange("p b c -> p (b c)")
            own(v.tensor_tensor_scan(s3.rearrange("p b c -> p (b c)"), mflat, mflat, 0.0, ALU.add, ALU.max))
            ends, cnt = small(0)[0:EP, :], small(1)[0:EP, :]
            own(v.tensor_copy(ends, s3[:, :, EC - 1]))
            own(v.tensor_copy(cnt[:, 0:1], ends[:, 0:1]))
            v.tensor_tensor(cnt[:, 1:W], ends[:, 1:W], ends[:, 0:W - 1], ALU.subtract).then_inc(s_cnt, 1)
            dve.wait_ge(s_cnt, 1)
            dve.wait_ge(s_tot, 1)
            tot, pre = ps[6][:, 0:W], ps[6][0:EP, 32:32 + W]
            own(v.tensor_scalar(sci_w := r_p[:, 11650:11650 + W].bitcast(I32), tot, 255.0, None, ALU.add))
            own(v.tensor_scalar(sci_w, sci_w, 8, None, ALU.logical_shift_right))
            own(v.tensor_copy(small(2), sci_w))
            own(v.tensor_tensor_scan(small(3), small(2), small(2), 0.0, ALU.add, ALU.max))
            own(v.tensor_tensor(small(4), small(3), small(2), ALU.subtract))
            off = small(5)[0:EP, :]
            own(v.scalar_tensor_tensor(off, small(4)[0:EP, :], 256.0, pre, ALU.mult, ALU.add))
            own(v.tensor_tensor(off, off, ends, ALU.subtract))
            own(v.scalar_tensor_tensor(off, off, -1.0, cnt, ALU.add, ALU.add))
            own(v.tensor_tensor(s3, s3, off.unsqueeze(2).broadcast_to([EP, W, EC]), ALU.add))
            own(v.tensor_tensor(s3, s3, m3, ALU.mult))
            own(v.tensor_reduce(tmp_f, s3.rearrange("p b c -> p c b"), AX.X, ALU.add))
            own(v.tensor_copy(tmp_i, tmp_f))
            own(v.tensor_scalar(tmp2_i, tmp_i, 127, None, ALU.bitwise_and))
            own(v.tensor_scalar(tmp_i, tmp_i, 7, None, ALU.logical_shift_right))
            own(v.tensor_copy(tmp_f, tmp2_i))
            own(v.tensor_copy(tmp2_f, tmp_i))
            own(v.scalar_tensor_tensor(idx[0:EP, :], tmp_f, float(NT), tmp2_f, ALU.mult, ALU.add))

            dve.wait_ge(s_ea, 32)
            dve.wait_ge(s_w, 32)
            dve.wait_ge(s_cr, 96)
            mxc = lambda n, p=128: mx[0:p, n:n + 1]
            v.tensor_reduce(mxc(0), wAB[:, 0:2, :].rearrange("p a b -> p (a b)"), AX.X, ALU.max, apply_absolute_value=True).then_inc(s_mx, 1)
            v.tensor_reduce(mxc(1), wAB[:, 2:4, :].rearrange("p a b -> p (a b)"), AX.X, ALU.max, apply_absolute_value=True).then_inc(s_mx, 1)
            v.tensor_reduce(mxc(2, KE), cdup[:, :], AX.X, ALU.max, apply_absolute_value=True).then_inc(s_mx, 1)
            v.tensor_reduce(mxc(3, 1), b1row[0:1, :], AX.X, ALU.max, apply_absolute_value=True).then_inc(s_mx, 1)
            v.tensor_reduce(mxc(4, EP), ea[0:EP].rearrange("p a b -> p (a b)"), AX.X, ALU.max, apply_absolute_value=True).then_inc(s_mx, 1)
            dve.wait_ge(s_all, 1)
            own(v.tensor_tensor(sc[:, 3:4], mxa[:, 0:1], mxa[:, 1:2], ALU.add))
            own(v.scalar_tensor_tensor(sc[:, 4:5], mxa[:, 2:3], float(EA), mxa[:, 4:5], ALU.mult, ALU.mult))
            own(v.scalar_tensor_tensor(sc[:, 5:6], sc[:, 3:4], float(D), sc[:, 4:5], ALU.mult, ALU.add))
            own(v.tensor_tensor(sc[:, 0:1], sc[:, 5:6], mxa[:, 3:4], ALU.add))
            own(v.tensor_scalar(sci[:, 0:1], sc[:, 0:1].bitcast(I32), 23, None, ALU.logical_shift_right))
            own(v.tensor_scalar(sci[:, 1:2], sci[:, 0:1], 40.0, 240.0, ALU.max, ALU.min))
            own(v.tensor_scalar(sci[:, 2:3], sci[:, 1:2], -1.0, 268.0, ALU.mult, ALU.add))
            own(v.tensor_scalar(sci[:, 3:4], sci[:, 1:2], -14.0, None, ALU.add))
            own(v.tensor_scalar(f_sc.bitcast(I32), sci[:, 2:3], 23, None, ALU.logical_shift_left))
            own(v.tensor_scalar(finv.bitcast(I32), sci[:, 3:4], 23, None, ALU.logical_shift_left))
            own(v.tensor_scalar(wAB.rearrange("p a b -> p (a b)"), wAB.rearrange("p a b -> p (a b)"), f_sc, None, ALU.mult))
            v.tensor_scalar(b1row[0:1, :], b1row[0:1, :], f_sc[0:1, :], None, ALU.mult).then_inc(s_f, 1)
            own(v.tensor_scalar(cdup[:, :], cdup[:, :], f_sc[0:KE, :], None, ALU.mult))
            cpart = [qst[0:KE, 0, 0:H].bitcast(BF16), qst[0:KE, 0, H:2 * H].bitcast(BF16), qst[0:KE, 1, 0:H].bitcast(BF16)]
            own(v.tensor_copy(cpart[0], cdup[:, :]))
            own(v.tensor_tensor(cdup[:, :], cdup[:, :], cpart[0], ALU.subtract))
            own(v.tensor_copy(cpart[1], cdup[:, :]))
            v.tensor_tensor(cpart[2], cdup[:, :], cpart[1], ALU.subtract).then_inc(s_sp, 1)

            def norm_begin(src3, cent, sq, ready):
                own(v.tensor_reduce(stat[:, 0, :], src3, AX.X, ALU.add))
                own(v.tensor_scalar(stat[:, 0, :], stat[:, 0, :], 1.0 / D, None, ALU.mult))
                own(v.tensor_tensor(cent, src3, stat[:, 0, :].unsqueeze(2).broadcast_to([128, W, D]), ALU.subtract))
                own(v.tensor_tensor(sq, cent, cent, ALU.mult))
                v.tensor_reduce(stat[:, 1, :], sq, AX.X, ALU.add).then_inc(ready, 1)

            def norm_end():
                own(v.reciprocal(stat[:, 3, :], stat[:, 2, :]))
                own(v.tensor_scalar(stat[:, 4, :], stat[:, 1, :], 1.0 / D, EPS, ALU.mult, ALU.add))
                own(v.tensor_tensor(stat[:, 5, :], stat[:, 3, :], stat[:, 3, :], ALU.mult))
                own(v.tensor_tensor(stat[:, 4, :], stat[:, 4, :], stat[:, 5, :], ALU.mult))
                own(v.tensor_scalar(stat[:, 4, :], stat[:, 4, :], -0.5, 1.5, ALU.mult, ALU.add))
                own(v.tensor_tensor(stat[:, 3, :], stat[:, 3, :], stat[:, 4, :], ALU.mult))

            dve.wait_ge(s_x, 32)
            sq1 = r_p[:, 0:W * D].rearrange("p (w d) -> p w d", w=W)
            dve.wait_ge(s_ub, 16)
            norm_begin(xs, xc, sq1, s_sqr)
            dve.wait_ge(s_sqr, 1)
            dve.wait_ge(s_sd, 1)
            norm_end()
            own(v.tensor_tensor(xs, xs, ub2b.unsqueeze(1).broadcast_to([128, W, D]), ALU.add))

            own(v.memset(wtab, 0.0))
            for b in range(W - 1):
                own(v.scalar_tensor_tensor(wtab, pair_no, small(3)[:, b:b + 1], wtab, ALU.is_ge, ALU.add))
            v.tensor_copy(wtab_i[:, :], wtab).then_inc(s_wtab, 1)

            dbase = made[0]
            OWN = 4

            def step(k, par):
                n = [0]

                def own2(ins):
                    ins.then_inc(dv, 1)
                    n[0] += 1
                    dve.wait_ge(dv, OWN * k + (dbase + n[0]))
                rk = rec[0:EP, par]

                def cols(a, dims=1):
                    return a[0:EP, k * CH:(k + 1) * CH] if isinstance(k, int) else a[0:EP, ds(k * CH, CH)]
                if static_ge(k, 2):
                    dve.wait_ge(s_sc[par], 8 * CH * k if par == 0 else 8 * CH * k - 8 * CH)
                if isinstance(k, int) and k == 0:
                    dve.wait_ge(s_pad, 16 * (-(-NT // (2 * CH))))
                gate(dve, s_gd)
                eac = cols(ea)
                own2(v.tensor_copy(rk[:, :, 0:EA], eac))
                own2(v.tensor_tensor(r1[0:EP], eac, rk[:, :, 0:EA], ALU.subtract))
                own2(v.tensor_copy(rk[:, :, 3 * EA:4 * EA], r1[0:EP]))
                v.tensor_copy(rk[:, :, 4 * EA:5 * EA], r1[0:EP])
                v.tensor_copy(rk[:, :, EA:2 * EA], eac)
                v.tensor_copy(rk[:, :, 2 * EA:3 * EA], eac)
                v.tensor_tensor(rk[:, :, 5 * EA:6 * EA], r1[0:EP], rk[:, :, 3 * EA:4 * EA], ALU.subtract)
                v.tensor_copy(rk[:, :, KE:KE + 2].bitcast(I32), cols(dst_i).unsqueeze(2))
                v.tensor_copy(rk[:, :, KE + 2:KE + 3], cols(lo_b).unsqueeze(2))
                v.tensor_copy(idx_s[0:EP, par, :], cols(idx)).then_inc(s_chunk, 1)
                if static_ge(k, 1):
                    dve.wait_ge(s_hist, k)
                v.tensor_tensor(oh_lo[0:EP], cols(lo_b).unsqueeze(2).broadcast_to([EP, CH, 128]),
                                iota[0:EP, :].unsqueeze(1).broadcast_to([EP, CH, 128]), ALU.is_equal).then_inc(s_oh, 1)
                dve.wait_ge(s_oh, 2 * k + 1)
                v.tensor_tensor(oh_hi[0:EP], cols(hi_b).unsqueeze(2).broadcast_to([EP, CH, W]),
                                iota_w[0:EP, :].unsqueeze(1).broadcast_to([EP, CH, W]), ALU.is_equal).then_inc(s_oh, 1)
                if static_ge(k, 1):
                    dve.wait_ge(s_tp, k)
                xk = lambda a: a[:, k, :] if isinstance(k, int) else a[:, ds(k, 1), :].rearrange("p a d -> p (a d)")
                stk = stat[:, 3, k:k + 1] if isinstance(k, int) else stat[:, 3, ds(k, 1)]
                v.tensor_scalar(xstage, xk(xc), stk, None, ALU.mult).then_inc(s_xst, 1)
                dve.wait_ge(s_xst, k + 1)
                own2(v.tensor_tensor(xk(xs), xk(xs), xstage, ALU.add))
                assert n[0] == OWN
                pd1 = P12[:, k, 0, :] if isinstance(k, int) else P12[:, ds(k, 1), 0, :].rearrange("p a h -> p (a h)")
                pd2 = P12[:, k, 1, :] if isinstance(k, int) else P12[:, ds(k, 1), 1, :].rearrange("p a h -> p (a h)")
                dve.wait_ge(s_pq1, 2 * k + 1)
                v.tensor_tensor(pd2, ps[1][:, :], pd1, ALU.subtract).then_inc(s_pq2, 1)
                dve.wait_ge(s_pq1, 2 * k + 2)
                v.tensor_tensor(qst[:, par, H:2 * H], ps[2][:, :], qst[:, par, 0:H], ALU.subtract).then_inc(s_pq2, 1)
            paired(dve, W, step)
            made[0] = dbase + OWN * W
            dve.wait_ge(s_hist, W)
            v.tensor_copy(deg_s[:, :], ps[4][:, 0:W]).then_inc(s_deg, 1)
            v.memset(r_h[:, :], 0.0).then_inc(s_hz, 1)
            dve.wait_ge(s_hz, 1)

            def one_hot(j, t):
                v.tensor_scalar(oh[:, j, :], iota[:, :], recg[:, j // 4, j % 4, KE + 2:KE + 3], None,
                                ALU.is_equal).then_inc(e_oh, 1)

            def accumulate(p):
                wi = v.value_load(wtab_i[0:1, p:p + 1] if isinstance(p, int) else wtab_i[0:1, ds(p, 1)],
                                  min_val=0, max_val=W - 1)
                acc = Hacc[:, ds(wi, 1), :].rearrange("p a h -> p (a h)")
                return acc

            def edge_body(i, last=False):
                for j in range(8):
                    t = 8 * i + j
                    if j % 2 == 0 and (static_ge(i, 1) or j >= 4):
                        p = 4 * i + j // 2 - 2
                        dve.wait_ge(e_agg, 2 * p + 2)
                        if static_ge(p, 1):
                            dve.wait_ge(e_acc, p)
                        acc = accumulate(p)
                        v.tensor_tensor(acc, acc, ps[4 + (j // 2) % 2][:, :], ALU.add).then_inc(e_acc, 1)
                    dve.wait_ge(e_h1, t + 1)
                    v.scalar_tensor_tensor(h2[:, j % 4, :], ps[j % 4][:, :], 0.0, h1[:, j % 4, :],
                                           ALU.max, ALU.subtract).then_inc(e_h2, 1)
                    ja = j + 6
                    if not last or ja < 8:
                        if ja % 4 == 0:
                            dve.wait_ge(e_rec[(ja // 4) % 2], 16 * (i + 1 + ja // 8))
                        if static_ge(i, 1) or j >= 2:
                            dve.wait_ge(e_agg, t - 1)
                        one_hot(ja % 8, t + 6)
            dve.wait_ge(e_rec[0], 16)
            for j in range(4):
                one_hot(j, j)
            dve.wait_ge(e_rec[1], 16)
            for j in range(4, 6):
                one_hot(j, j)
            edge_body(0)
            with dve.Fori(1, NT // 8 - 1) as i:
                edge_body(i)
            edge_body(NT // 8 - 1, last=True)
            for p in (PAIRS - 2, PAIRS - 1):
                dve.wait_ge(e_agg, 2 * p + 2)
                dve.wait_ge(e_acc, p)
                acc = accumulate(p)
                v.tensor_tensor(acc, acc, ps[4 + p % 2][:, :], ALU.add).then_inc(e_acc, 1)
            dve.wait_ge(e_acc, PAIRS)

            def update_chunk(c, n):
                for j in range(n):
                    t = 4 * c + j
                    if static_ge(c, 1) or j >= 1:
                        dve.wait_ge(u_tr, t)
                    src_t = Hacc[:, t, :] if isinstance(t, int) else Hacc[:, ds(t, 1), :].rearrange("p a h -> p (a h)")
                    v.tensor_scalar(hst, src_t, finv, None, ALU.mult).then_inc(u_st, 1)
                    if j == 0 and static_ge(c, 1):
                        dve.wait_ge(u_ag, 2 * c)
                    dt = deg_s[:, t:t + 1] if isinstance(t, int) else deg_s[:, ds(t, 1)]
                    v.tensor_scalar(diag[:, j * 128:(j + 1) * 128], ident[:, :], dt, None, ALU.mult).then_inc(u_dg, 1)
                for j in range(n):
                    t = 4 * c + j
                    dve.wait_ge(u_o, t + 1)
                    xt = xs[:, t, :] if isinstance(t, int) else xs[:, ds(t, 1), :].rearrange("p a d -> p (a d)")
                    v.tensor_tensor(xt, xt, ps[5 + j % 2][:, 0:D], ALU.add).then_inc(u_x, 1)
            update_chunk(0, 4)
            with dve.Fori(1, NCH) as c:
                update_chunk(c, 4)
            update_chunk(NCH, 1)
            dve.wait_ge(u_x, W)

            for r in range(2):
                norm_begin(xs if r == 0 else z, z, zsq, z_sq)
                dve.wait_ge(z_sq, r + 1)
                dve.wait_ge(z_sd, r + 1)
                norm_end()
                own(v.tensor_tensor(z, z, stat[:, 3, :].unsqueeze(2).broadcast_to([128, W, D]), ALU.mult))
            dve.wait_ge(z_gb, 48)
            own(v.tensor_tensor(z, z, gam.unsqueeze(1).broadcast_to([128, W, D]), ALU.mult))
            own(v.tensor_tensor(z, z, bet.unsqueeze(1).broadcast_to([128, W, D]), ALU.add))
            dve.wait_ge(f_w2, 32)

            def z_tile(k, par):
                if static_ge(k, 1):
                    dve.wait_ge(z_tr, k)
                zk = z[:, k, :] if isinstance(k, int) else z[:, ds(k, 1), :].rearrange("p a d -> p (a d)")
                gate(dve, s_gd)
                v.tensor_copy(zst, zk).then_inc(z_st, 1)
                dve.wait_ge(z_lg, k + 1)
                lk = lg[:, k, :] if isinstance(k, int) else lg[:, ds(k, 1), :].rearrange("p a d -> p (a d)")
                v.tensor_tensor(lk, ps[2][:, 0:NX], brb[:, :], ALU.add).then_inc(z_le, 1)
            paired(dve, W, z_tile)
            dve.wait_ge(z_le, W)

            bc = lambda a: a.unsqueeze(2).broadcast_to([128, W, NX])
            rio = riota[:, :].unsqueeze(1).broadcast_to([128, W, NX])
            def pick(logits, value, hot, scratch, first):
                own(v.tensor_reduce(value, logits, AX.X, ALU.max))
                own(v.tensor_tensor(scratch, logits, bc(value), ALU.is_equal))
                own(v.tensor_tensor(scratch, scratch, rio, ALU.mult))
                own(v.tensor_reduce(first, scratch, AX.X, ALU.max))
                own(v.tensor_tensor(hot, rio, bc(first), ALU.is_equal))
            pick(lg, rs[:, 0, :], rt[:, 0], rt[:, 2], rs[:, 7, :])
            own(v.tensor_scalar(rt[:, 2], rt[:, 0], -1.0, 1.0, ALU.mult, ALU.add))
            own(v.tensor_tensor(rt[:, 2], rt[:, 2], lg, ALU.mult))
            own(v.scalar_tensor_tensor(rt[:, 3].rearrange("p a b -> p (a b)"), rt[:, 0].rearrange("p a b -> p (a b)"), -3.0e38,
                                       rt[:, 2].rearrange("p a b -> p (a b)"), ALU.mult, ALU.add))
            pick(rt[:, 3], rs[:, 1, :], rt[:, 1], rt[:, 2], rs[:, 7, :])
            v.tensor_tensor(rs[:, 2, :], rs[:, 1, :], rs[:, 0, :], ALU.subtract).then_inc(z_d, 1)
            dve.wait_ge(z_ex, 1)
            own(v.tensor_scalar(rs[:, 4, :], rs[:, 3, :], 1.0, None, ALU.add))
            own(v.reciprocal(rs[:, 5, :], rs[:, 4, :]))
            own(v.tensor_tensor(rs[:, 6, :], rs[:, 5, :], rs[:, 3, :], ALU.mult))
            own(v.tensor_tensor(rt[:, 0], rt[:, 0], bc(rs[:, 5, :]), ALU.mult))
            own(v.tensor_tensor(rt[:, 1], rt[:, 1], bc(rs[:, 6, :]), ALU.mult))
            v.tensor_tensor(wf, rt[:, 0], rt[:, 1], ALU.add).then_inc(z_wf, 1)
            dve.wait_ge(z_wf, 1)
            def bias_tile(k, par):
                if static_ge(k, 1):
                    dve.wait_ge(b_tr, k)
                wk = wf[:, k, :] if isinstance(k, int) else wf[:, ds(k, 1), :].rearrange("p a d -> p (a d)")
                gate(dve, s_gd)
                v.tensor_copy(zst[:, 0:NX], wk).then_inc(z_wf, 1)
                dve.wait_ge(b_o, k + 1)
                xk = xs[:, k, :] if isinstance(k, int) else xs[:, ds(k, 1), :].rearrange("p a d -> p (a d)")
                v.tensor_tensor(xk, xk, ps[2][:, 0:D], ALU.add).then_inc(b_x, 1)
            paired(dve, W, bias_tile)
            dve.wait_ge(b_x, W)

            def expert_chunk(c, n):
                for e in range(NX):
                    for j in range(n):
                        q = 4 * NX * c + e * n + j
                        t = 4 * c + j
                        dve.wait_ge(f_o, q + 1)
                        if static_ge(q, n):
                            dve.wait_ge(f_x, q + 1 - n) if (static_ge(c, 1) or e >= 1) else None
                        if isinstance(t, int):
                            xt, we = xs[:, t, :], wf[:, t, e:e + 1]
                        else:
                            xt = xs[:, ds(t, 1), :].rearrange("p a d -> p (a d)")
                            we = wf[:, ds(t, 1), e:e + 1].rearrange("p a d -> p (a d)")
                        v.scalar_tensor_tensor(xt, ps[4 + (j if n == 4 else e % 4)][:, 0:D], we, xt,
                                               ALU.mult, ALU.add).then_inc(f_x, 1)
            expert_chunk(0, 4)
            with dve.Fori(1, NCH) as c:
                expert_chunk(c, 4)
            expert_chunk(NCH, 1)

        @block.tensor
        def _(pe):
            mm = nc.tensor.matmul
            pe.wait_ge(s_cst, 12)
            pe.wait_ge(s_cnt, 1)
            cnt = sq_rows[0:EP, W:2 * W]
            mm(ps[6][:, 0:W], ones[0:EP, :], cnt, start=True, stop=True)
            mm(ps[6][0:EP, 32:32 + W], before[0:EP, 0:EP], cnt, start=True, stop=True).then_inc(s_tot, 1)

            pe.wait_ge(s_f, 1)

            def node_tile(k, par):
                first, last = isinstance(k, int) and k == 0, isinstance(k, int) and k == W - 1
                pe.wait_ge(s_xst, k + 1)
                if static_ge(k, 1):
                    pe.wait_ge(s_xT, 2 * k)
                for m in range(KD):
                    ins = nc.tensor.transpose(ps[0][:, m * 128:(m + 1) * 128], xstage[:, m * 128:(m + 1) * 128], ident[:, :])
                ins.then_inc(s_tp, 1)
                pe.wait_ge(s_xT, 2 * k + 1)
                for q in range(2):
                    if static_ge(k, 1):
                        pe.wait_ge(s_pq2, 2 * k - 1 + q)
                    for m in range(KD):
                        ins = mm(ps[1 + q][:, :], xTst[:, m, :], wAB[:, KD * q + m, :], start=(m == 0), stop=(q == 1 and m == KD - 1))
                    if q == 0:
                        ins = mm(ps[1][:, :], ones[0:1, :], b1row[0:1, :], start=False, stop=True)
                    ins.then_inc(s_pq, 1)
                pe.wait_ge(s_oh, 2 * k + 2)
                for c in range(CH):
                    ins = mm(ps[4][:, 0:W], oh_lo[0:EP, c, :], oh_hi[0:EP, c, :], start=(first and c == 0), stop=(last and c == CH - 1),
                             skip_group_check=True)
                ins.then_inc(s_hist, 1)
            paired(pe, W, node_tile)

            def transposes(par):
                tb = ps[7][:, :].bitcast(BF16)
                for j in range(4):
                    nc.tensor.transpose(tb[:, j * 128:(j + 1) * 128], recg[:, par, j, :], identb[:, :])
                for j in range(4):
                    ins = nc.tensor.transpose(tb[:, (4 + j) * 128:(5 + j) * 128], oh[:, 4 * par + j, :], identb[:, :])
                ins.then_inc(e_tr, 1)

            def group(g, par, first=False):
                pe.wait_ge(e_rec[par], 8 * g + 16 if par == 0 else 8 * g + 8)
                pe.wait_ge(e_oh, 4 * g + 4)
                if not first:
                    pe.wait_ge(e_te, g)
                transposes(par)

            def aggregate(j, t, first):
                pe.wait_ge(e_h2, t + 1)
                if j % 2 == 0 and not first:
                    pe.wait_ge(e_acc, (4 * ((t - j) // 8) if isinstance(t, int) else None) if False else t_half(t, j))
                bank = ps[4 + (j // 2) % 2]
                mm(bank[:, :], oh[:, j, :], h1[:, j % 4, :], start=(j % 2 == 0), stop=False)
                mm(bank[:, :], oh[:, j, :], h2[:, j % 4, :], start=False, stop=(j % 2 == 1)).then_inc(e_agg, 1)

            def t_half(i4, j):
                return i4

            def agg(i, j, first_pairs=False):
                t = 8 * i + j
                pe.wait_ge(e_h2, t + 1)
                if j % 2 == 0 and not first_pairs:
                    pe.wait_ge(e_acc, 4 * i + j // 2 - 1)
                bank = ps[4 + (j // 2) % 2]
                mm(bank[:, :], oh[:, j, :], h1[:, j % 4, :], start=(j % 2 == 0), stop=False)
                mm(bank[:, :], oh[:, j, :], h2[:, j % 4, :], start=False, stop=(j % 2 == 1)).then_inc(e_agg, 1)

            def edge_body(i, last=False):
                for j in range(8):
                    t = 8 * i + j
                    if j % 4 == 0:
                        pe.wait_ge(e_te, 2 * i + 1 + j // 4)
                    if static_ge(i, 1) or j >= 4:
                        pe.wait_ge(e_h2, t - 3)
                    if j % 2 == 0:
                        p = 4 * i + j // 2
                        wi = nc.tensor.value_load(wtab_i[0:1, p:p + 1] if isinstance(p, int) else wtab_i[0:1, ds(p, 1)],
                                                  min_val=0, max_val=W - 1)
                    bank = ps[j % 4][:, :]
                    ohT = trs[:, j // 4, (4 + j % 4) * 128:(5 + j % 4) * 128]
                    mm(bank, trs[0:KE, j // 4, (j % 4) * 128:(j % 4 + 1) * 128], C6[:, :], start=True, stop=False)
                    mm(bank, ohT, P12[:, ds(wi, 1), 0, :].rearrange("p a h -> p (a h)"), start=False, stop=False)
                    mm(bank, ohT, P12[:, ds(wi, 1), 1, :].rearrange("p a h -> p (a h)"), start=False, stop=False)
                    pe.wait_ge(e_q[j], 16 * (i + 1))
                    mm(bank, identb[:, :], qg[:, j, 0:H], start=False, stop=False)
                    mm(bank, identb[:, :], qg[:, j, H:2 * H], start=False, stop=True).then_inc(e_s, 1)
                    if j >= 2:
                        agg(i, j - 2, first_pairs=not static_ge(i, 1) and j - 2 < 4)
                    elif static_ge(i, 1):
                        agg(i - 1, j + 6, first_pairs=False)
                    if j == 2:
                        group(2 * i + 1, 1)
                    if j == 6 and not last:
                        group(2 * i + 2, 0)
            pe.wait_ge(s_wtab, 1)
            pe.wait_ge(s_c6, 96)
            pe.wait_ge(s_pq2, 2 * W)
            group(0, 0, first=True)
            edge_body(0)
            with pe.Fori(1, NT // 8 - 1) as i:
                edge_body(i)
            edge_body(NT // 8 - 1, last=True)
            agg(NT // 8 - 1, 6)
            agg(NT // 8 - 1, 7)

            pe.wait_ge(u_w, 48)
            pe.wait_ge(u_mb, 16)

            def update_chunk(c, n):
                cols = n * 128
                c0 = 512 * c
                nodes = lambda a: a[:, c0:c0 + cols] if isinstance(c, int) else a[:, ds(c0, cols)]
                for j in range(n):
                    t = 4 * c + j
                    pe.wait_ge(u_st, t + 1)
                    if static_ge(c, 1) or j >= 1:
                        pe.wait_ge(u_ht, t)
                    for m in range(KH):
                        ins = nc.tensor.transpose(ps[0][:, m * 128:(m + 1) * 128], hst[:, m * 128:(m + 1) * 128], ident[:, :])
                    ins.then_inc(u_tr, 1)
                pe.wait_ge(u_ht, 4 * c + n)
                pe.wait_ge(u_dg, 4 * c + n)
                for m in range(KD):
                    if static_ge(c, 1):
                        pe.wait_ge(u_ae, 2 * c - 1 + m)
                    for k in range(KH):
                        mm(ps[1 + m][:, 0:cols], mW2s[:, k, m * 128:(m + 1) * 128], HT[:, k, 0:cols], start=(k == 0), stop=False)
                    mm(ps[1 + m][:, 0:cols], mb2b[:, m * 128:(m + 1) * 128], diag[:, 0:cols], start=False, stop=True).then_inc(u_ag, 1)
                pe.wait_ge(u_ae, 2 * c + 2)
                for m in range(KH):
                    if static_ge(c, 1) or m >= 2:
                        pe.wait_ge(u_ue, 4 * c + m - 1)
                    for k in range(2 * KD):
                        rhs = nodes(xnT[:, k, :]) if k < KD else aggT[:, k - KD, 0:cols]
                        ins = mm(ps[3 + m % 2][:, 0:cols], uW1s[:, k, m * 128:(m + 1) * 128], rhs, start=(k == 0), stop=(k == 2 * KD - 1))
                    ins.then_inc(u_u, 1)
                pe.wait_ge(u_ue, 4 * c + 4)
                for j in range(n):
                    t = 4 * c + j
                    if static_ge(c, 1) or j >= 2:
                        pe.wait_ge(u_x, t - 1)
                    for k in range(KH):
                        ins = mm(ps[5 + j % 2][:, 0:D], uT[:, k, j * 128:(j + 1) * 128], uW2s[:, k, :], start=(k == 0), stop=(k == KH - 1))
                    ins.then_inc(u_o, 1)
            update_chunk(0, 4)
            with pe.Fori(1, NCH) as c:
                update_chunk(c, 4)
            update_chunk(NCH, 1)

            def z_tile(k, par):
                pe.wait_ge(z_st, k + 1)
                if static_ge(k, 1):
                    pe.wait_ge(z_te, 2 * k)
                for m in range(KD):
                    ins = nc.tensor.transpose(ps[0][:, m * 128:(m + 1) * 128], zst[:, m * 128:(m + 1) * 128], ident[:, :])
                ins.then_inc(z_tr, 1)
                pe.wait_ge(z_te, 2 * k + 1)
                if static_ge(k, 1):
                    pe.wait_ge(z_le, k)
                for m in range(KD):
                    ins = mm(ps[2][:, 0:NX], zTst[:, m, :], Wrs[:, m, :], start=(m == 0), stop=(m == KD - 1))
                ins.then_inc(z_lg, 1)
            paired(pe, W, z_tile)

            def bias_tile(k, par):
                pe.wait_ge(z_wf, k + 2)
                if static_ge(k, 1):
                    pe.wait_ge(b_te, k)
                nc.tensor.transpose(ps[1][0:NX, 0:128], zst[:, 0:NX], ident[:, :]).then_inc(b_tr, 1)
                pe.wait_ge(b_te, k + 1)
                if static_ge(k, 1):
                    pe.wait_ge(b_x, k)
                mm(ps[2][:, 0:D], wfT[0:NX, :], b2s[0:NX, :], start=True, stop=True).then_inc(b_o, 1)
            paired(pe, W, bias_tile)

            pe.wait_ge(f_w1, 16)
            pe.wait_ge(f_w2, 32)
            pe.wait_ge(b_x, W)

            def expert_chunk(c, n):
                cols = n * 128
                c0 = 512 * c
                nodes = lambda a: a[:, c0:c0 + cols] if isinstance(c, int) else a[:, ds(c0, cols)]

                def hidden(e):
                    for m in range(KH):
                        q = NX * KH * c + e * KH + m
                        if static_ge(c, 1) or e >= 1:
                            pe.wait_ge(f_he, q - KH + 1)
                        elif False:
                            pass
                        for k in range(KD):
                            ins = mm(ps[m][:, 0:cols], W1s[:, e, k, m * 128:(m + 1) * 128], nodes(xnT[:, k, :]),
                                     start=(k == 0), stop=(k == KD - 1))
                        ins.then_inc(f_h, 1)

                def output(e):
                    w2 = (w2lo if e < NX // 2 else w2hi)
                    e4 = e % (NX // 2)
                    pe.wait_ge(f_he, NX * KH * c + (e + 1) * KH)
                    for j in range(n):
                        q = 4 * NX * c + e * n + j
                        b = j if n == 4 else e % 4
                        if static_ge(c, 1) or (e >= 1 if n == 4 else True):
                            pe.wait_ge(f_x, q - 3)
                        for k in range(KH):
                            ins = mm(ps[4 + b][:, 0:D], hT[:, e % 2, k, j * 128:(j + 1) * 128], w2[:, e4 * KH + k, :],
                                     start=(k == 0), stop=(k == KH - 1))
                        ins.then_inc(f_o, 1)
                hidden(0)
                for e in range(NX):
                    if e + 1 < NX:
                        hidden(e + 1)
                    output(e)
            expert_chunk(0, 4)
            with pe.Fori(1, NCH) as c:
                expert_chunk(c, 4)
            expert_chunk(NCH, 1)


_INS = ['x', 'src', 'dst', 'edge_attr_16', 'L0_gnn_mW1', 'L0_gnn_mb1', 'L0_gnn_mW2', 'L0_gnn_mb2', 'L0_gnn_uW1',
        'L0_gnn_ub1', 'L0_gnn_uW2', 'L0_gnn_ub2', 'L0_ffn_gamma', 'L0_ffn_beta', 'L0_ffn_Wr', 'L0_ffn_br',
        'L0_ffn_W1', 'L0_ffn_b1', 'L0_ffn_W2', 'L0_ffn_b2']
_OUTS = [((3125, 256), 'float32')]


def kernel(**inputs):
    import numpy as _np
    import concourse.bacc as _bacc
    from concourse import mybir as _mybir
    from concourse.bass_utils import run_bass_kernel_spmd as _run

    nc = _bacc.Bacc("TRN2", target_bir_lowering=False, num_devices=1)
    arrays, args = {}, []
    for name in _INS:
        a = _np.ascontiguousarray(inputs[name])
        arrays[f"in_{name}_dram"] = a
        args.append(nc.dram_tensor(f"in_{name}_dram", a.shape, _mybir.dt.from_np(a.dtype), kind="ExternalInput").ap())
    for i, (shape, dtype) in enumerate(_OUTS):
        dt = _mybir.dt.from_np(_np.dtype(dtype))
        args.append(nc.dram_tensor(f"out_{i}_dram", shape, dt, kind="ExternalOutput").ap())
    build_kernel(nc, *args)
    r = _run(nc, [arrays], core_ids=[0])
    got = tuple(r.results[0][f"out_{i}_dram"] for i in range(len(_OUTS)))
    return got[0]
```

```python
from contextlib import ExitStack

import concourse.bass as bass
from concourse import mybir


def build_kernel(nc, x, src, dst, edge_attr, mW1, mb1, mW2, mb2, uW1, ub1, uW2, ub2,
                 gamma, beta, Wr, br, W1, b1, W2, b2, out):
    F32, F16, BF16, I32 = mybir.dt.float32, mybir.dt.float16, mybir.dt.bfloat16, mybir.dt.int32
    ALU = mybir.AluOpType
    ACT = mybir.ActivationFunctionType
    AX = mybir.AxisListType
    ds = bass.ds

    N, D = x.shape
    E, EA = edge_attr.shape
    H = mW2.shape[0]
    NX, DM, HE = W1.shape
    EPS = 1e-5
    W = -(-N // 128)
    NP = W * 128
    TAIL = N - (W - 1) * 128
    EP = 125
    EC = E // EP
    PAIRS = (E + W * 255) // 256
    NT = 2 * PAIRS
    CH = EC // W
    REC = 128
    KE = 6 * EA
    NA = 2 * NP
    NTE = (NA + NX * 127) // 128
    ZW = D + 2
    PLACE, WEIGHT = D, D + 1
    KD, KH = D // 128, H // 128
    WC = KD * H
    NO_NODE = 200.0
    assert KH * DM == WC and HE == H and NTE == 57 and D == DM
    assert EP * EC == E and CH * W == EC and NT % 8 == 0 and W % 2 == 1

    recs_d = nc.dram_tensor("recs_d", [128 * NT, REC], BF16, kind="Internal").ap()
    z_d = nc.dram_tensor("z_d", [128 * NTE, ZW], F32, kind="Internal").ap()
    y_d = nc.dram_tensor("y_d", [NA + 128 * NTE, D], F32, kind="Internal").ap()
    q_d = nc.dram_tensor("q_d", [NP, 2 * H], F16, kind="Internal").ap()

    with ExitStack() as ctx:
        def sb(name, shape, dt=F32):
            return ctx.enter_context(nc.sbuf_tensor("sb_" + name, list(shape), dt))

        def sem(name):
            return ctx.enter_context(nc.semaphore(name))

        r_xs = sb("r_xs", [128, W * D])
        r_xt = sb("r_xt", [128, KD * NP])
        r_p = sb("r_p", [128, W * H])
        r_h = sb("r_h", [128, W * H])
        r_w = sb("r_w", [128, 12288])

        xs = r_xs[:, :].rearrange("p (w d) -> p w d", w=W)
        xnT = r_xt[:, :].rearrange("p (k n) -> p k n", k=KD)
        P12 = r_p[:, :].bitcast(F16).rearrange("p (w s h) -> p w s h", w=W, s=2)
        Hacc = r_h[:, :].rearrange("p (w h) -> p w h", w=W)
        scan = r_p[:, 0:W * EC].rearrange("p (b c) -> p b c", b=W)
        xc = r_h[:, 0:W * D].rearrange("p (w d) -> p w d", w=W)
        ea = r_h[:, W * D:W * D + EC * EA].rearrange("p (c a) -> p c a", c=EC)

        def carve(region, start):
            at = [start]

            def take(shape, dt=F32):
                n = 1
                for s in shape:
                    n *= s
                words = n if dt in (F32, I32) else n // 2
                a = region[:, at[0]:at[0] + words]
                at[0] += words
                assert at[0] <= region.shape[1], (at[0], region.shape)
                if dt != F32:
                    a = a.bitcast(dt)
                if len(shape) == 2:
                    a = a.rearrange("p (a b) -> p a b", a=shape[0])
                if len(shape) == 3:
                    a = a.rearrange("p (a b c) -> p a b c", a=shape[0], b=shape[1])
                return a
            return take

        t1 = carve(r_w, 0)
        hi_b = t1([EC], BF16)
        lo_b = t1([EC], BF16)
        dst_i = t1([EC], I32)
        idx = t1([EC], I32)
        rec = t1([2, CH, REC], BF16)
        idx_s = t1([2, CH], I32)
        oh_lo = t1([CH, 128], BF16)
        oh_hi = t1([CH, W], BF16)
        wAB = t1([4, H])
        b1row = t1([H])
        xstage = t1([D])
        xTst = t1([KD, 128])
        qst = t1([2, 2 * H], F16)
        r1 = t1([CH, EA])
        sq_rows = t1([256])
        pair_no = t1([PAIRS])
        wtab = t1([PAIRS])
        ub2b = t1([D])
        mask = r_h[:, 0:W * EC // 2].bitcast(BF16).rearrange("p (b c) -> p b c", b=W)
        cdup = r_p[0:KE, 11700:11700 + H]
        t3 = carve(r_w, 0)
        recg = t3([2, 4, REC], BF16)
        trs = t3([2, 8 * 128], BF16)
        oh = t3([8, 128], BF16)
        qg = t3([8, 2 * H], F16)
        h1 = t3([4, H], F16)
        h2 = t3([4, H], F16)
        wst = t1([2, WC])
        t4 = carve(r_w, 0)
        HT = [t4([KH, H]), t4([KH, H])]
        aggT = t4([KD, H])
        uT = t4([KH, H])
        t4w = carve(r_w, 8192)
        mW2s = t4w([KH, D])
        uW1s = t4w([2 * KD, H])
        uW2s = t4w([KH, D])
        t4p = carve(r_p, 0)
        hst = t4p([H])
        diag = t4p([H])
        mb2b = t4p([D])
        zst = t4p([2, D])
        zTst = t4p([KD, 128])
        gam = t4p([D])
        bet = t4p([D])
        bns = t4p([8])
        mv = t4p([2, 8])
        zr = t4p([6, 4])
        z3 = r_h[:, 0:W * ZW].rearrange("p (w c) -> p w c", w=W)
        z16 = r_h[:, 0:W * ZW].bitcast(F16).rearrange("p (w c) -> p w c", w=W)
        W1p = r_p[:, 0:NX * WC].bitcast(F16).rearrange("p (e s k h) -> p e s k h", e=NX, s=2, k=KD)
        W2p = r_w[:, 4096:4096 + NX * WC].bitcast(F16).rearrange("p (e s k d) -> p e s k d", e=NX, s=2, k=KH)
        wstage = r_xt[:, 0:6 * WC].rearrange("p (r w) -> p r w", r=6)
        t5 = carve(r_w, 0)
        rt = t5([4, W, NX])
        wf = t5([W, NX])
        rs = t5([8, W])
        m2 = t5([NX, 2 * W])
        s2 = t5([NX, 2 * W])
        pr = t5([8, NX])
        slot_f = t5([2 * W])
        t5p = carve(r_p, NX * WC)
        zt = t5p([4, ZW])
        yo = t5p([4, D])
        zT = t5p([2, 2 * KD, 128], F16)
        hp = t5p([2, 2 * KH, 128], F16)
        t5x = carve(r_h, W * ZW)
        h32 = t5x([2, H])
        b2r = t5x([NX, D], BF16)
        b2s = t5x([D])
        b2p = [t5x([D], BF16) for _ in range(3)]
        y_in = r_p[:, :].rearrange("p (w s d) -> p w s d", w=W, s=2)

        C6 = sb("C6", [KE, H], BF16)
        ident = sb("ident", [128, 128])
        identb = sb("identb", [128, 128], BF16)
        identh = sb("identh", [128, 128], F16)
        ones3 = sb("ones3", [3, 128], BF16)
        place = sb("place", [128, 2, W], I32)
        before = sb("before", [128, 128])
        iota = sb("iota", [128, 128], BF16)
        iota_w = sb("iota_w", [128, W], BF16)
        ones = sb("ones", [128, 128])
        wtab_i = sb("wtab_i", [128, PAIRS], I32)
        deg_s = sb("deg_s", [128, W])
        ub1c = sb("ub1c", [128, KH])
        Wrs = sb("Wrs", [128, KD, NX])
        brb = sb("brb", [128, NX])
        b1c = sb("b1c", [128, NX, KH])
        lg = sb("lg", [128, W, NX])
        fro = sb("fro", [128, 20])
        frs = sb("frs", [128, 3])
        sx = sb("sx", [128, 16])
        sxi = sb("sxi", [128, 8], I32)
        etab = sb("etab", [128, NTE + 3])
        etab_i = sb("etab_i", [128, NTE + 3], I32)
        tile_no = sb("tile_no", [128, NTE + 3])
        slot_i = sb("slot_i", [128, 2 * W], I32)
        padm = sb("padm", [128, NTE, 2])
        epsc = sb("epsc", [128, 1])
        mx = sb("mx", [128, 8])
        mxa = sb("mxa", [128, 8])
        sc = sb("sc", [128, 8])
        sci = sb("sci", [128, 8], I32)
        stat = sb("stat", [128, 6, W])
        riota = sb("riota", [128, NX])
        f_sc, finv = sc[:, 1:2], sc[:, 2:3]
        g_z, g_1, g_h, g_2 = (sx[:, n:n + 1] for n in range(4))
        un1, g_o, un2 = (sx[:, n:n + 1] for n in range(4, 7))

        ps = [ctx.enter_context(nc.psum_tensor(f"ps{i}", [128, 512], F32)) for i in range(8)]

        s_src = sem("src_loaded")
        s_x = sem("x_loaded")
        s_ea = sem("edges_loaded")
        s_w = sem("weights_loaded")
        s_cr = sem("c_replicated")
        s_c6 = sem("c6_placed")
        s_cst = sem("constants_made")
        s_pad = sem("pads_written")
        s_padm = sem("pads_made")
        dv = sem("dve_done")
        s_mx = sem("maxima_made")
        s_all = sem("maxima_reduced")
        s_f = sem("scale_made")
        s_sp = sem("c_split")
        s_cnt = sem("counts_made")
        s_tot = sem("totals_made")
        s_sqr = sem("variance_made")
        s_sd = sem("deviation_made")
        s_chunk = sem("chunk_made")
        s_sc = [sem(f"chunk_scattered{i}") for i in range(2)]
        s_oh = sem("onehots_made")
        s_hist = sem("onehots_counted")
        s_xst = sem("xn_tile_made")
        s_tp = sem("xn_tile_transposed")
        s_xT = sem("xn_tile_evacuated")
        s_pq = sem("pq_made")
        s_pq1 = sem("pq_first_half")
        s_pq2 = sem("pq_second_half")
        s_qst = [sem(f"q_stored{i}") for i in range(2)]
        s_wtab = sem("window_table_made")
        s_deg = sem("degree_made")
        s_ub = sem("ub2_loaded")
        s_wp = sem("small_weights_loaded")
        u_mb = sem("mb2_loaded")
        u_dg = sem("u_diagonal_made")
        s_hz = sem("sums_zeroed")
        e_rec = [sem(f"records_in{i}") for i in range(2)]
        e_oh = sem("tile_onehot_made")
        e_tr = sem("group_transposed")
        e_te = sem("group_evacuated")
        e_q = [sem(f"q_rows_in{i}") for i in range(8)]
        e_s = sem("tile_summed")
        e_h1 = sem("hidden_first_half")
        e_h2 = sem("hidden_second_half")
        e_agg = sem("tile_aggregated")
        e_acc = sem("pair_accumulated")
        u_w = sem("update_weights_loaded")
        u_st = sem("u_sum_staged")
        u_tr = sem("u_sum_transposed")
        u_ht = sem("u_sum_evacuated")
        u_ag = sem("u_agg_made")
        u_ae = sem("u_agg_evacuated")
        u_u = sem("u_hidden_made")
        u_ue = sem("u_hidden_evacuated")
        u_o = sem("u_out_made")
        u_x = sem("u_x_updated")
        s_zp = sem("routed_pads_made")
        s_zw = sem("routed_pads_written")
        n_w = [sem(f"norm_chunk_in{i}") for i in range(2)]
        n_f = sem("norm_chunk_squared")
        n_r = sem("norm_sums_reduced")
        n_t = sem("norm_totals_made")
        n_q = sem("norm_totals_copied")
        n_s = sem("norms_made")
        n_gb = sem("gamma_beta_loaded")
        z_u = sem("z_variances_made")
        z_sd = sem("z_deviations_made")
        z_st = sem("z_tile_staged")
        z_1 = sem("z_first_half")
        z_2 = sem("z_second_half")
        z_tr = sem("z_tile_transposed")
        z_te = sem("z_tile_evacuated")
        z_lg = sem("z_logits_made")
        z_le = sem("z_logits_evacuated")
        z_gap = sem("z_gap_made")
        z_ex = sem("z_gap_exp")
        r_cnt = sem("route_counts_made")
        r_tot = sem("route_totals_made")
        r_slot = sem("route_slots_made")
        r_meta = [sem(f"route_meta_made{i}") for i in range(2)]
        r_sc = [sem(f"routes_scattered{i}") for i in range(2)]
        r_et = sem("expert_table_made")
        w_in = [sem(f"w_chunk_in{i}") for i in range(6)]
        w_a = sem("w_first_half")
        w_b = sem("w_second_half")
        b_in = sem("b2_loaded")
        b_p = sem("b2_parts_made")
        b_r = sem("b2_parts_placed")
        x_in = [sem(f"x_rows_in{i}") for i in range(4)]
        x_tr = sem("x_rows_transposed")
        x_te = sem("x_rows_evacuated")
        x_h = sem("x_hidden_made")
        x_g = sem("x_hidden_gelu")
        x_h1 = sem("x_hidden_first_half")
        x_h2 = sem("x_hidden_second_half")
        x_o = sem("x_out_made")
        x_y = sem("x_out_weighted")
        x_sc = [sem(f"x_out_scattered{i}") for i in range(4)]
        y_ld = [sem(f"y_loaded{i}") for i in range(5)]
        y_ad = sem("y_added")
        s_gp, s_gs, s_gd, s_ga = (sem(f"gates_{n}") for n in ("gpsimd", "sync", "vector", "scalar"))
        s_out = sem("result_stored")

        block = ctx.enter_context(nc.Block())

        def sel(ap, k, n=1):
            return ap[:, k:k + n] if isinstance(k, int) else ap[:, ds(k, n)]

        def gate(eng, passed):
            eng.sem_inc(passed, 1)

        def paired(eng, count, body):
            body(0, 0)
            body(1, 1)
            with eng.Fori(1, count // 2) as i:
                body(2 * i, 0)
                body(2 * i + 1, 1)
            body(count - 1, (count - 1) % 2)

        def static_ge(k, n):
            return (not isinstance(k, int)) or k >= n

        FULL = N - TAIL
        x_full = x[0:FULL, :].rearrange("(w p) d -> p w d", p=128)
        rec_rows = recs_d.rearrange("(q t) r -> q (t r)", q=128)
        row = lambda a: a.rearrange("(o n) -> o n", o=1)
        NCH = W // 4
        CHUNKS = [(c * 4, 4) for c in range(NCH)] + ([(NCH * 4, W - NCH * 4)] if W % 4 else [])
        assert W - NCH * 4 == 1

        src_i = r_p[0:EP, 12250:12250 + EC].bitcast(I32)

        def x_out(w0, m):
            return out[w0 * 128:(w0 + m) * 128, :].rearrange("(w p) d -> p w d", p=128)

        def pair_chunks(eng, update_chunk):
            with eng.Fori(0, (NCH - 2) // 2) as i:
                update_chunk(2 * i + 1, 1, 4, 4, 4)
                update_chunk(2 * i + 2, 0, 4, 4, 4)

        def w_half(n, s):
            half = W1p[:, n, s] if n < NX else W2p[:, n - NX, s]
            return half.rearrange("p k h -> p (k h)")

        def quads(eng, body):
            for T in range(4):
                body(T, 0, T)
            with eng.Fori(1, NTE // 4 - 1) as i:
                for j in range(4):
                    body(4 * i + j, i, j)
            for T in range(NTE // 4 * 4 - 4, NTE):
                body(T, T // 4, T % 4)

        @block.sync
        def _(sp):
            sp.dma_start(src_i, src.rearrange("(p c) -> p c", p=EP)).then_inc(s_src, 16)
            sp.dma_start(ea[0:EP], edge_attr.rearrange("(p c) a -> p c a", p=EP)).then_inc(s_ea, 16)
            sp.dma_start(dst_i[0:EP, :], dst.rearrange("(p c) -> p c", p=EP)).then_inc(s_ea, 16)
            sp.wait_ge(s_padm, 2)
            sp.dma_start(xs[:, 0:W - 1, :], x_full).then_inc(s_x, 16)
            sp.dma_start(xs[0:TAIL, W - 1, :], x[FULL:N, :]).then_inc(s_x, 16)
            sp.dma_start(wAB, mW1[0:2 * D, :].rearrange("(k p) h -> p k h", p=128)).then_inc(s_w, 16)
            sp.dma_start(b1row[0:1, :], row(mb1)).then_inc(s_w, 16)
            for r in range(6):
                sp.dma_start(cdup[r * EA:(r + 1) * EA, :], mW1[2 * D:2 * D + EA, :]).then_inc(s_cr, 16)
            sp.dma_start(ub2b, row(ub2).broadcast_to([128, D])).then_inc(s_ub, 16)
            sp.dma_start(ub1c[:, :], ub1.rearrange("(k p) -> p k", p=128), allow_slow_non_contiguous=True).then_inc(s_wp, 16)
            sp.dma_start(Wrs[:, :, :], Wr.rearrange("(k p) e -> p k e", p=128)).then_inc(s_wp, 16)
            sp.dma_start(brb[:, :], row(br).broadcast_to([128, NX])).then_inc(s_wp, 16)
            sp.dma_start(b1c[:, :, :], b1.rearrange("e (k p) -> p e k", p=128), allow_slow_non_contiguous=True).then_inc(s_wp, 16)
            for n in range(2 * NX):
                if n >= 2:
                    sp.wait_ge(n_f, n - 1)
                mat = W1 if n < NX else W2
                sp.dma_start(wst[:, n % 2, :], mat[n % NX].rearrange("(p a) h -> p (a h)", p=128)).then_inc(n_w[n % 2], 16)
            sp.wait_ge(s_sp, 1)
            for r, part in enumerate((0, 1, 2, 0, 1, 0)):
                sp.dma_start(C6[r * EA:(r + 1) * EA, :], qst[r * EA:(r + 1) * EA, 0, 0:H].bitcast(BF16) if part == 0
                             else qst[r * EA:(r + 1) * EA, 0, H:2 * H].bitcast(BF16) if part == 1
                             else qst[r * EA:(r + 1) * EA, 1, 0:H].bitcast(BF16)).then_inc(s_c6, 16)

            def store_q(k, par):
                sp.wait_ge(s_pq2, 2 * k + 2)
                sp.wait_ge(s_pq1, 2 * k + 2)
                gate(sp, s_gs)
                rows = q_d[k * 128:(k + 1) * 128, :] if isinstance(k, int) else q_d[ds(k * 128, 128), :]
                sp.dma_start(rows, qst[:, par, :]).then_inc(s_qst[par], 16)
            paired(sp, W, store_q)
            for par in range(2):
                sp.wait_ge(s_sc[par], 16 * CH * ((W + 1 - par) // 2))
            sp.wait_ge(s_hz, 1)
            def load_group(g, i, par):
                if static_ge(i, 1):
                    sp.wait_ge(e_tr, g - 1)
                    sp.wait_ge(e_oh, 4 * g - 4)
                    gate(sp, s_gs)
                    for j in range(4):
                        sp.wait_ge(e_q[4 * par + j], 16 * i)
                gate(sp, s_gs)
                cols = (rec_rows[:, g * 4 * REC:(g + 1) * 4 * REC] if isinstance(g, int)
                        else rec_rows[:, ds(g * (4 * REC), 4 * REC)])
                sp.dma_start(recg[:, par, :, :].rearrange("p a b -> p (a b)"), cols).then_inc(e_rec[par], 16)
            load_group(0, 0, 0)
            load_group(1, 0, 1)
            sp.dma_start(mW2s, mW2.rearrange("(k p) d -> p k d", p=128)).then_inc(u_w, 16)
            sp.dma_start(uW1s, uW1.rearrange("(k p) h -> p k h", p=128)).then_inc(u_w, 16)
            sp.dma_start(uW2s, uW2.rearrange("(k p) d -> p k d", p=128)).then_inc(u_w, 16)
            with sp.Fori(1, NT // 8) as i:
                load_group(2 * i, i, 0)
                load_group(2 * i + 1, i, 1)

            sp.wait_ge(e_s, NT)
            sp.dma_start(mb2b, row(mb2).broadcast_to([128, D])).then_inc(u_mb, 16)
            sp.dma_start(gam, row(gamma).broadcast_to([128, D])).then_inc(n_gb, 16)
            sp.dma_start(bet, row(beta).broadcast_to([128, D])).then_inc(n_gb, 16)

            sp.wait_ge(u_u, KH * (NCH + 1))
            for n in range(2 * NX):
                if n >= 6:
                    sp.wait_ge(w_b, n - 5)
                mat = W1 if n < NX else W2
                view = mat[n % NX].rearrange("(k p) h -> p k h", p=128)
                sp.dma_start(wstage[:, n % 6, :].rearrange("p (k h) -> p k h", h=mat.shape[2]), view).then_inc(w_in[n % 6], 16)
                if n == 3:
                    sp.wait_ge(z_2, W)
                    sp.dma_start(b2s[0:NX, :], b2).then_inc(b_in, 16)
            sp.wait_ge(b_p, 1)
            for r in range(3):
                sp.dma_start(b2r[r:r + 1, :, :].rearrange("p e d -> p (e d)"), b2p[r][0:NX, :]).then_inc(b_r, 16)

            for k in range(2):
                sp.wait_ge(r_sc[k], 16 * W)
            def load_rows(T, i, j):
                if static_ge(i, 1):
                    sp.wait_ge(x_sc[j], 16 * i)
                rows = z_d[T * 128:(T + 1) * 128, :] if isinstance(T, int) else z_d[ds(T * 128, 128), :]
                sp.dma_start(zt[:, j, :], rows).then_inc(x_in[j], 16)
            quads(sp, load_rows)

            for j in range(4):
                sp.wait_ge(x_sc[j], 16 * ((NTE + 3 - j) // 4))
            for n in range(5):
                sp.dma_start(y_in[:, 5 * n:5 * n + 5, :, :],
                             y_d[640 * 2 * n:640 * 2 * (n + 1), :].rearrange("(w p s) d -> p w s d", p=128, s=2)).then_inc(y_ld[n], 16)
            for n in range(5):
                sp.wait_ge(y_ad, n + 1)
                m = min(5, W - 1 - 5 * n)
                sp.dma_start(x_out(5 * n, m), xs[:, 5 * n:5 * n + m, :]).then_inc(s_out, 16)
            sp.dma_start(out[FULL:N, :], xs[0:TAIL, W - 1, :]).then_inc(s_out, 16)
            sp.wait_ge(s_out, 96)

        @block.gpsimd
        def _(pool):
            g = nc.gpsimd
            g.memset(xs[:, W - 1, :], 0.0).then_inc(s_padm, 1)
            zero_words = xstage
            g.memset(xstage, 0.0).then_inc(s_zp, 1)
            g.memset(rec[:, :, :, :].rearrange("p a b c -> p (a b c)"), 0.0).then_inc(s_padm, 1)
            pool.wait_ge(s_padm, 2)
            g.memset(rec[:, :, :, KE + 2:KE + 3].rearrange("p a b c -> p (a b c)"), NO_NODE).then_inc(s_padm, 1)
            pool.wait_ge(s_padm, 3)
            per, left = 2 * CH, NT
            n_pad = 0
            while left:
                m = min(per, left)
                pool.dma_start(rec_rows[:, (NT - left) * REC:(NT - left + m) * REC],
                               rec.rearrange("p a b c -> p (a b c)")[:, 0:m * REC]).then_inc(s_pad, 16)
                left -= m
                n_pad += 1
            g.memset(padm[:, :, :].rearrange("p a b -> p (a b)"), 0.0).then_inc(s_zp, 1)
            pool.wait_ge(s_zp, 2)
            g.iota(padm[:, :, 0:1].bitcast(I32), [[128, NTE]], base=NA, channel_multiplier=1).then_inc(s_zp, 1)
            pool.wait_ge(s_zp, 3)
            z_rows = z_d.rearrange("(t p) c -> p t c", p=128)
            pool.dma_start(z_rows[:, :, D:D + 2], padm[:, :, :]).then_inc(s_zw, 16)
            pool.dma_start(z_rows[:, :, 0:D], zero_words.unsqueeze(1).broadcast_to([128, NTE, D])).then_inc(s_zw, 16)
            g.memset(ident[:, :], 0.0).then_inc(s_cst, 1)
            g.memset(before[:, :], 0.0).then_inc(s_cst, 1)
            g.memset(ones[:, :], 1.0).then_inc(s_cst, 1)
            g.memset(epsc[:, :], EPS).then_inc(s_cst, 1)
            g.memset(mx[:, :], 0.0).then_inc(s_cst, 1)
            g.iota(iota[:, :], [[1, 128]], base=0, channel_multiplier=0, allow_small_or_imprecise_dtypes=True).then_inc(s_cst, 1)
            g.iota(iota_w[:, :], [[1, W]], base=0, channel_multiplier=0, allow_small_or_imprecise_dtypes=True).then_inc(s_cst, 1)
            g.iota(pair_no, [[1, PAIRS]], base=0, channel_multiplier=0, allow_small_or_imprecise_dtypes=True).then_inc(s_cst, 1)
            g.iota(riota[:, :], [[-1, NX]], base=NX, channel_multiplier=0, allow_small_or_imprecise_dtypes=True).then_inc(s_cst, 1)
            g.iota(tile_no[:, :], [[1, NTE + 3]], base=0, channel_multiplier=0, allow_small_or_imprecise_dtypes=True).then_inc(s_cst, 1)
            pool.wait_ge(s_cst, 10)
            g.affine_select(out=ident[:, :], in_=ident[:, :], compare_op=ALU.not_equal, fill=1.0,
                            base=0, pattern=[[-1, 128]], channel_multiplier=1).then_inc(s_cst, 1)
            g.affine_select(out=before[:, :], in_=before[:, :], compare_op=ALU.is_ge, fill=1.0,
                            base=0, pattern=[[-1, 128]], channel_multiplier=1).then_inc(s_cst, 1)
            pool.wait_ge(s_cst, 12)
            g.tensor_copy(identb[:, :], ident[:, :]).then_inc(s_cst, 1)
            g.tensor_copy(identh[:, :], ident[:, :]).then_inc(s_cst, 1)
            g.memset(ones3[:, :], 1.0).then_inc(s_cst, 1)
            for k in range(2):
                g.iota(place[:, k, :], [[256, W]], base=k, channel_multiplier=2).then_inc(s_cst, 1)
            pool.wait_ge(s_mx, 5)
            g.partition_all_reduce(mxa[:, :], mx[:, :], 128, bass.bass_isa.ReduceOp.max).then_inc(s_all, 1)
            pool.wait_ge(s_pad, 16 * n_pad)

            def scatter(k, par):
                pool.wait_ge(s_chunk, k + 1)
                gate(pool, s_gp)
                for c in range(CH):
                    g.indirect_dma_start(recs_d, bass.IndirectOffsetOnAxis(ap=idx_s[0:EP, par, c:c + 1], axis=0),
                                         rec[0:EP, par, c, :], None).then_inc(s_sc[par], 16)
            paired(pool, W, scatter)

            for par in range(2):
                pool.wait_ge(s_qst[par], 16 * ((W + 1 - par) // 2))
            def gather(i):
                for j in range(8):
                    if j % 4 == 0:
                        pool.wait_ge(e_rec[j // 4], 16 * (i + 1))
                    if static_ge(i, 1):
                        pool.wait_ge(e_s, 8 * i + j - 7)
                    gate(pool, s_gp)
                    g.indirect_dma_start(qg[:, j, :], None, q_d, bass.IndirectOffsetOnAxis(
                        ap=recg[:, j // 4, j % 4, KE:KE + 2].bitcast(I32), axis=0)).then_inc(e_q[j], 16)
            gather(0)
            with pool.Fori(1, NT // 8) as i:
                gather(i)

            pool.wait_ge(s_zw, 32)
            pool.wait_ge(r_slot, 1)
            for k in range(2):
                for w in range(W):
                    pool.wait_ge(r_meta[k], 1 if k == 0 else w // 5 + 1)
                    g.indirect_dma_start(z_d, bass.IndirectOffsetOnAxis(ap=slot_i[:, k * W + w:k * W + w + 1], axis=0),
                                         z3[:, w, :], None).then_inc(r_sc[k], 16)

            def scatter_out(T, i, j):
                pool.wait_ge(x_y, T + 1)
                gate(pool, s_gp)
                g.indirect_dma_start(y_d, bass.IndirectOffsetOnAxis(ap=zt[:, j, PLACE:PLACE + 1].bitcast(I32), axis=0),
                                     yo[:, j, :], None).then_inc(x_sc[j], 16)
            quads(pool, scatter_out)

        @block.scalar
        def _(act):
            a = nc.scalar
            for n in range(2 * NX):
                act.wait_ge(n_w[n % 2], 16 * (n // 2 + 1))
                a.activation(wst[:, n % 2, :], wst[:, n % 2, :], ACT.Square, accum_out=fro[:, n:n + 1]).then_inc(n_f, 1)
            act.wait_ge(s_wp, 64)
            act.wait_ge(n_f, 2 * NX)
            a.activation(wst[:, 0, 0:NX * KH], b1c[:, :, :].rearrange("p a b -> p (a b)"), ACT.Square,
                         accum_out=fro[:, 2 * NX:2 * NX + 1]).then_inc(n_f, 1)
            act.wait_ge(s_sqr, 1)
            act.wait_ge(s_cst, 4)
            a.activation(stat[:, 2, :], stat[:, 1, :], ACT.Sqrt, bias=epsc[:, :], scale=1.0 / D).then_inc(s_sd, 1)
            act.wait_ge(n_q, 1)
            a.activation(frs[:, :], sx[:, 8:11], ACT.Sqrt).then_inc(n_s, 1)

            def node_tile(k, par):
                act.wait_ge(s_tp, k + 1)
                if static_ge(k, 1):
                    act.wait_ge(s_pq, 2 * k)
                a.activation(xTst.rearrange("p k n -> p (k n)"), ps[0][:, 0:D], ACT.Copy).then_inc(s_xT, 1)
                dst_t = xnT[:, :, k * 128:(k + 1) * 128] if isinstance(k, int) else xnT[:, :, ds(k * 128, 128)]
                a.activation(dst_t, ps[0][:, 0:D].rearrange("p (k n) -> p k n", k=KD), ACT.Copy).then_inc(s_xT, 1)
                act.wait_ge(s_pq, 2 * k + 1)
                pd = P12[:, k, 0, :] if isinstance(k, int) else P12[:, ds(k, 1), 0, :].rearrange("p a h -> p (a h)")
                a.activation(pd, ps[1][:, :], ACT.Copy).then_inc(s_pq1, 1)
                act.wait_ge(s_pq, 2 * k + 2)
                if static_ge(k, 2):
                    act.wait_ge(s_qst[par], 8 * k if par == 0 else 8 * k - 8)
                a.activation(qst[:, par, 0:H], ps[2][:, :], ACT.Copy).then_inc(s_pq1, 1)
            act.wait_ge(s_c6, 96)
            paired(act, W, node_tile)

            def te(g, i):
                act.wait_ge(e_tr, g + 1)
                if static_ge(i, 1):
                    act.wait_ge(e_s, 4 * g - 4)
            def evac(par):
                a.activation(trs[:, par, :], ps[7][:, :].bitcast(BF16), ACT.Copy).then_inc(e_te, 1)

            def edge_body(i, last=False):
                for j in range(8):
                    t = 8 * i + j
                    act.wait_ge(e_s, t + 1)
                    if static_ge(i, 1) or j >= 4:
                        act.wait_ge(e_agg, t - 3)
                    a.activation(h1[:, j % 4, :], ps[j % 4][:, :], ACT.Relu).then_inc(e_h1, 1)
                    if j == 2:
                        te(2 * i + 1, i)
                        evac(1)
                    if j == 6 and not last:
                        g = 2 * i + 2
                        act.wait_ge(e_tr, g + 1)
                        act.wait_ge(e_s, 4 * g - 4)
                        evac(0)
            te(0, 0)
            evac(0)
            edge_body(0)
            with act.Fori(1, NT // 8 - 1) as i:
                edge_body(i)
            edge_body(NT // 8 - 1, last=True)

            def update_chunk(c, par, n, nxt, prv):
                for m in range(KD):
                    act.wait_ge(u_ag, 2 * c + m + 1)
                    if static_ge(c, 1) and m == 0:
                        act.wait_ge(u_u, 4 * c)
                    a.activation(aggT[:, m, 0:n * 128], ps[1 + m][:, 0:n * 128], ACT.Copy).then_inc(u_ae, 1)
                if prv:
                    act.wait_ge(z_u, c)
                    a.activation(zr[:, 1, 0:prv], zr[:, 0, 0:prv], ACT.Sqrt).then_inc(z_sd, 1)
                for m in range(KH):
                    if m < nxt:
                        evacuate_sums(4 * c + 4 + m, m, 1 - par)
                    act.wait_ge(u_u, 4 * c + m + 1)
                    if m == 0 and static_ge(c, 1):
                        act.wait_ge(u_o, 4 * c)
                    a.activation(uT[:, m, 0:n * 128], ps[3 + m % 2][:, 0:n * 128], ACT.Relu,
                                 bias=ub1c[:, m:m + 1]).then_inc(u_ue, 1)
                for j in range(prv):
                    z_tile(4 * c - 4 + j, j)

            def evacuate_sums(t, j, par):
                act.wait_ge(u_tr, t + 1)
                gate(act, s_ga)
                cols = slice(j * 128, (j + 1) * 128)
                src_b = ps[0][:, :].rearrange("p (k n) -> p k n", k=KH)
                a.activation(HT[par][:, :, cols], src_b, ACT.Copy).then_inc(u_ht, 1)

            def z_tile(t, j):
                act.wait_ge(z_st, t + 1)
                zd = z16[:, t, 0:D] if isinstance(t, int) else z16[:, ds(t, 1), 0:D].rearrange("p a d -> p (a d)")
                a.activation(zd, zst[:, j % 2, :], ACT.Copy, scale=g_z).then_inc(z_1, 1)
                act.wait_ge(z_tr, t + 1)
                if static_ge(t, 1):
                    act.wait_ge(z_lg, t)
                a.activation(zTst.rearrange("p k n -> p (k n)"), ps[7][:, 0:D], ACT.Copy).then_inc(z_te, 1)
                act.wait_ge(z_lg, t + 1)
                ld = lg[:, t, :] if isinstance(t, int) else lg[:, ds(t, 1), :].rearrange("p a d -> p (a d)")
                a.activation(ld, ps[7][:, D:D + NX], ACT.Copy).then_inc(z_le, 1)
            for j in range(4):
                evacuate_sums(j, j, 0)
            update_chunk(0, 0, 4, 4, 0)
            pair_chunks(act, update_chunk)
            update_chunk(NCH - 1, (NCH - 1) % 2, 4, 1, 4)
            update_chunk(NCH, NCH % 2, 1, 0, 4)
            act.wait_ge(z_u, NCH + 1)
            a.activation(zr[:, 1, 0:1], zr[:, 0, 0:1], ACT.Sqrt).then_inc(z_sd, 1)
            z_tile(4 * NCH, 0)

            act.wait_ge(z_gap, 1)
            a.activation(rs[:, 3, :], rs[:, 2, :], ACT.Exp).then_inc(z_ex, 1)
            for n in range(2 * NX):
                act.wait_ge(w_in[n % 6], 16 * (n // 6 + 1))
                if n == NX:
                    act.wait_ge(r_slot, 1)
                a.activation(w_half(n, 0), wstage[:, n % 6, :], ACT.Copy, scale=g_1 if n < NX else g_2).then_inc(w_a, 1)

            def gelu(T, i, j):
                if isinstance(T, int):
                    e = a.value_load(etab_i[0:1, T:T + 1], min_val=0, max_val=NX - 1)
                else:
                    e = a.value_load(etab_i[0:1, ds(T, 1)], min_val=0, max_val=NX - 1)
                act.wait_ge(x_h, T + 1)
                if static_ge(T, 2):
                    act.wait_ge(x_h2, T - 1)
                for m in range(KH):
                    ins = a.activation(h32[:, j % 2, m * 128:(m + 1) * 128], ps[2 + j % 2][:, m * 128:(m + 1) * 128],
                                       ACT.Gelu, bias=b1c[:, ds(e, 1), m:m + 1].rearrange("p a b -> p (a b)"), scale=un1)
                ins.then_inc(x_g, 1)
            quads(act, gelu)

        @block.vector
        def _(dve):
            v = nc.vector
            made = [0]

            def own(instruction, also=None):
                instruction.then_inc(dv, 1)
                made[0] += 1
                dve.wait_ge(dv, made[0])

            def small(n):
                return sq_rows[:, n * W:(n + 1) * W]

            tmp_i = r_p[0:EP, 10000:10000 + EC].bitcast(I32)
            tmp_f = r_p[0:EP, 10400:10400 + EC]
            tmp2_i = r_p[0:EP, 10800:10800 + EC].bitcast(I32)
            tmp2_f = r_p[0:EP, 11200:11200 + EC]
            dve.wait_ge(s_src, 16)
            dve.wait_ge(s_cst, 17)
            own(v.tensor_scalar(tmp_i, src_i, 7, None, ALU.logical_shift_right))
            own(v.tensor_scalar(tmp2_i, src_i, 127, None, ALU.bitwise_and))
            own(v.tensor_copy(hi_b[0:EP, :], tmp_i))
            own(v.tensor_copy(lo_b[0:EP, :], tmp2_i))
            m3 = mask[0:EP]
            s3 = scan[0:EP]
            own(v.tensor_tensor(m3, hi_b[0:EP, :].unsqueeze(1).broadcast_to([EP, W, EC]),
                                iota_w[0:EP, :].unsqueeze(2).broadcast_to([EP, W, EC]), ALU.is_equal))
            mflat = m3.rearrange("p b c -> p (b c)")
            own(v.tensor_tensor_scan(s3.rearrange("p b c -> p (b c)"), mflat, mflat, 0.0, ALU.add, ALU.max))
            ends, cnt = small(0)[0:EP, :], small(1)[0:EP, :]
            own(v.tensor_copy(ends, s3[:, :, EC - 1]))
            own(v.tensor_copy(cnt[:, 0:1], ends[:, 0:1]))
            v.tensor_tensor(cnt[:, 1:W], ends[:, 1:W], ends[:, 0:W - 1], ALU.subtract).then_inc(s_cnt, 1)
            dve.wait_ge(s_cnt, 1)
            dve.wait_ge(s_tot, 1)
            tot, pre = ps[6][:, 0:W], ps[6][0:EP, 32:32 + W]
            own(v.tensor_scalar(sci_w := r_p[:, 11650:11650 + W].bitcast(I32), tot, 255.0, None, ALU.add))
            own(v.tensor_scalar(sci_w, sci_w, 8, None, ALU.logical_shift_right))
            own(v.tensor_copy(small(2), sci_w))
            own(v.tensor_tensor_scan(small(3), small(2), small(2), 0.0, ALU.add, ALU.max))
            own(v.tensor_tensor(small(4), small(3), small(2), ALU.subtract))
            off = small(5)[0:EP, :]
            own(v.scalar_tensor_tensor(off, small(4)[0:EP, :], 256.0, pre, ALU.mult, ALU.add))
            own(v.tensor_tensor(off, off, ends, ALU.subtract))
            own(v.scalar_tensor_tensor(off, off, -1.0, cnt, ALU.add, ALU.add))
            own(v.tensor_tensor(s3, s3, off.unsqueeze(2).broadcast_to([EP, W, EC]), ALU.add))
            own(v.tensor_tensor(s3, s3, m3, ALU.mult))
            own(v.tensor_reduce(tmp_f, s3.rearrange("p b c -> p c b"), AX.X, ALU.add))
            own(v.tensor_copy(tmp_i, tmp_f))
            own(v.tensor_scalar(tmp2_i, tmp_i, 127, None, ALU.bitwise_and))
            own(v.tensor_scalar(tmp_i, tmp_i, 7, None, ALU.logical_shift_right))
            own(v.tensor_copy(tmp_f, tmp2_i))
            own(v.tensor_copy(tmp2_f, tmp_i))
            own(v.scalar_tensor_tensor(idx[0:EP, :], tmp_f, float(NT), tmp2_f, ALU.mult, ALU.add))

            dve.wait_ge(s_ea, 32)
            dve.wait_ge(s_w, 32)
            dve.wait_ge(s_cr, 96)
            mxc = lambda n, p=128: mx[0:p, n:n + 1]
            v.tensor_reduce(mxc(0), wAB[:, 0:2, :].rearrange("p a b -> p (a b)"), AX.X, ALU.max, apply_absolute_value=True).then_inc(s_mx, 1)
            v.tensor_reduce(mxc(1), wAB[:, 2:4, :].rearrange("p a b -> p (a b)"), AX.X, ALU.max, apply_absolute_value=True).then_inc(s_mx, 1)
            v.tensor_reduce(mxc(2, KE), cdup[:, :], AX.X, ALU.max, apply_absolute_value=True).then_inc(s_mx, 1)
            v.tensor_reduce(mxc(3, 1), b1row[0:1, :], AX.X, ALU.max, apply_absolute_value=True).then_inc(s_mx, 1)
            v.tensor_reduce(mxc(4, EP), ea[0:EP].rearrange("p a b -> p (a b)"), AX.X, ALU.max, apply_absolute_value=True).then_inc(s_mx, 1)
            dve.wait_ge(s_all, 1)
            own(v.tensor_tensor(sc[:, 3:4], mxa[:, 0:1], mxa[:, 1:2], ALU.add))
            own(v.scalar_tensor_tensor(sc[:, 4:5], mxa[:, 2:3], float(EA), mxa[:, 4:5], ALU.mult, ALU.mult))
            own(v.scalar_tensor_tensor(sc[:, 5:6], sc[:, 3:4], float(D), sc[:, 4:5], ALU.mult, ALU.add))
            own(v.tensor_tensor(sc[:, 0:1], sc[:, 5:6], mxa[:, 3:4], ALU.add))
            own(v.tensor_scalar(sci[:, 0:1], sc[:, 0:1].bitcast(I32), 23, None, ALU.logical_shift_right))
            own(v.tensor_scalar(sci[:, 1:2], sci[:, 0:1], 40.0, 240.0, ALU.max, ALU.min))
            own(v.tensor_scalar(sci[:, 2:3], sci[:, 1:2], -1.0, 268.0, ALU.mult, ALU.add))
            own(v.tensor_scalar(sci[:, 3:4], sci[:, 1:2], -14.0, None, ALU.add))
            own(v.tensor_scalar(f_sc.bitcast(I32), sci[:, 2:3], 23, None, ALU.logical_shift_left))
            own(v.tensor_scalar(finv.bitcast(I32), sci[:, 3:4], 23, None, ALU.logical_shift_left))
            own(v.tensor_scalar(wAB.rearrange("p a b -> p (a b)"), wAB.rearrange("p a b -> p (a b)"), f_sc, None, ALU.mult))
            v.tensor_scalar(b1row[0:1, :], b1row[0:1, :], f_sc[0:1, :], None, ALU.mult).then_inc(s_f, 1)
            own(v.tensor_scalar(cdup[:, :], cdup[:, :], f_sc[0:KE, :], None, ALU.mult))
            cpart = [qst[0:KE, 0, 0:H].bitcast(BF16), qst[0:KE, 0, H:2 * H].bitcast(BF16), qst[0:KE, 1, 0:H].bitcast(BF16)]
            own(v.tensor_copy(cpart[0], cdup[:, :]))
            own(v.tensor_tensor(cdup[:, :], cdup[:, :], cpart[0], ALU.subtract))
            own(v.tensor_copy(cpart[1], cdup[:, :]))
            v.tensor_tensor(cpart[2], cdup[:, :], cpart[1], ALU.subtract).then_inc(s_sp, 1)

            def norm_begin(src3, cent, sq, ready):
                own(v.tensor_reduce(stat[:, 0, :], src3, AX.X, ALU.add))
                own(v.tensor_scalar(stat[:, 0, :], stat[:, 0, :], 1.0 / D, None, ALU.mult))
                own(v.tensor_tensor(cent, src3, stat[:, 0, :].unsqueeze(2).broadcast_to([128, W, D]), ALU.subtract))
                own(v.tensor_tensor(sq, cent, cent, ALU.mult))
                v.tensor_reduce(stat[:, 1, :], sq, AX.X, ALU.add).then_inc(ready, 1)

            def norm_end():
                own(v.reciprocal(stat[:, 3, :], stat[:, 2, :]))
                own(v.tensor_scalar(stat[:, 4, :], stat[:, 1, :], 1.0 / D, EPS, ALU.mult, ALU.add))
                own(v.tensor_tensor(stat[:, 5, :], stat[:, 3, :], stat[:, 3, :], ALU.mult))
                own(v.tensor_tensor(stat[:, 4, :], stat[:, 4, :], stat[:, 5, :], ALU.mult))
                own(v.tensor_scalar(stat[:, 4, :], stat[:, 4, :], -0.5, 1.5, ALU.mult, ALU.add))
                own(v.tensor_tensor(stat[:, 3, :], stat[:, 3, :], stat[:, 4, :], ALU.mult))

            dve.wait_ge(s_x, 32)
            sq1 = r_p[:, 0:W * D].rearrange("p (w d) -> p w d", w=W)
            dve.wait_ge(s_ub, 16)
            norm_begin(xs, xc, sq1, s_sqr)
            dve.wait_ge(s_sqr, 1)
            dve.wait_ge(s_sd, 1)
            norm_end()
            own(v.tensor_tensor(xs, xs, ub2b.unsqueeze(1).broadcast_to([128, W, D]), ALU.add))

            own(v.memset(wtab, 0.0))
            for b in range(W - 1):
                own(v.scalar_tensor_tensor(wtab, pair_no, small(3)[:, b:b + 1], wtab, ALU.is_ge, ALU.add))
            v.tensor_copy(wtab_i[:, :], wtab).then_inc(s_wtab, 1)

            dve.wait_ge(n_f, 2 * NX + 1)
            own(v.tensor_reduce(sx[:, 12:13], fro[:, 0:NX], AX.X, ALU.add))
            own(v.tensor_reduce(sx[:, 13:14], fro[:, NX:2 * NX], AX.X, ALU.add))
            v.tensor_copy(sx[:, 14:15], fro[:, 2 * NX:2 * NX + 1]).then_inc(n_r, 1)
            dve.wait_ge(n_t, 1)
            v.tensor_copy(sx[:, 8:11], ps[6][:, 64:67]).then_inc(n_q, 1)

            dbase = made[0]
            OWN = 4

            def step(k, par):
                n = [0]

                def own2(ins):
                    ins.then_inc(dv, 1)
                    n[0] += 1
                    dve.wait_ge(dv, OWN * k + (dbase + n[0]))
                rk = rec[0:EP, par]

                def cols(a, dims=1):
                    return a[0:EP, k * CH:(k + 1) * CH] if isinstance(k, int) else a[0:EP, ds(k * CH, CH)]
                if static_ge(k, 2):
                    dve.wait_ge(s_sc[par], 8 * CH * k if par == 0 else 8 * CH * k - 8 * CH)
                if isinstance(k, int) and k == 0:
                    dve.wait_ge(s_pad, 16 * (-(-NT // (2 * CH))))
                    dve.wait_ge(s_zw, 32)
                gate(dve, s_gd)
                eac = cols(ea)
                own2(v.tensor_copy(rk[:, :, 0:EA], eac))
                own2(v.tensor_tensor(r1[0:EP], eac, rk[:, :, 0:EA], ALU.subtract))
                own2(v.tensor_copy(rk[:, :, 3 * EA:4 * EA], r1[0:EP]))
                v.tensor_copy(rk[:, :, 4 * EA:5 * EA], r1[0:EP])
                v.tensor_copy(rk[:, :, EA:2 * EA], eac)
                v.tensor_copy(rk[:, :, 2 * EA:3 * EA], eac)
                v.tensor_tensor(rk[:, :, 5 * EA:6 * EA], r1[0:EP], rk[:, :, 3 * EA:4 * EA], ALU.subtract)
                v.tensor_copy(rk[:, :, KE:KE + 2].bitcast(I32), cols(dst_i).unsqueeze(2))
                v.tensor_copy(rk[:, :, KE + 2:KE + 3], cols(lo_b).unsqueeze(2))
                v.tensor_copy(idx_s[0:EP, par, :], cols(idx)).then_inc(s_chunk, 1)
                if static_ge(k, 1):
                    dve.wait_ge(s_hist, k)
                v.tensor_tensor(oh_lo[0:EP], cols(lo_b).unsqueeze(2).broadcast_to([EP, CH, 128]),
                                iota[0:EP, :].unsqueeze(1).broadcast_to([EP, CH, 128]), ALU.is_equal).then_inc(s_oh, 1)
                dve.wait_ge(s_oh, 2 * k + 1)
                v.tensor_tensor(oh_hi[0:EP], cols(hi_b).unsqueeze(2).broadcast_to([EP, CH, W]),
                                iota_w[0:EP, :].unsqueeze(1).broadcast_to([EP, CH, W]), ALU.is_equal).then_inc(s_oh, 1)
                if static_ge(k, 1):
                    dve.wait_ge(s_tp, k)
                xk = lambda a: a[:, k, :] if isinstance(k, int) else a[:, ds(k, 1), :].rearrange("p a d -> p (a d)")
                stk = stat[:, 3, k:k + 1] if isinstance(k, int) else stat[:, 3, ds(k, 1)]
                v.tensor_scalar(xstage, xk(xc), stk, None, ALU.mult).then_inc(s_xst, 1)
                dve.wait_ge(s_xst, k + 1)
                own2(v.tensor_tensor(xk(xs), xk(xs), xstage, ALU.add))
                assert n[0] == OWN
                pd1 = P12[:, k, 0, :] if isinstance(k, int) else P12[:, ds(k, 1), 0, :].rearrange("p a h -> p (a h)")
                pd2 = P12[:, k, 1, :] if isinstance(k, int) else P12[:, ds(k, 1), 1, :].rearrange("p a h -> p (a h)")
                dve.wait_ge(s_pq1, 2 * k + 1)
                v.tensor_tensor(pd2, ps[1][:, :], pd1, ALU.subtract).then_inc(s_pq2, 1)
                dve.wait_ge(s_pq1, 2 * k + 2)
                v.tensor_tensor(qst[:, par, H:2 * H], ps[2][:, :], qst[:, par, 0:H], ALU.subtract).then_inc(s_pq2, 1)
            paired(dve, W, step)
            made[0] = dbase + OWN * W
            dve.wait_ge(s_hist, W)
            v.tensor_copy(deg_s[:, :], ps[4][:, 0:W]).then_inc(s_deg, 1)
            v.memset(r_h[:, :], 0.0).then_inc(s_hz, 1)
            dve.wait_ge(s_hz, 1)

            def one_hot(j, t):
                v.tensor_scalar(oh[:, j, :], iota[:, :], recg[:, j // 4, j % 4, KE + 2:KE + 3], None,
                                ALU.is_equal).then_inc(e_oh, 1)

            def accumulate(p):
                wi = v.value_load(wtab_i[0:1, p:p + 1] if isinstance(p, int) else wtab_i[0:1, ds(p, 1)],
                                  min_val=0, max_val=W - 1)
                acc = Hacc[:, ds(wi, 1), :].rearrange("p a h -> p (a h)")
                return acc

            def edge_body(i, last=False):
                for j in range(8):
                    t = 8 * i + j
                    if j % 2 == 0 and (static_ge(i, 1) or j >= 4):
                        p = 4 * i + j // 2 - 2
                        dve.wait_ge(e_agg, 2 * p + 2)
                        if static_ge(p, 1):
                            dve.wait_ge(e_acc, p)
                        acc = accumulate(p)
                        v.tensor_tensor(acc, acc, ps[4 + (j // 2) % 2][:, :], ALU.add).then_inc(e_acc, 1)
                    dve.wait_ge(e_h1, t + 1)
                    v.scalar_tensor_tensor(h2[:, j % 4, :], ps[j % 4][:, :], 0.0, h1[:, j % 4, :],
                                           ALU.max, ALU.subtract).then_inc(e_h2, 1)
                    ja = j + 6
                    if not last or ja < 8:
                        if ja % 4 == 0:
                            dve.wait_ge(e_rec[(ja // 4) % 2], 16 * (i + 1 + ja // 8))
                        if static_ge(i, 1) or j >= 2:
                            dve.wait_ge(e_agg, t - 1)
                        one_hot(ja % 8, t + 6)
            dve.wait_ge(e_rec[0], 16)
            for j in range(4):
                one_hot(j, j)
            dve.wait_ge(e_rec[1], 16)
            for j in range(4, 6):
                one_hot(j, j)
            edge_body(0)
            with dve.Fori(1, NT // 8 - 1) as i:
                edge_body(i)
            edge_body(NT // 8 - 1, last=True)
            for p in (PAIRS - 2, PAIRS - 1):
                dve.wait_ge(e_agg, 2 * p + 2)
                dve.wait_ge(e_acc, p)
                acc = accumulate(p)
                v.tensor_tensor(acc, acc, ps[4 + p % 2][:, :], ALU.add).then_inc(e_acc, 1)
            dve.wait_ge(e_acc, PAIRS)

            def scale(out_f, bound, inverse=None):
                own(v.tensor_scalar(sxi[:, 0:1], bound.bitcast(I32), 23, None, ALU.logical_shift_right))
                own(v.tensor_scalar(sxi[:, 1:2], sxi[:, 0:1], 90.0, 190.0, ALU.max, ALU.min))
                own(v.tensor_scalar(sxi[:, 2:3], sxi[:, 1:2], -1.0, 268.0, ALU.mult, ALU.add))
                own(v.tensor_scalar(out_f.bitcast(I32), sxi[:, 2:3], 23, None, ALU.logical_shift_left))
            dve.wait_ge(n_s, 1)
            dve.wait_ge(n_gb, 32)
            own(v.tensor_reduce(sx[:, 8:9], gam, AX.X, ALU.max, apply_absolute_value=True))
            own(v.tensor_reduce(sx[:, 9:10], bet, AX.X, ALU.max, apply_absolute_value=True))
            own(v.scalar_tensor_tensor(sx[:, 10:11], sx[:, 8:9], float(D) ** 0.5, sx[:, 9:10], ALU.mult, ALU.add))
            scale(g_z, sx[:, 10:11])
            scale(g_1, frs[:, 0:1])
            scale(g_2, frs[:, 1:2])
            own(v.tensor_tensor(sx[:, 11:12], sx[:, 8:9], sx[:, 9:10], ALU.add))
            own(v.scalar_tensor_tensor(sx[:, 11:12], sx[:, 11:12], float(D) ** 0.5, frs[:, 0:1], ALU.mult, ALU.mult))
            own(v.tensor_tensor(sx[:, 11:12], sx[:, 11:12], frs[:, 2:3], ALU.add))
            scale(g_h, sx[:, 11:12])
            own(v.tensor_tensor(sx[:, 12:13], g_z, g_1, ALU.mult))
            own(v.tensor_tensor(g_o, g_h, g_2, ALU.mult))
            own(v.reciprocal(un1, sx[:, 12:13]))
            own(v.reciprocal(un2, g_o))

            def stage_sums(t, j):
                if static_ge(t, 1):
                    dve.wait_ge(u_tr, t)
                src_t = Hacc[:, t, :] if isinstance(t, int) else Hacc[:, ds(t, 1), :].rearrange("p a h -> p (a h)")
                v.tensor_scalar(hst, src_t, finv, None, ALU.mult).then_inc(u_st, 1)
                dt = deg_s[:, t:t + 1] if isinstance(t, int) else deg_s[:, ds(t, 1)]
                v.tensor_scalar(diag[:, j * 128:(j + 1) * 128], ident[:, :], dt, None, ALU.mult).then_inc(u_dg, 1)

            def x_t(t):
                return xs[:, t, :] if isinstance(t, int) else xs[:, ds(t, 1), :].rearrange("p a d -> p (a d)")

            def update_results(c, n, prv, own_c):
                if prv:
                    dve.wait_ge(z_sd, c)
                    r, q = zr[:, 2, 0:prv], zr[:, 3, 0:prv]
                    own_c(v.reciprocal(r, zr[:, 1, 0:prv]))
                    own_c(v.tensor_tensor(q, r, r, ALU.mult))
                    own_c(v.tensor_tensor(q, q, zr[:, 0, 0:prv], ALU.mult))
                    own_c(v.tensor_scalar(q, q, -0.5, 1.5, ALU.mult, ALU.add))
                    own_c(v.tensor_tensor(r, r, q, ALU.mult))
                for j in range(max(n, prv)):
                    tz, t = 4 * c - 4 + j, 4 * c + j
                    if j < prv:
                        if j >= 2:
                            dve.wait_ge(z_tr, tz - 1)
                            dve.wait_ge(z_2, tz - 1)
                        elif j == 0 and static_ge(tz, 1):
                            dve.wait_ge(z_2, tz)
                        zj = zst[:, j % 2, :]
                        own_c(v.tensor_scalar(zj, x_t(tz), mv[:, 0, j:j + 1], zr[:, 2, j:j + 1], ALU.subtract, ALU.mult))
                        own_c(v.tensor_tensor(zj, zj, gam, ALU.mult))
                        v.tensor_tensor(zj, zj, bet, ALU.add).then_inc(z_st, 1)
                        dve.wait_ge(z_st, tz + 1)
                    if j < n:
                        dve.wait_ge(u_o, t + 1)
                        v.tensor_tensor(x_t(t), x_t(t), ps[5 + j % 2][:, 0:D], ALU.add).then_inc(u_x, 1)
                        dve.wait_ge(u_x, t + 1)
                        gate(dve, s_gd)
                        own_c(v.bn_stats(bns[:, 0:6], x_t(t)))
                        gate(dve, s_gd)
                        own_c(v.bn_aggr(mv[:, 1, 0:2], bns[:, 0:6]))
                        own_c(v.tensor_copy(mv[:, 0, j:j + 1], mv[:, 1, 0:1]))
                        own_c(v.tensor_scalar(zr[:, 4, j:j + 1], mv[:, 1, 1:2], 1.0 + EPS, EPS * EPS, ALU.mult, ALU.add))
                    if j < prv:
                        dve.wait_ge(z_1, tz + 1)
                        a1 = z16[:, tz, 0:D] if isinstance(tz, int) else z16[:, ds(tz, 1), 0:D].rearrange("p a d -> p (a d)")
                        a2 = z16[:, tz, D:2 * D] if isinstance(tz, int) else z16[:, ds(tz, 1), D:2 * D].rearrange("p a d -> p (a d)")
                        v.scalar_tensor_tensor(a2, zst[:, j % 2, :], g_z, a1, ALU.mult, ALU.subtract).then_inc(z_2, 1)
                if n:
                    v.tensor_copy(zr[:, 0, 0:n], zr[:, 4, 0:n]).then_inc(z_u, 1)

            OWNC = 5 + 2 * 4 + 4 * 4

            def update_chunk(c, par, n, nxt, prv):
                cbase, cn = made[0], [0]

                def own_c(ins):
                    ins.then_inc(dv, 1)
                    cn[0] += 1
                    at = cbase + cn[0] if isinstance(c, int) else OWNC * c + (loop_base - OWNC + cn[0])
                    dve.wait_ge(dv, at)
                for j in range(nxt):
                    if j == 0:
                        dve.wait_ge(u_ag, 2 * c + 2)
                    stage_sums(4 * c + 4 + j, j)
                update_results(c, n, prv, own_c)
                if isinstance(c, int):
                    made[0] += cn[0]
                else:
                    assert cn[0] == OWNC
            for j in range(4):
                stage_sums(j, j)
            update_chunk(0, 0, 4, 4, 0)
            loop_base = made[0]
            pair_chunks(dve, update_chunk)
            made[0] = loop_base + OWNC * (NCH - 2)
            update_chunk(NCH - 1, (NCH - 1) % 2, 4, 1, 4)
            update_chunk(NCH, NCH % 2, 1, 0, 4)
            dve.wait_ge(z_u, NCH + 1)
            update_results(NCH + 1, 0, 1, own)
            dve.wait_ge(z_le, W)
            own(v.tensor_tensor(lg[:, :, :], lg[:, :, :], brb[:, :].unsqueeze(1).broadcast_to([128, W, NX]), ALU.add))

            bc = lambda a: a.unsqueeze(2).broadcast_to([128, W, NX])
            rio = riota[:, :].unsqueeze(1).broadcast_to([128, W, NX])

            def pick(logits, value, hot, scratch, first):
                own(v.tensor_reduce(value, logits, AX.X, ALU.max))
                own(v.tensor_tensor(scratch, logits, bc(value), ALU.is_equal))
                own(v.tensor_tensor(scratch, scratch, rio, ALU.mult))
                own(v.tensor_reduce(first, scratch, AX.X, ALU.max))
                own(v.tensor_tensor(hot, rio, bc(first), ALU.is_equal))
            pick(lg[:, :, :], rs[:, 0, :], rt[:, 0], rt[:, 2], rs[:, 7, :])
            own(v.tensor_scalar(rt[:, 2], rt[:, 0], -1.0, 1.0, ALU.mult, ALU.add))
            own(v.tensor_tensor(rt[:, 2], rt[:, 2], lg[:, :, :], ALU.mult))
            own(v.scalar_tensor_tensor(rt[:, 3].rearrange("p a b -> p (a b)"), rt[:, 0].rearrange("p a b -> p (a b)"), -3.0e38,
                                       rt[:, 2].rearrange("p a b -> p (a b)"), ALU.mult, ALU.add))
            pick(rt[:, 3], rs[:, 1, :], rt[:, 1], rt[:, 2], rs[:, 7, :])
            v.tensor_tensor(rs[:, 2, :], rs[:, 1, :], rs[:, 0, :], ALU.subtract).then_inc(z_gap, 1)

            for k in range(2):
                own(v.tensor_copy(m2[:, :, k * W:(k + 1) * W], rt[:, k].rearrange("p w e -> p e w")))
            m2f, s2f = (q.rearrange("p e a -> p (e a)") for q in (m2, s2))
            own(v.tensor_tensor_scan(s2f, m2f, m2f, 0.0, ALU.add, ALU.max))
            own(v.tensor_copy(pr[:, 0, :], s2[:, :, 2 * W - 1]))
            own(v.tensor_copy(pr[:, 1, 0:1], pr[:, 0, 0:1]))
            v.tensor_tensor(pr[:, 1, 1:NX], pr[:, 0, 1:NX], pr[:, 0, 0:NX - 1], ALU.subtract).then_inc(r_cnt, 1)
            dve.wait_ge(z_ex, 1)
            own(v.tensor_scalar(rs[:, 4, :], rs[:, 3, :], 1.0, None, ALU.add))
            own(v.reciprocal(rs[:, 5, :], rs[:, 4, :]))
            own(v.tensor_tensor(rs[:, 6, :], rs[:, 5, :], rs[:, 3, :], ALU.mult))
            dve.wait_ge(r_tot, 1)
            own(v.tensor_scalar(sxi[:, 0:NX], ps[6][:, 0:NX], 127.0, None, ALU.add))
            own(v.tensor_scalar(sxi[:, 0:NX], sxi[:, 0:NX], 7, None, ALU.logical_shift_right))
            own(v.tensor_copy(pr[:, 2, :], sxi[:, 0:NX]))
            own(v.tensor_tensor_scan(pr[:, 3, :], pr[:, 2, :], pr[:, 2, :], 0.0, ALU.add, ALU.max))
            own(v.tensor_tensor(pr[:, 4, :], pr[:, 3, :], pr[:, 2, :], ALU.subtract))
            own(v.scalar_tensor_tensor(pr[:, 5, :], pr[:, 4, :], 128.0, ps[6][:, 32:32 + NX], ALU.mult, ALU.add))
            own(v.tensor_tensor(pr[:, 5, :], pr[:, 5, :], pr[:, 0, :], ALU.subtract))
            own(v.scalar_tensor_tensor(pr[:, 5, :], pr[:, 5, :], -1.0, pr[:, 1, :], ALU.add, ALU.add))
            own(v.tensor_tensor(s2, s2, pr[:, 5, :].unsqueeze(2).broadcast_to([128, NX, 2 * W]), ALU.add))
            own(v.tensor_tensor(s2, s2, m2, ALU.mult))
            own(v.tensor_reduce(slot_f, s2.rearrange("p e a -> p a e"), AX.X, ALU.add))
            v.tensor_copy(slot_i[:, :], slot_f).then_inc(r_slot, 1)
            dve.wait_ge(z_2, W)

            def meta(k, w0, w1):
                v.tensor_copy(z3[:, w0:w1, PLACE:PLACE + 1].bitcast(I32), place[:, k, w0:w1].unsqueeze(2))
                v.tensor_copy(z3[:, w0:w1, WEIGHT:WEIGHT + 1], rs[:, 5 + k, w0:w1].unsqueeze(2)).then_inc(r_meta[k], 1)
            meta(0, 0, W)
            own(v.memset(etab[:, :], 0.0))
            for e in range(NX - 1):
                own(v.scalar_tensor_tensor(etab[:, :], tile_no[:, :], pr[:, 3, e:e + 1], etab[:, :], ALU.is_ge, ALU.add))
            v.tensor_copy(etab_i[:, :], etab[:, :]).then_inc(r_et, 1)
            dve.wait_ge(r_et, 1)
            for n in range(5):
                dve.wait_ge(r_sc[0], 16 * W)
                meta(1, 5 * n, 5 * n + 5)
            for n in range(2 * NX):
                dve.wait_ge(w_a, n + 1)
                v.scalar_tensor_tensor(w_half(n, 1), wstage[:, n % 6, :], g_1 if n < NX else g_2, w_half(n, 0),
                                       ALU.mult, ALU.subtract).then_inc(w_b, 1)
            dve.wait_ge(b_in, 16)
            own(v.tensor_scalar(b2s[0:NX, :], b2s[0:NX, :], g_o[0:NX, :], None, ALU.mult))
            own(v.tensor_copy(b2p[0][0:NX, :], b2s[0:NX, :]))
            own(v.tensor_tensor(b2s[0:NX, :], b2s[0:NX, :], b2p[0][0:NX, :], ALU.subtract))
            own(v.tensor_copy(b2p[1][0:NX, :], b2s[0:NX, :]))
            v.tensor_tensor(b2p[2][0:NX, :], b2s[0:NX, :], b2p[1][0:NX, :], ALU.subtract).then_inc(b_p, 1)

            def rows_T(T, j):
                dve.wait_ge(x_tr, T + 1)
                if static_ge(T, 2):
                    dve.wait_ge(x_h, T - 1)
                v.tensor_copy(zT[:, j % 2].rearrange("p a b -> p (a b)"),
                              ps[j % 2][:, 0:D].bitcast(F16)).then_inc(x_te, 1)

            def split_and_weigh(T, i, j):
                if not (isinstance(T, int) and T + 2 >= NTE):
                    rows_T(T + 2, j)
                dve.wait_ge(x_g, T + 1)
                if static_ge(T, 2):
                    dve.wait_ge(x_o, T - 1)
                one, two = (hp[:, j % 2, s * KH:(s + 1) * KH].rearrange("p a b -> p (a b)") for s in range(2))
                v.tensor_scalar(one, h32[:, j % 2, :], g_h, None, ALU.mult).then_inc(x_h1, 1)
                dve.wait_ge(x_h1, T + 1)
                v.scalar_tensor_tensor(two, h32[:, j % 2, :], g_h, one, ALU.mult, ALU.subtract).then_inc(x_h2, 1)
                if static_ge(T, 1):
                    weigh(T - 1, i, (j - 1) % 4)

            def weigh(T, i, j):
                dve.wait_ge(x_o, T + 1)
                if static_ge(T, 4):
                    dve.wait_ge(x_sc[j], 16 * i if j != 3 else 16 * i - 16)
                v.tensor_scalar(yo[:, j, :], ps[4 + j % 2][:, 0:D], zt[:, j, WEIGHT:WEIGHT + 1], un2,
                                ALU.mult, ALU.mult).then_inc(x_y, 1)
            rows_T(0, 0)
            rows_T(1, 1)
            quads(dve, split_and_weigh)
            weigh(NTE - 1, (NTE - 1) // 4, (NTE - 1) % 4)

            for n in range(5):
                dve.wait_ge(y_ld[n], 16)
                part = xs[:, 5 * n:5 * n + 5, :]
                own(v.tensor_tensor(part, part, y_in[:, 5 * n:5 * n + 5, 0, :], ALU.add))
                v.tensor_tensor(part, part, y_in[:, 5 * n:5 * n + 5, 1, :], ALU.add).then_inc(y_ad, 1)

        @block.tensor
        def _(pe):
            mm = nc.tensor.matmul
            pe.wait_ge(s_cst, 17)
            pe.wait_ge(s_cnt, 1)
            cnt = sq_rows[0:EP, W:2 * W]
            mm(ps[6][:, 0:W], ones[0:EP, :], cnt, start=True, stop=True)
            mm(ps[6][0:EP, 32:32 + W], before[0:EP, 0:EP], cnt, start=True, stop=True).then_inc(s_tot, 1)

            pe.wait_ge(s_f, 1)
            pe.wait_ge(n_r, 1)
            mm(ps[6][:, 64:67], ones[:, :], sx[:, 12:15], start=True, stop=True).then_inc(n_t, 1)

            def node_tile(k, par):
                first, last = isinstance(k, int) and k == 0, isinstance(k, int) and k == W - 1
                pe.wait_ge(s_xst, k + 1)
                if static_ge(k, 1):
                    pe.wait_ge(s_xT, 2 * k)
                for m in range(KD):
                    ins = nc.tensor.transpose(ps[0][:, m * 128:(m + 1) * 128], xstage[:, m * 128:(m + 1) * 128], ident[:, :])
                ins.then_inc(s_tp, 1)
                pe.wait_ge(s_xT, 2 * k + 1)
                for q in range(2):
                    if static_ge(k, 1):
                        pe.wait_ge(s_pq2, 2 * k - 1 + q)
                    for m in range(KD):
                        ins = mm(ps[1 + q][:, :], xTst[:, m, :], wAB[:, KD * q + m, :], start=(m == 0), stop=(q == 1 and m == KD - 1))
                    if q == 0:
                        ins = mm(ps[1][:, :], ones[0:1, :], b1row[0:1, :], start=False, stop=True)
                    ins.then_inc(s_pq, 1)
                pe.wait_ge(s_oh, 2 * k + 2)
                for c in range(CH):
                    ins = mm(ps[4][:, 0:W], oh_lo[0:EP, c, :], oh_hi[0:EP, c, :], start=(first and c == 0), stop=(last and c == CH - 1),
                             skip_group_check=True)
                ins.then_inc(s_hist, 1)
            paired(pe, W, node_tile)

            def transposes(par):
                tb = ps[7][:, :].bitcast(BF16)
                for j in range(4):
                    nc.tensor.transpose(tb[:, j * 128:(j + 1) * 128], recg[:, par, j, :], identb[:, :])
                for j in range(4):
                    ins = nc.tensor.transpose(tb[:, (4 + j) * 128:(5 + j) * 128], oh[:, 4 * par + j, :], identb[:, :])
                ins.then_inc(e_tr, 1)

            def group(g, par, first=False):
                pe.wait_ge(e_rec[par], 8 * g + 16 if par == 0 else 8 * g + 8)
                pe.wait_ge(e_oh, 4 * g + 4)
                if not first:
                    pe.wait_ge(e_te, g)
                transposes(par)

            def agg(i, j, first_pairs=False):
                t = 8 * i + j
                pe.wait_ge(e_h2, t + 1)
                if j % 2 == 0 and not first_pairs:
                    pe.wait_ge(e_acc, 4 * i + j // 2 - 1)
                bank = ps[4 + (j // 2) % 2]
                mm(bank[:, :], oh[:, j, :], h1[:, j % 4, :], start=(j % 2 == 0), stop=False)
                mm(bank[:, :], oh[:, j, :], h2[:, j % 4, :], start=False, stop=(j % 2 == 1)).then_inc(e_agg, 1)

            def edge_body(i, last=False):
                for j in range(8):
                    t = 8 * i + j
                    if j % 4 == 0:
                        pe.wait_ge(e_te, 2 * i + 1 + j // 4)
                    if static_ge(i, 1) or j >= 4:
                        pe.wait_ge(e_h2, t - 3)
                    if j % 2 == 0:
                        p = 4 * i + j // 2
                        wi = nc.tensor.value_load(wtab_i[0:1, p:p + 1] if isinstance(p, int) else wtab_i[0:1, ds(p, 1)],
                                                  min_val=0, max_val=W - 1)
                    bank = ps[j % 4][:, :]
                    ohT = trs[:, j // 4, (4 + j % 4) * 128:(5 + j % 4) * 128]
                    mm(bank, trs[0:KE, j // 4, (j % 4) * 128:(j % 4 + 1) * 128], C6[:, :], start=True, stop=False)
                    mm(bank, ohT, P12[:, ds(wi, 1), 0, :].rearrange("p a h -> p (a h)"), start=False, stop=False)
                    mm(bank, ohT, P12[:, ds(wi, 1), 1, :].rearrange("p a h -> p (a h)"), start=False, stop=False)
                    pe.wait_ge(e_q[j], 16 * (i + 1))
                    mm(bank, identb[:, :], qg[:, j, 0:H], start=False, stop=False)
                    mm(bank, identb[:, :], qg[:, j, H:2 * H], start=False, stop=True).then_inc(e_s, 1)
                    if j >= 2:
                        agg(i, j - 2, first_pairs=not static_ge(i, 1) and j - 2 < 4)
                    elif static_ge(i, 1):
                        agg(i - 1, j + 6, first_pairs=False)
                    if j == 2:
                        group(2 * i + 1, 1)
                    if j == 6 and not last:
                        group(2 * i + 2, 0)
            pe.wait_ge(s_wtab, 1)
            pe.wait_ge(s_c6, 96)
            pe.wait_ge(s_pq2, 2 * W)
            group(0, 0, first=True)
            edge_body(0)
            with pe.Fori(1, NT // 8 - 1) as i:
                edge_body(i)
            edge_body(NT // 8 - 1, last=True)
            agg(NT // 8 - 1, 6)
            agg(NT // 8 - 1, 7)

            pe.wait_ge(u_w, 48)
            pe.wait_ge(u_mb, 16)

            def transpose_sums(t):
                pe.wait_ge(u_st, t + 1)
                if static_ge(t, 1):
                    pe.wait_ge(u_ht, t)
                for m in range(KH):
                    ins = nc.tensor.transpose(ps[0][:, m * 128:(m + 1) * 128], hst[:, m * 128:(m + 1) * 128], ident[:, :])
                ins.then_inc(u_tr, 1)

            def z_transpose(t, j):
                pe.wait_ge(z_st, t + 1)
                if static_ge(t, 1):
                    pe.wait_ge(z_le, t)
                for m in range(KD):
                    ins = nc.tensor.transpose(ps[7][:, m * 128:(m + 1) * 128], zst[:, j % 2, m * 128:(m + 1) * 128], ident[:, :])
                ins.then_inc(z_tr, 1)

            def z_logits(t):
                pe.wait_ge(z_te, t + 1)
                for m in range(KD):
                    ins = mm(ps[7][:, D:D + NX], zTst[:, m, :], Wrs[:, m, :], start=(m == 0), stop=(m == KD - 1))
                ins.then_inc(z_lg, 1)

            def update_chunk(c, par, n, nxt, prv):
                cols = n * 128
                c0 = 512 * c
                nodes = lambda a: a[:, c0:c0 + cols] if isinstance(c, int) else a[:, ds(c0, cols)]
                pe.wait_ge(u_ht, 4 * c + n)
                pe.wait_ge(u_dg, 4 * c + n)
                for m in range(KD):
                    if static_ge(c, 1):
                        pe.wait_ge(u_ae, 2 * c - 1 + m)
                    for k in range(KH):
                        mm(ps[1 + m][:, 0:cols], mW2s[:, k, m * 128:(m + 1) * 128], HT[par][:, k, 0:cols], start=(k == 0), stop=False)
                    mm(ps[1 + m][:, 0:cols], mb2b[:, m * 128:(m + 1) * 128], diag[:, 0:cols], start=False, stop=True).then_inc(u_ag, 1)
                for m in range(KH):
                    if m < nxt:
                        transpose_sums(4 * c + 4 + m)
                    if static_ge(c, 1) or m >= 2:
                        pe.wait_ge(u_ue, 4 * c + m - 1)
                    for k in range(2 * KD):
                        if k == KD and m == 0:
                            pe.wait_ge(u_ae, 2 * c + 2)
                        rhs = nodes(xnT[:, k, :]) if k < KD else aggT[:, k - KD, 0:cols]
                        ins = mm(ps[3 + m % 2][:, 0:cols], uW1s[:, k, m * 128:(m + 1) * 128], rhs, start=(k == 0), stop=(k == 2 * KD - 1))
                    ins.then_inc(u_u, 1)
                for j in range(4):
                    if j < prv:
                        z_transpose(4 * c - 4 + j, j)
                    if j < n:
                        t = 4 * c + j
                        if j == 0:
                            pe.wait_ge(u_ue, 4 * c + 4)
                        if static_ge(c, 1) or j >= 2:
                            pe.wait_ge(u_x, t - 1)
                        for k in range(KH):
                            ins = mm(ps[5 + j % 2][:, 0:D], uT[:, k, j * 128:(j + 1) * 128], uW2s[:, k, :], start=(k == 0), stop=(k == KH - 1))
                        ins.then_inc(u_o, 1)
                    if j < prv:
                        z_logits(4 * c - 4 + j)
            for j in range(4):
                transpose_sums(j)
            update_chunk(0, 0, 4, 4, 0)
            pair_chunks(pe, update_chunk)
            update_chunk(NCH - 1, (NCH - 1) % 2, 4, 1, 4)
            update_chunk(NCH, NCH % 2, 1, 0, 4)
            z_transpose(W - 1, 0)
            z_logits(W - 1)

            pe.wait_ge(r_cnt, 1)
            pe.wait_ge(u_x, W)
            mm(ps[6][:, 0:NX], ones[:, :], pr[:, 1, :], start=True, stop=True)
            mm(ps[6][:, 32:32 + NX], before[:, :], pr[:, 1, :], start=True, stop=True).then_inc(r_tot, 1)

            pe.wait_ge(r_et, 1)
            pe.wait_ge(w_b, 2 * NX)
            pe.wait_ge(b_r, 48)

            def rows_T(T, i, j):
                pe.wait_ge(x_in[j], 16 * i + 16)
                if static_ge(T, 2):
                    pe.wait_ge(x_te, T - 1)
                bank = ps[j % 2][:, 0:D].bitcast(F16)
                rows = zt[:, j, 0:D].bitcast(F16)
                for q in range(2 * KD):
                    ins = nc.tensor.transpose(bank[:, q * 128:(q + 1) * 128], rows[:, q * 128:(q + 1) * 128], identh[:, :])
                ins.then_inc(x_tr, 1)

            def expert_of(T):
                return nc.tensor.value_load(etab_i[0:1, T:T + 1] if isinstance(T, int) else etab_i[0:1, ds(T, 1)],
                                            min_val=0, max_val=NX - 1)

            def first_product(T, j):
                e = expert_of(T)
                pe.wait_ge(x_te, T + 1)
                if static_ge(T, 2):
                    pe.wait_ge(x_g, T - 1)
                for m in range(KH):
                    n = 0
                    for k in range(KD):
                        for sw, sz in ((0, 0), (0, 1), (1, 0)):
                            ins = mm(ps[2 + j % 2][:, m * 128:(m + 1) * 128],
                                     W1p[:, ds(e, 1), sw, k, m * 128:(m + 1) * 128].rearrange("p a b -> p (a b)"),
                                     zT[:, j % 2, sz * KD + k, :], start=(n == 0), stop=(n == 3 * KD - 1))
                            n += 1
                ins.then_inc(x_h, 1)

            def second_product(T, j):
                e = expert_of(T)
                pe.wait_ge(x_h2, T + 1)
                if static_ge(T, 2):
                    pe.wait_ge(x_y, T - 1)
                bank = ps[4 + j % 2][:, 0:D]
                mm(bank, ones3[:, :], b2r[0:3, ds(e, 1), :].rearrange("p a d -> p (a d)"), start=True, stop=False)
                n = 0
                for k in range(KH):
                    for sh, sw in ((0, 0), (1, 0), (0, 1)):
                        n += 1
                        ins = mm(bank, hp[:, j % 2, sh * KH + k, :],
                                 W2p[:, ds(e, 1), sw, k, :].rearrange("p a d -> p (a d)"), start=False, stop=(n == 3 * KH))
                ins.then_inc(x_o, 1)

            def expert_tile(T, i, j):
                if not (isinstance(T, int) and T + 2 >= NTE):
                    rows_T(T + 2, i + (j + 2) // 4, (j + 2) % 4)
                if not (isinstance(T, int) and T + 1 >= NTE):
                    first_product(T + 1, j + 1)
                second_product(T, j)
            rows_T(0, 0, 0)
            rows_T(1, 0, 1)
            first_product(0, 0)
            quads(pe, expert_tile)


_INS = ['x', 'src', 'dst', 'edge_attr_16', 'L0_gnn_mW1', 'L0_gnn_mb1', 'L0_gnn_mW2', 'L0_gnn_mb2', 'L0_gnn_uW1',
        'L0_gnn_ub1', 'L0_gnn_uW2', 'L0_gnn_ub2', 'L0_ffn_gamma', 'L0_ffn_beta', 'L0_ffn_Wr', 'L0_ffn_br',
        'L0_ffn_W1', 'L0_ffn_b1', 'L0_ffn_W2', 'L0_ffn_b2']
_OUTS = [((3125, 256), 'float32')]


def kernel(**inputs):
    import numpy as _np
    import concourse.bacc as _bacc
    from concourse import mybir as _mybir
    from concourse.bass_utils import run_bass_kernel_spmd as _run

    nc = _bacc.Bacc("TRN2", target_bir_lowering=False, num_devices=1)
    arrays, args = {}, []
    for name in _INS:
        a = _np.ascontiguousarray(inputs[name])
        arrays[f"in_{name}_dram"] = a
        args.append(nc.dram_tensor(f"in_{name}_dram", a.shape, _mybir.dt.from_np(a.dtype), kind="ExternalInput").ap())
    for i, (shape, dtype) in enumerate(_OUTS):
        dt = _mybir.dt.from_np(_np.dtype(dtype))
        args.append(nc.dram_tensor(f"out_{i}_dram", shape, dt, kind="ExternalOutput").ap())
    build_kernel(nc, *args)
    r = _run(nc, [arrays], core_ids=[0])
    got = tuple(r.results[0][f"out_{i}_dram"] for i in range(len(_OUTS)))
    return got[0]
```

```python
from contextlib import ExitStack

import concourse.bass as bass
from concourse import mybir


def build_kernel(nc, x, src, dst, edge_attr, mW1, mb1, mW2, mb2, uW1, ub1, uW2, ub2,
                 gamma, beta, Wr, br, W1, b1, W2, b2, out):
    F32, F16, BF16, I32 = mybir.dt.float32, mybir.dt.float16, mybir.dt.bfloat16, mybir.dt.int32
    ALU = mybir.AluOpType
    ACT = mybir.ActivationFunctionType
    AX = mybir.AxisListType
    ds = bass.ds

    N, D = x.shape
    E, EA = edge_attr.shape
    H = mW2.shape[0]
    NX, DM, HE = W1.shape
    EPS = 1e-5
    W = -(-N // 128)
    NP = W * 128
    TAIL = N - (W - 1) * 128
    EP = 125
    EC = E // EP
    PAIRS = (E + W * 255) // 256
    NT = 2 * PAIRS
    CH = EC // W
    RW = EA + 2
    LEAD = 4
    EVEN = 2 * LEAD
    KE = 6 * EA
    NA = 2 * NP
    NTE = (NA + NX * 127) // 128
    AHEAD = 4
    RING = 8
    ROUNDS = NTE // RING + 1
    KD, KH = D // 128, H // 128
    WC = KD * H
    NO_NODE = 200.0
    assert KH * DM == WC and HE == H and NTE == 57 and D == DM
    assert EP * EC == E and CH * W == EC and NT % 8 == 0 and W % 2 == 1

    recs_d = nc.dram_tensor("recs_d", [128 * NT, RW], F32, kind="Internal").ap()
    z_d = nc.dram_tensor("z_d", [NP, D], F32, kind="Internal").ap()
    y_d = nc.dram_tensor("y_d", [NA + 128 * NTE, D], F32, kind="Internal").ap()
    q_d = nc.dram_tensor("q_d", [NP, 2 * H], F16, kind="Internal").ap()

    with ExitStack() as ctx:
        def sb(name, shape, dt=F32):
            return ctx.enter_context(nc.sbuf_tensor("sb_" + name, list(shape), dt))

        def sem(name):
            return ctx.enter_context(nc.semaphore(name))

        r_xs = sb("r_xs", [128, W * D])
        r_xt = sb("r_xt", [128, KD * NP])
        r_p = sb("r_p", [128, W * H])
        r_h = sb("r_h", [128, W * H])
        r_w = sb("r_w", [128, 12288])

        xs = r_xs[:, :].rearrange("p (w d) -> p w d", w=W)
        xnT = r_xt[:, :].rearrange("p (k n) -> p k n", k=KD)
        P12 = r_p[:, :].bitcast(F16).rearrange("p (w s h) -> p w s h", w=W, s=2)
        Hacc = r_h[:, :].rearrange("p (w h) -> p w h", w=W)
        ea = r_h[:, W * D:W * D + EC * EA].rearrange("p (c a) -> p c a", c=EC)

        def carve(region, start):
            at = [start]

            def take(shape, dt=F32):
                n = 1
                for s in shape:
                    n *= s
                words = n if dt in (F32, I32) else n // 2
                a = region[:, at[0]:at[0] + words]
                at[0] += words
                assert at[0] <= region.shape[1], (at[0], region.shape)
                if dt != F32:
                    a = a.bitcast(dt)
                if len(shape) == 2:
                    a = a.rearrange("p (a b) -> p a b", a=shape[0])
                if len(shape) == 3:
                    a = a.rearrange("p (a b c) -> p a b c", a=shape[0], b=shape[1])
                return a
            return take

        t1 = carve(r_w, 0)
        hi_b = t1([EC], BF16)
        lo_b = t1([EC], BF16)
        dst_i = t1([EC], I32)
        ranked = t1([CH, W])
        slot_c = t1([3, CH], I32)
        rec = t1([2, CH, RW])
        idx_s = t1([2, CH], I32)
        oh_lo = t1([CH, 128], BF16)
        oh_hi = t1([CH, W], BF16)
        wAB = t1([4, H])
        b1row = t1([H])
        xstage = t1([D])
        xTst = t1([KD, 128])
        qst = t1([2, 2 * H], F16)
        sq_rows = t1([256])
        pair_no = t1([PAIRS])
        wtab = t1([PAIRS])
        ub2b = t1([D])
        mask = r_p[:, 0:W * EC // 2].bitcast(BF16).rearrange("p (b c) -> p b c", b=W)
        th = carve(r_h, 0)
        scan = th([W, EC], F16)
        bns1 = th([W, 6])
        mv1 = th([W, 2])
        assert W * EC // 2 + W * 8 <= W * D
        cdup = r_p[0:KE, 11700:11700 + H]
        t3 = carve(r_w, 0)
        recg = sb("recg", [128, 2, 4, RW])
        rec6 = t3([2, 4, 128], BF16)
        rest = sb("rest", [128, 4, EA])[:, :, :]
        trs = t3([2, 8 * 128], BF16)
        oh = t3([8, 128], BF16)
        qg = t3([8, 2 * H], F16)
        h1 = t3([4, H], F16)
        h2 = t3([4, H], F16)
        wst = t1([2, WC])
        t4 = carve(r_w, 0)
        HT = [t4([KH, H]), t4([KH, H])]
        aggT = t4([KD, H])
        uT = t4([KH, H])
        t4w = carve(r_w, 8192)
        mW2s = t4w([KH, D])
        uW1s = t4w([2 * KD, H])
        uW2s = t4w([KH, D])
        t4p = carve(r_p, 0)
        hst = t4p([H])
        diag = t4p([H])
        mb2b = t4p([D])
        zst = t4p([2, D])
        zTst = t4p([KD, 128])
        gam = t4p([D])
        bet = t4p([D])
        bns = t4p([8])
        mv = t4p([4, 2])
        zr = t4p([6, 4])
        z3 = r_h[:, 0:W * D].rearrange("p (w c) -> p w c", w=W)
        z16 = r_h[:, 0:W * D].bitcast(F16).rearrange("p (w c) -> p w c", w=W)
        W1p = r_p[:, 0:NX * WC].bitcast(F16).rearrange("p (e s k h) -> p e s k h", e=NX, s=2, k=KD)
        W2p = r_w[:, 4096:4096 + NX * WC].bitcast(F16).rearrange("p (e s k d) -> p e s k d", e=NX, s=2, k=KH)
        wstage = r_xt[:, 0:6 * WC].rearrange("p (r w) -> p r w", r=6)
        t5 = carve(r_w, 0)
        rt = t5([4, W, NX])
        rs = t5([8, W])
        m2 = t5([NX, 2 * W])
        s2 = t5([NX, 2 * W])
        pr = t5([8, NX])
        slot_f = t5([2 * W])
        part_f = t5([2, 2 * W])
        carried = t5([2 * W, 2])
        row_hot = t5([4, 128])
        tile_val = t5([4, 2 * NTE])
        pad_of = t5([NTE])
        bare = t5([NTE], I32)
        t5p = carve(r_p, NX * WC)
        zt = t5p([RING, D])
        zT = t5p([2, 2 * KD, 128], F16)
        hp = t5p([2, 2 * KH, 128], F16)
        t5x = carve(r_h, W * D)
        h32 = t5x([2, H])
        yo = t5x([RING, D])
        b2r = t5x([NX, D], BF16)
        b2s = t5x([D])
        b2p = [t5x([D], BF16) for _ in range(3)]
        y_in = r_p[:, :].rearrange("p (w s d) -> p w s d", w=W, s=2)

        C6 = sb("C6", [KE, H], BF16)
        ident = sb("ident", [128, 128])
        identb = sb("identb", [128, 128], BF16)
        identh = sb("identh", [128, 128], F16)
        ones3 = sb("ones3", [3, 128], BF16)
        place = sb("place", [128, 2, W], I32)
        before = sb("before", [128, 128])
        iota = sb("iota", [128, 128], BF16)
        iota_w = sb("iota_w", [128, W], BF16)
        ones = sb("ones", [128, 128])
        wtab_i = sb("wtab_i", [128, PAIRS], I32)
        deg_s = sb("deg_s", [128, W])
        ub1c = sb("ub1c", [128, KH])
        Wrs = sb("Wrs", [128, KD, NX])
        brb = sb("brb", [128, NX])
        b1c = sb("b1c", [128, NX, KH])
        lg = sb("lg", [128, W, NX])
        fro = sb("fro", [128, 20])
        frs = sb("frs", [128, 3])
        sx = sb("sx", [128, 16])
        sxi = sb("sxi", [128, 8], I32)
        etab = sb("etab", [128, ROUNDS * RING])
        ep = sb("ep", [128, ROUNDS])
        ep_i = sb("ep_i", [128, ROUNDS], I32)
        tile_no = sb("tile_no", [128, ROUNDS * RING])
        slot_i = sb("slot_i", [128, 2 * W], I32)
        low_i = sb("low_i", [128, 2 * W], I32)
        padm = sb("padm", [128, NTE])
        at_tile = sb("at_tile", [128, NTE, 2], I32)
        weight = sb("weight", [128, NTE])
        at_ring = sb("at_ring", [128, RING, 2], I32)
        epsc = sb("epsc", [128, 1])
        mx = sb("mx", [128, 8])
        mxa = sb("mxa", [128, 8])
        sc = sb("sc", [128, 8])
        sci = sb("sci", [128, 8], I32)
        stat = sb("stat", [128, 6, W])
        riota = sb("riota", [128, NX])
        f_sc, finv = sc[:, 1:2], sc[:, 2:3]
        g_z, g_1, g_h, g_2 = (sx[:, n:n + 1] for n in range(4))
        un1, g_o, un2 = (sx[:, n:n + 1] for n in range(4, 7))

        ps = [ctx.enter_context(nc.psum_tensor(f"ps{i}", [128, 512], F32)) for i in range(8)]

        s_src = sem("src_loaded")
        s_x = sem("x_loaded")
        s_ea = sem("edges_loaded")
        s_w = sem("weights_loaded")
        s_cr = sem("c_replicated")
        s_c6 = sem("c6_placed")
        s_cst = sem("constants_made")
        s_pad = sem("pads_written")
        s_padm = sem("pads_made")
        dv = sem("dve_done")
        s_mx = sem("maxima_made")
        s_all = sem("maxima_reduced")
        s_f = sem("scale_made")
        s_sp = sem("c_split")
        s_cnt = sem("counts_made")
        s_tot = sem("totals_made")
        s_sqr = sem("variance_made")
        s_sd = sem("deviation_made")
        s_chunk = sem("chunk_made")
        s_sc = [sem(f"chunk_scattered{i}") for i in range(2)]
        s_oh = sem("onehots_made")
        s_hist = sem("onehots_counted")
        s_xst = sem("xn_tile_made")
        s_tp = sem("xn_tile_transposed")
        s_xT = sem("xn_tile_evacuated")
        s_pq = sem("pq_made")
        s_pq1 = sem("pq_first_half")
        s_pq2 = sem("pq_second_half")
        s_qst = [sem(f"q_stored{i}") for i in range(2)]
        s_wtab = sem("window_table_made")
        s_deg = sem("degree_made")
        s_ub = sem("ub2_loaded")
        s_wp = sem("small_weights_loaded")
        u_mb = sem("mb2_loaded")
        u_dg = sem("u_diagonal_made")
        s_hz = sem("sums_zeroed")
        e_rec = [sem(f"records_in{i}") for i in range(2)]
        e_oh = sem("tile_onehot_made")
        e_sp = sem("group_split")
        e_tr = sem("group_transposed")
        e_te = sem("group_evacuated")
        e_q = [sem(f"q_rows_in{i}") for i in range(8)]
        e_s = sem("tile_summed")
        e_h1 = sem("hidden_first_half")
        e_h2 = sem("hidden_second_half")
        e_agg = sem("tile_aggregated")
        e_acc = sem("pair_accumulated")
        u_w = sem("update_weights_loaded")
        u_st = sem("u_sum_staged")
        u_tr = sem("u_sum_transposed")
        u_ht = sem("u_sum_evacuated")
        u_ag = sem("u_agg_made")
        u_ae = sem("u_agg_evacuated")
        u_u = sem("u_hidden_made")
        u_ue = sem("u_hidden_evacuated")
        u_o = sem("u_out_made")
        u_x = sem("u_x_updated")
        z_out = sem("z_stored")
        n_w = [sem(f"norm_chunk_in{i}") for i in range(2)]
        n_f = sem("norm_chunk_squared")
        n_r = sem("norm_sums_reduced")
        n_t = sem("norm_totals_made")
        n_q = sem("norm_totals_copied")
        n_s = sem("norms_made")
        n_gb = sem("gamma_beta_loaded")
        z_u = sem("z_variances_made")
        z_sd = sem("z_deviations_made")
        z_st = sem("z_tile_staged")
        z_1 = sem("z_first_half")
        z_2 = sem("z_second_half")
        z_tr = sem("z_tile_transposed")
        z_te = sem("z_tile_evacuated")
        z_lg = sem("z_logits_made")
        z_le = sem("z_logits_evacuated")
        z_gap = sem("z_gap_made")
        z_ex = sem("z_gap_exp")
        r_cnt = sem("route_counts_made")
        r_tot = sem("route_totals_made")
        r_hot = sem("route_onehots_made")
        r_put = sem("route_placed")
        x_at = sem("x_indices_made")
        r_et = sem("expert_table_made")
        w_in = [sem(f"w_chunk_in{i}") for i in range(6)]
        w_a = sem("w_first_half")
        w_b = sem("w_second_half")
        b_in = sem("b2_loaded")
        b_p = sem("b2_parts_made")
        b_r = sem("b2_parts_placed")
        x_in = [sem(f"x_rows_in{i}") for i in range(RING)]
        x_tr = sem("x_rows_transposed")
        x_te = sem("x_rows_evacuated")
        x_h = sem("x_hidden_made")
        x_g = sem("x_hidden_gelu")
        x_h1 = sem("x_hidden_first_half")
        x_h2 = sem("x_hidden_second_half")
        x_o = sem("x_out_made")
        x_y = sem("x_out_weighted")
        x_sc = [sem(f"x_out_scattered{i}") for i in range(RING)]
        y_ld = [sem(f"y_loaded{i}") for i in range(5)]
        y_ad = sem("y_added")
        s_gp, s_gs, s_gd, s_ga = (sem(f"gates_{n}") for n in ("gpsimd", "sync", "vector", "scalar"))
        s_out = sem("result_stored")

        block = ctx.enter_context(nc.Block())

        def gate(eng, passed):
            eng.sem_inc(passed, 1)

        def paired(eng, count, body):
            body(0, 0)
            body(1, 1)
            with eng.Fori(1, count // 2) as i:
                body(2 * i, 0)
                body(2 * i + 1, 1)
            body(count - 1, (count - 1) % 2)

        def static_ge(k, n):
            return (not isinstance(k, int)) or k >= n

        FULL = N - TAIL
        x_full = x[0:FULL, :].rearrange("(w p) d -> p w d", p=128)
        rec_rows = recs_d.rearrange("(q t) r -> q (t r)", q=128)
        row = lambda a: a.rearrange("(o n) -> o n", o=1)
        NCH = W // 4
        assert W - NCH * 4 == 1

        src_i = r_p[0:EP, 12250:12250 + EC].bitcast(I32)

        def x_out(w0, m):
            return out[w0 * 128:(w0 + m) * 128, :].rearrange("(w p) d -> p w d", p=128)

        def pair_chunks(eng, update_chunk):
            with eng.Fori(0, (NCH - 2) // 2) as i:
                update_chunk(2 * i + 1, 1, 4, 4, 4)
                update_chunk(2 * i + 2, 0, 4, 4, 4)

        def w_half(n, s):
            half = W1p[:, n, s] if n < NX else W2p[:, n - NX, s]
            return half.rearrange("p k h -> p (k h)")

        def ring(eng, body):
            for T in range(RING):
                body(T, 0, T)
            with eng.Fori(1, NTE // RING - 1) as i:
                for j in range(RING):
                    body(RING * i + j, i, j)
            for T in range(NTE // RING * RING - RING, NTE):
                body(T, T // RING, T % RING)

        def round_experts(eng, i):
            return eng.value_load(ep_i[0:1, i:i + 1] if isinstance(i, int) else ep_i[0:1, ds(i, 1)],
                                  min_val=0, max_val=NX ** RING - 1)

        def tile_expert(packed, j):
            return (packed >> (3 * j)) % NX if j else packed % NX

        @block.sync
        def _(sp):
            sp.dma_start(src_i, src.rearrange("(p c) -> p c", p=EP)).then_inc(s_src, 16)
            sp.dma_start(ea[0:EP], edge_attr.rearrange("(p c) a -> p c a", p=EP)).then_inc(s_ea, 16)
            sp.dma_start(dst_i[0:EP, :], dst.rearrange("(p c) -> p c", p=EP)).then_inc(s_ea, 16)
            sp.wait_ge(s_padm, 1)
            sp.dma_start(xs[:, 0:W - 1, :], x_full).then_inc(s_x, 16)
            sp.dma_start(xs[0:TAIL, W - 1, :], x[FULL:N, :]).then_inc(s_x, 16)
            sp.dma_start(wAB, mW1[0:2 * D, :].rearrange("(k p) h -> p k h", p=128)).then_inc(s_w, 16)
            sp.dma_start(b1row[0:1, :], row(mb1)).then_inc(s_w, 16)
            for r in range(6):
                sp.dma_start(cdup[r * EA:(r + 1) * EA, :], mW1[2 * D:2 * D + EA, :]).then_inc(s_cr, 16)
            sp.dma_start(ub2b, row(ub2).broadcast_to([128, D])).then_inc(s_ub, 16)
            sp.dma_start(ub1c[:, :], ub1.rearrange("(k p) -> p k", p=128), allow_slow_non_contiguous=True).then_inc(s_wp, 16)
            sp.dma_start(Wrs[:, :, :], Wr.rearrange("(k p) e -> p k e", p=128)).then_inc(s_wp, 16)
            sp.dma_start(brb[:, :], row(br).broadcast_to([128, NX])).then_inc(s_wp, 16)
            sp.dma_start(b1c[:, :, :], b1.rearrange("e (k p) -> p e k", p=128), allow_slow_non_contiguous=True).then_inc(s_wp, 16)
            sp.wait_ge(s_sp, 1)
            for r, part in enumerate((0, 1, 2, 0, 1, 0)):
                sp.dma_start(C6[r * EA:(r + 1) * EA, :], qst[r * EA:(r + 1) * EA, 0, 0:H].bitcast(BF16) if part == 0
                             else qst[r * EA:(r + 1) * EA, 0, H:2 * H].bitcast(BF16) if part == 1
                             else qst[r * EA:(r + 1) * EA, 1, 0:H].bitcast(BF16)).then_inc(s_c6, 16)

            def store_q(k, par):
                sp.wait_ge(s_pq2, 2 * k + 2)
                sp.wait_ge(s_pq1, 2 * k + 2)
                gate(sp, s_gs)
                rows = q_d[k * 128:(k + 1) * 128, :] if isinstance(k, int) else q_d[ds(k * 128, 128), :]
                sp.dma_start(rows, qst[:, par, :]).then_inc(s_qst[par], 16)
            paired(sp, W, store_q)
            for n in range(2 * NX):
                if n >= 2:
                    sp.wait_ge(n_f, n - 1)
                mat = W1 if n < NX else W2
                sp.dma_start(wst[:, n % 2, :], mat[n % NX].rearrange("(p a) h -> p (a h)", p=128)).then_inc(n_w[n % 2], 16)
            for par in range(2):
                sp.wait_ge(s_sc[par], 16 * CH * ((W + 1 - par) // 2))
            sp.wait_ge(s_hz, 1)
            def load_group(g, i, par):
                if static_ge(i, 1):
                    sp.wait_ge(e_sp, 4 * g - 4)
                    sp.wait_ge(e_oh, 4 * g - 4)
                    gate(sp, s_gs)
                    for j in range(4):
                        sp.wait_ge(e_q[4 * par + j], 16 * i)
                gate(sp, s_gs)
                cols = (rec_rows[:, g * 4 * RW:(g + 1) * 4 * RW] if isinstance(g, int)
                        else rec_rows[:, ds(g * (4 * RW), 4 * RW)])
                sp.dma_start(recg[:, par, :, :].rearrange("p a b -> p (a b)"), cols).then_inc(e_rec[par], 16)
            load_group(0, 0, 0)
            load_group(1, 0, 1)
            sp.wait_ge(n_f, 2 * NX + 1)
            sp.dma_start(mW2s, mW2.rearrange("(k p) d -> p k d", p=128)).then_inc(u_w, 16)
            sp.dma_start(uW1s, uW1.rearrange("(k p) h -> p k h", p=128)).then_inc(u_w, 16)
            sp.dma_start(uW2s, uW2.rearrange("(k p) d -> p k d", p=128)).then_inc(u_w, 16)
            with sp.Fori(1, NT // 8) as i:
                load_group(2 * i, i, 0)
                load_group(2 * i + 1, i, 1)

            sp.wait_ge(e_s, NT)
            sp.dma_start(mb2b, row(mb2).broadcast_to([128, D])).then_inc(u_mb, 16)
            sp.dma_start(gam, row(gamma).broadcast_to([128, D])).then_inc(n_gb, 16)
            sp.dma_start(bet, row(beta).broadcast_to([128, D])).then_inc(n_gb, 16)

            def store_z(w0, w1):
                sp.wait_ge(z_2, w1 + 1)
                sp.dma_start(z_d[w0 * 128:w1 * 128, :].rearrange("(w p) d -> p w d", p=128), z3[:, w0:w1, :]).then_inc(z_out, 16)
            store_z(0, 8)
            store_z(8, 16)
            sp.wait_ge(u_u, KH * (NCH + 1))
            for n in range(2 * NX):
                if n >= 6:
                    sp.wait_ge(w_b, n - 5)
                mat = W1 if n < NX else W2
                view = mat[n % NX].rearrange("(k p) h -> p k h", p=128)
                sp.dma_start(wstage[:, n % 6, :].rearrange("p (k h) -> p k h", h=mat.shape[2]), view).then_inc(w_in[n % 6], 16)
                if n == 3:
                    store_z(16, W)
                    sp.dma_start(b2s[0:NX, :], b2).then_inc(b_in, 16)
            sp.wait_ge(b_p, 1)
            for r in range(3):
                sp.dma_start(b2r[r:r + 1, :, :].rearrange("p e d -> p (e d)"), b2p[r][0:NX, :]).then_inc(b_r, 16)

            for j in range(RING):
                sp.wait_ge(x_sc[j], 16 * ((NTE - 1 - j) // RING + 1))
            for n in range(5):
                sp.dma_start(y_in[:, 5 * n:5 * n + 5, :, :],
                             y_d[640 * 2 * n:640 * 2 * (n + 1), :].rearrange("(w p s) d -> p w s d", p=128, s=2)).then_inc(y_ld[n], 16)
            for n in range(5):
                sp.wait_ge(y_ad, n + 1)
                m = min(5, W - 1 - 5 * n)
                sp.dma_start(x_out(5 * n, m), xs[:, 5 * n:5 * n + m, :]).then_inc(s_out, 16)
            sp.dma_start(out[FULL:N, :], xs[0:TAIL, W - 1, :]).then_inc(s_out, 16)
            sp.wait_ge(s_out, 96)

        @block.gpsimd
        def _(pool):
            g = nc.gpsimd
            g.memset(xs[:, W - 1, :], 0.0).then_inc(s_padm, 1)
            g.iota(iota[:, :], [[1, 128]], base=0, channel_multiplier=0, allow_small_or_imprecise_dtypes=True).then_inc(s_cst, 1)
            g.iota(iota_w[:, :], [[1, W]], base=0, channel_multiplier=0, allow_small_or_imprecise_dtypes=True).then_inc(s_cst, 1)
            g.memset(rec[:, :, :, :].rearrange("p a b c -> p (a b c)"), 0.0).then_inc(s_padm, 1)
            pool.wait_ge(s_padm, 2)
            g.memset(rec[:, :, :, EA + 1:EA + 2].rearrange("p a b c -> p (a b c)"), NO_NODE).then_inc(s_padm, 1)
            pool.wait_ge(s_padm, 3)
            per, left = 2 * CH, NT
            n_pad = 0
            while left:
                m = min(per, left)
                pool.dma_start(rec_rows[:, (NT - left) * RW:(NT - left + m) * RW],
                               rec.rearrange("p a b c -> p (a b c)")[:, 0:m * RW]).then_inc(s_pad, 16)
                left -= m
                n_pad += 1
            g.memset(ident[:, :], 0.0).then_inc(s_cst, 1)
            g.memset(before[:, :], 0.0).then_inc(s_cst, 1)
            g.memset(ones[:, :], 1.0).then_inc(s_cst, 1)
            g.memset(epsc[:, :], EPS).then_inc(s_cst, 1)
            g.memset(mx[:, :], 0.0).then_inc(s_cst, 1)
            g.iota(pair_no, [[1, PAIRS]], base=0, channel_multiplier=0, allow_small_or_imprecise_dtypes=True).then_inc(s_cst, 1)
            g.iota(riota[:, :], [[-1, NX]], base=NX, channel_multiplier=0, allow_small_or_imprecise_dtypes=True).then_inc(s_cst, 1)
            g.iota(tile_no[:, :], [[1, ROUNDS * RING]], base=0, channel_multiplier=0, allow_small_or_imprecise_dtypes=True).then_inc(s_cst, 1)
            pool.wait_ge(s_cst, 10)
            g.affine_select(out=ident[:, :], in_=ident[:, :], compare_op=ALU.not_equal, fill=1.0,
                            base=0, pattern=[[-1, 128]], channel_multiplier=1).then_inc(s_cst, 1)
            g.affine_select(out=before[:, :], in_=before[:, :], compare_op=ALU.is_ge, fill=1.0,
                            base=0, pattern=[[-1, 128]], channel_multiplier=1).then_inc(s_cst, 1)
            pool.wait_ge(s_cst, 12)
            g.tensor_copy(identb[:, :], ident[:, :]).then_inc(s_cst, 1)
            g.tensor_copy(identh[:, :], ident[:, :]).then_inc(s_cst, 1)
            g.memset(ones3[:, :], 1.0).then_inc(s_cst, 1)
            for k in range(2):
                g.iota(place[:, k, :], [[256, W]], base=k + 1, channel_multiplier=2).then_inc(s_cst, 1)
            g.iota(padm[:, :], [[128, NTE]], base=NA + 1, channel_multiplier=1, allow_small_or_imprecise_dtypes=True).then_inc(s_cst, 1)
            pool.wait_ge(s_pad, 16 * n_pad)

            def scatter(k, par):
                pool.wait_ge(s_chunk, k + 1)
                gate(pool, s_gp)
                for c in range(CH):
                    g.indirect_dma_start(recs_d, bass.IndirectOffsetOnAxis(ap=idx_s[0:EP, par, c:c + 1], axis=0),
                                         rec[0:EP, par, c, :], None).then_inc(s_sc[par], 16)
            scatter(0, 0)
            pool.wait_ge(s_mx, 5)
            g.partition_all_reduce(mxa[:, :], mx[:, :], 128, bass.bass_isa.ReduceOp.max).then_inc(s_all, 1)
            scatter(1, 1)
            with pool.Fori(1, W // 2) as i:
                scatter(2 * i, 0)
                scatter(2 * i + 1, 1)
            scatter(W - 1, (W - 1) % 2)

            for par in range(2):
                pool.wait_ge(s_qst[par], 16 * ((W + 1 - par) // 2))
            def gather(i):
                for j in range(8):
                    if j % 4 == 0:
                        pool.wait_ge(e_rec[j // 4], 16 * (i + 1))
                    if static_ge(i, 1):
                        pool.wait_ge(e_s, 8 * i + j - 7)
                    gate(pool, s_gp)
                    g.indirect_dma_start(qg[:, j, :], None, q_d, bass.IndirectOffsetOnAxis(
                        ap=recg[:, j // 4, j % 4, EA:EA + 1].bitcast(I32), axis=0)).then_inc(e_q[j], 16)
            gather(0)
            with pool.Fori(1, NT // 8) as i:
                gather(i)

            for n in range(2 * NX):
                pool.wait_ge(w_a, n + 1)
                g.tensor_tensor(w_half(n, 1), wstage[:, n % 6, :], w_half(n, 0), ALU.subtract).then_inc(w_b, 1)

            pool.wait_ge(z_out, 48)

            def gather_rows(T, j):
                pool.wait_ge(x_at, T + 1)
                gate(pool, s_gp)
                g.indirect_dma_start(zt[:, j, :], None, z_d, bass.IndirectOffsetOnAxis(
                    ap=at_ring[:, j, 0:1], axis=0)).then_inc(x_in[j], 16)

            def experts_io(T, i, j):
                if not (isinstance(T, int) and T + AHEAD >= NTE):
                    gather_rows(T + AHEAD, (j + AHEAD) % RING)
                pool.wait_ge(x_y, T + 1)
                gate(pool, s_gp)
                g.indirect_dma_start(y_d, bass.IndirectOffsetOnAxis(ap=at_ring[:, j, 1:2], axis=0),
                                     yo[:, j, :], None).then_inc(x_sc[j], 16)
            for T in range(AHEAD):
                gather_rows(T, T)
            ring(pool, experts_io)

        @block.scalar
        def _(act):
            a = nc.scalar
            act.wait_ge(s_sqr, 1)
            act.wait_ge(s_cst, 10)
            a.activation(stat[:, 2, :], mv1[:, :, 1], ACT.Sqrt, bias=epsc[:, :], scale=1.0).then_inc(s_sd, 1)

            def node_tile(k, par):
                act.wait_ge(s_tp, k + 1)
                if static_ge(k, 1):
                    act.wait_ge(s_pq, 2 * k)
                a.activation(xTst.rearrange("p k n -> p (k n)"), ps[0][:, 0:D], ACT.Copy).then_inc(s_xT, 1)
                dst_t = xnT[:, :, k * 128:(k + 1) * 128] if isinstance(k, int) else xnT[:, :, ds(k * 128, 128)]
                a.activation(dst_t, ps[0][:, 0:D].rearrange("p (k n) -> p k n", k=KD), ACT.Copy).then_inc(s_xT, 1)
                act.wait_ge(s_pq, 2 * k + 1)
                pd = P12[:, k, 0, :] if isinstance(k, int) else P12[:, ds(k, 1), 0, :].rearrange("p a h -> p (a h)")
                a.activation(pd, ps[1][:, :], ACT.Copy).then_inc(s_pq1, 1)
                act.wait_ge(s_pq, 2 * k + 2)
                if static_ge(k, 2):
                    act.wait_ge(s_qst[par], 8 * k if par == 0 else 8 * k - 8)
                a.activation(qst[:, par, 0:H], ps[2][:, :], ACT.Copy).then_inc(s_pq1, 1)
            act.wait_ge(s_c6, 96)
            paired(act, W, node_tile)
            for n in range(2 * NX):
                act.wait_ge(n_w[n % 2], 16 * (n // 2 + 1))
                a.activation(wst[:, n % 2, :], wst[:, n % 2, :], ACT.Square, accum_out=fro[:, n:n + 1]).then_inc(n_f, 1)
            act.wait_ge(s_wp, 64)
            act.wait_ge(n_f, 2 * NX)
            a.activation(wst[:, 0, 0:NX * KH], b1c[:, :, :].rearrange("p a b -> p (a b)"), ACT.Square,
                         accum_out=fro[:, 2 * NX:2 * NX + 1]).then_inc(n_f, 1)
            act.wait_ge(n_q, 1)
            a.activation(frs[:, :], sx[:, 8:11], ACT.Sqrt).then_inc(n_s, 1)

            def te(g, i):
                act.wait_ge(e_tr, g + 1)
                if static_ge(i, 1):
                    act.wait_ge(e_s, 4 * g - 4)
            def evac(par):
                a.activation(trs[:, par, :], ps[7][:, :].bitcast(BF16), ACT.Copy).then_inc(e_te, 1)

            def edge_body(i, last=False):
                for j in range(8):
                    t = 8 * i + j
                    act.wait_ge(e_s, t + 1)
                    if static_ge(i, 1) or j >= 4:
                        act.wait_ge(e_agg, t - 3)
                    a.activation(h1[:, j % 4, :], ps[j % 4][:, :], ACT.Relu).then_inc(e_h1, 1)
                    if j == 2:
                        te(2 * i + 1, i)
                        evac(1)
                    if j == 6 and not last:
                        g = 2 * i + 2
                        act.wait_ge(e_tr, g + 1)
                        act.wait_ge(e_s, 4 * g - 4)
                        evac(0)
            te(0, 0)
            evac(0)
            edge_body(0)
            with act.Fori(1, NT // 8 - 1) as i:
                edge_body(i)
            edge_body(NT // 8 - 1, last=True)

            def update_chunk(c, par, n, nxt, prv):
                for m in range(KD):
                    act.wait_ge(u_ag, 2 * c + m + 1)
                    if static_ge(c, 1) and m == 0:
                        act.wait_ge(u_u, 4 * c)
                    a.activation(aggT[:, m, 0:n * 128], ps[1 + m][:, 0:n * 128], ACT.Copy).then_inc(u_ae, 1)
                if prv:
                    act.wait_ge(z_u, c)
                    a.activation(zr[:, 1, 0:prv], zr[:, 0, 0:prv], ACT.Sqrt).then_inc(z_sd, 1)
                for m in range(KH):
                    if m < nxt:
                        evacuate_sums(4 * c + 4 + m, m, 1 - par)
                    act.wait_ge(u_u, 4 * c + m + 1)
                    if m == 0 and static_ge(c, 1):
                        act.wait_ge(u_o, 4 * c)
                    a.activation(uT[:, m, 0:n * 128], ps[3 + m % 2][:, 0:n * 128], ACT.Relu,
                                 bias=ub1c[:, m:m + 1]).then_inc(u_ue, 1)
                for j in range(prv):
                    z_tile(4 * c - 4 + j, j)

            def evacuate_sums(t, j, par):
                act.wait_ge(u_tr, t + 1)
                gate(act, s_ga)
                cols = slice(j * 128, (j + 1) * 128)
                src_b = ps[0][:, :].rearrange("p (k n) -> p k n", k=KH)
                a.activation(HT[par][:, :, cols], src_b, ACT.Copy).then_inc(u_ht, 1)

            def z_tile(t, j):
                act.wait_ge(z_st, t + 1)
                zd = z16[:, t, 0:D] if isinstance(t, int) else z16[:, ds(t, 1), 0:D].rearrange("p a d -> p (a d)")
                a.activation(zd, zst[:, j % 2, :], ACT.Copy, scale=g_z).then_inc(z_1, 1)
                act.wait_ge(z_tr, t + 1)
                if static_ge(t, 1):
                    act.wait_ge(z_lg, t + 1)
                a.activation(zTst.rearrange("p k n -> p (k n)"), ps[7][:, 0:D], ACT.Copy).then_inc(z_te, 1)
                act.wait_ge(z_lg, t + 2)
                ld = lg[:, t, :] if isinstance(t, int) else lg[:, ds(t, 1), :].rearrange("p a d -> p (a d)")
                a.activation(ld, ps[7][:, D:D + NX], ACT.Copy).then_inc(z_le, 1)
            act.sem_inc(z_le, 1)
            for j in range(4):
                evacuate_sums(j, j, 0)
            update_chunk(0, 0, 4, 4, 0)
            pair_chunks(act, update_chunk)
            update_chunk(NCH - 1, (NCH - 1) % 2, 4, 1, 4)
            update_chunk(NCH, NCH % 2, 1, 0, 4)
            act.wait_ge(z_u, NCH + 1)
            a.activation(zr[:, 1, 0:1], zr[:, 0, 0:1], ACT.Sqrt).then_inc(z_sd, 1)
            z_tile(4 * NCH, 0)

            act.wait_ge(z_gap, 1)
            a.activation(rs[:, 3, :], rs[:, 2, :], ACT.Exp).then_inc(z_ex, 1)
            for n in range(2 * NX):
                act.wait_ge(w_in[n % 6], 16 * (n // 6 + 1))
                g_n = g_1 if n < NX else g_2
                a.activation(w_half(n, 0), wstage[:, n % 6, :], ACT.Copy, scale=g_n)
                a.activation(wstage[:, n % 6, :], wstage[:, n % 6, :], ACT.Copy, scale=g_n).then_inc(w_a, 1)

            act.wait_ge(r_et, 1)
            round_now = [None]

            def gelu(T, i, j):
                if j == 0:
                    round_now[0] = round_experts(a, i)
                e = tile_expert(round_now[0], j)
                act.wait_ge(x_h, T + 1)
                if static_ge(T, 2):
                    act.wait_ge(x_h2, T - 1)
                for m in range(KH):
                    ins = a.activation(h32[:, j % 2, m * 128:(m + 1) * 128], ps[2 + j % 2][:, m * 128:(m + 1) * 128],
                                       ACT.Gelu, bias=b1c[:, ds(e, 1), m:m + 1].rearrange("p a b -> p (a b)"), scale=un1)
                ins.then_inc(x_g, 1)
            ring(act, gelu)

        @block.vector
        def _(dve):
            v = nc.vector
            made = [0]

            def own(instruction, also=None):
                instruction.then_inc(dv, 1)
                made[0] += 1
                dve.wait_ge(dv, made[0])

            def small(n):
                return sq_rows[:, n * W:(n + 1) * W]

            tmp_i = r_p[0:EP, 10000:10000 + EC].bitcast(I32)
            tmp2_i = r_p[0:EP, 10800:10800 + EC].bitcast(I32)
            dve.wait_ge(s_src, 16)
            dve.wait_ge(s_cst, 2)
            own(v.tensor_scalar(tmp_i, src_i, 7, None, ALU.logical_shift_right))
            own(v.tensor_scalar(tmp2_i, src_i, 127, None, ALU.bitwise_and))
            own(v.tensor_copy(hi_b[0:EP, :], tmp_i))
            own(v.tensor_copy(lo_b[0:EP, :], tmp2_i))
            m3 = mask[0:EP]
            s3 = scan[0:EP]
            own(v.tensor_tensor(m3, hi_b[0:EP, :].unsqueeze(1).broadcast_to([EP, W, EC]),
                                iota_w[0:EP, :].unsqueeze(2).broadcast_to([EP, W, EC]), ALU.is_equal))
            mflat = m3.rearrange("p b c -> p (b c)")
            own(v.tensor_tensor_scan(s3.rearrange("p b c -> p (b c)"), mflat, mflat, 0.0, ALU.add, ALU.max))
            ends, cnt = small(0)[0:EP, :], small(1)[0:EP, :]
            own(v.tensor_copy(ends, s3[:, :, EC - 1]))
            own(v.tensor_copy(cnt[:, 0:1], ends[:, 0:1]))
            v.tensor_tensor(cnt[:, 1:W], ends[:, 1:W], ends[:, 0:W - 1], ALU.subtract).then_inc(s_cnt, 1)
            dve.wait_ge(s_cnt, 1)
            dve.wait_ge(s_tot, 1)
            tot, pre = ps[6][:, 0:W], ps[6][0:EP, 32:32 + W]
            own(v.tensor_scalar(sci_w := r_p[:, 11650:11650 + W].bitcast(I32), tot, 255.0, None, ALU.add))
            own(v.tensor_scalar(sci_w, sci_w, 8, None, ALU.logical_shift_right))
            own(v.tensor_copy(small(2), sci_w))
            own(v.tensor_tensor_scan(small(3), small(2), small(2), 0.0, ALU.add, ALU.max))
            own(v.tensor_tensor(small(4), small(3), small(2), ALU.subtract))
            off = small(5)[0:EP, :]
            own(v.scalar_tensor_tensor(off, small(4)[0:EP, :], 256.0, pre, ALU.mult, ALU.add))
            own(v.tensor_tensor(off, off, ends, ALU.subtract))
            own(v.scalar_tensor_tensor(off, off, -1.0, cnt, ALU.add, ALU.add))

            OWN = 8
            loop_at = [0, 0]

            def own_at(k):
                def own_k(ins):
                    ins.then_inc(dv, 1)
                    if isinstance(k, int):
                        made[0] += 1
                        dve.wait_ge(dv, made[0])
                    else:
                        loop_at[1] += 1
                        dve.wait_ge(dv, OWN * k + (loop_at[0] - OWN * EVEN + loop_at[1]))
                return own_k

            def chunk(c, par, own_k):
                rk = rec[0:EP, par]

                def cols(a):
                    return a[0:EP, c * CH:(c + 1) * CH] if isinstance(c, int) else a[0:EP, ds(c * CH, CH)]
                if static_ge(c, 1):
                    dve.wait_ge(s_hist, c)
                    gate(dve, s_gd)
                v.tensor_tensor(oh_lo[0:EP], cols(lo_b).unsqueeze(2).broadcast_to([EP, CH, 128]),
                                iota[0:EP, :].unsqueeze(1).broadcast_to([EP, CH, 128]), ALU.is_equal).then_inc(s_oh, 1)
                v.tensor_tensor(oh_hi[0:EP], cols(hi_b).unsqueeze(2).broadcast_to([EP, CH, W]),
                                iota_w[0:EP, :].unsqueeze(1).broadcast_to([EP, CH, W]), ALU.is_equal).then_inc(s_oh, 1)
                sc_c = scan[0:EP, :, c * CH:(c + 1) * CH] if isinstance(c, int) else scan[0:EP, :, ds(c * CH, CH)]
                own_k(v.tensor_tensor(ranked[0:EP], sc_c.rearrange("p b c -> p c b"),
                                      off.unsqueeze(1).broadcast_to([EP, CH, W]), ALU.add))
                dve.wait_ge(s_oh, 2 * c + 2)
                gate(dve, s_gd)
                own_k(v.tensor_tensor(ranked[0:EP], ranked[0:EP], oh_hi[0:EP], ALU.mult))
                at, part, tile_of = (slot_c[0:EP, n, :] for n in range(3))
                own_k(v.tensor_reduce(part.bitcast(F32), ranked[0:EP], AX.X, ALU.add))
                own_k(v.tensor_copy(at, part.bitcast(F32)))
                own_k(v.tensor_scalar(part, at, 127, None, ALU.bitwise_and))
                own_k(v.tensor_scalar(tile_of, at, 7, None, ALU.logical_shift_right))
                if static_ge(c, 2):
                    dve.wait_ge(s_sc[par], 8 * CH * c if par == 0 else 8 * CH * c - 8 * CH)
                if isinstance(c, int) and c == 0:
                    dve.wait_ge(s_pad, 16 * (-(-NT // (2 * CH))))
                gate(dve, s_gd)
                v.scalar_tensor_tensor(idx_s[0:EP, par, :], part, float(NT), tile_of, ALU.mult, ALU.add)
                v.tensor_copy(rk[:, :, 0:EA], cols(ea))
                v.tensor_copy(rk[:, :, EA:EA + 1].bitcast(I32), cols(dst_i).unsqueeze(2))
                v.tensor_copy(rk[:, :, EA + 1:EA + 2], cols(lo_b).unsqueeze(2)).then_inc(s_chunk, 1)

            dve.wait_ge(s_ea, 32)
            chunk(0, 0, own)
            chunk(1, 1, own)
            dve.wait_ge(s_cst, 18)

            dve.wait_ge(s_w, 32)
            dve.wait_ge(s_cr, 96)
            mxc = lambda n, p=128: mx[0:p, n:n + 1]
            v.tensor_reduce(mxc(0), wAB[:, 0:2, :].rearrange("p a b -> p (a b)"), AX.X, ALU.max, apply_absolute_value=True).then_inc(s_mx, 1)
            v.tensor_reduce(mxc(1), wAB[:, 2:4, :].rearrange("p a b -> p (a b)"), AX.X, ALU.max, apply_absolute_value=True).then_inc(s_mx, 1)
            v.tensor_reduce(mxc(2, KE), cdup[:, :], AX.X, ALU.max, apply_absolute_value=True).then_inc(s_mx, 1)
            v.tensor_reduce(mxc(3, 1), b1row[0:1, :], AX.X, ALU.max, apply_absolute_value=True).then_inc(s_mx, 1)
            v.tensor_reduce(mxc(4, EP), ea[0:EP].rearrange("p a b -> p (a b)"), AX.X, ALU.max, apply_absolute_value=True).then_inc(s_mx, 1)
            dve.wait_ge(s_all, 1)
            own(v.tensor_tensor(sc[:, 3:4], mxa[:, 0:1], mxa[:, 1:2], ALU.add))
            own(v.scalar_tensor_tensor(sc[:, 4:5], mxa[:, 2:3], float(EA), mxa[:, 4:5], ALU.mult, ALU.mult))
            own(v.scalar_tensor_tensor(sc[:, 5:6], sc[:, 3:4], float(D), sc[:, 4:5], ALU.mult, ALU.add))
            own(v.tensor_tensor(sc[:, 0:1], sc[:, 5:6], mxa[:, 3:4], ALU.add))
            own(v.tensor_scalar(sci[:, 0:1], sc[:, 0:1].bitcast(I32), 23, None, ALU.logical_shift_right))
            own(v.tensor_scalar(sci[:, 1:2], sci[:, 0:1], 40.0, 240.0, ALU.max, ALU.min))
            own(v.tensor_scalar(sci[:, 2:3], sci[:, 1:2], -1.0, 268.0, ALU.mult, ALU.add))
            own(v.tensor_scalar(sci[:, 3:4], sci[:, 1:2], -14.0, None, ALU.add))
            own(v.tensor_scalar(f_sc.bitcast(I32), sci[:, 2:3], 23, None, ALU.logical_shift_left))
            own(v.tensor_scalar(finv.bitcast(I32), sci[:, 3:4], 23, None, ALU.logical_shift_left))
            own(v.tensor_scalar(wAB.rearrange("p a b -> p (a b)"), wAB.rearrange("p a b -> p (a b)"), f_sc, None, ALU.mult))
            v.tensor_scalar(b1row[0:1, :], b1row[0:1, :], f_sc[0:1, :], None, ALU.mult).then_inc(s_f, 1)
            own(v.tensor_scalar(cdup[:, :], cdup[:, :], f_sc[0:KE, :], None, ALU.mult))
            cpart = [qst[0:KE, 0, 0:H].bitcast(BF16), qst[0:KE, 0, H:2 * H].bitcast(BF16), qst[0:KE, 1, 0:H].bitcast(BF16)]
            own(v.tensor_copy(cpart[0], cdup[:, :]))
            own(v.tensor_tensor(cdup[:, :], cdup[:, :], cpart[0], ALU.subtract))
            own(v.tensor_copy(cpart[1], cdup[:, :]))
            v.tensor_tensor(cpart[2], cdup[:, :], cpart[1], ALU.subtract).then_inc(s_sp, 1)

            chunk(2, 0, own)
            dve.wait_ge(s_x, 32)
            dve.wait_ge(s_ub, 16)
            for w in range(W):
                ins = v.bn_stats(bns1[:, w, :], xs[:, w, :])
            own(ins)
            for w in range(W):
                ins = v.bn_aggr(mv1[:, w, :], bns1[:, w, :])
            ins.then_inc(s_sqr, 1)
            dve.wait_ge(s_sqr, 1)
            dve.wait_ge(s_sd, 1)
            own(v.reciprocal(stat[:, 3, :], stat[:, 2, :]))
            own(v.tensor_scalar(stat[:, 4, :], mv1[:, :, 1], EPS, None, ALU.add))
            own(v.tensor_tensor(stat[:, 5, :], stat[:, 3, :], stat[:, 3, :], ALU.mult))
            own(v.tensor_tensor(stat[:, 4, :], stat[:, 4, :], stat[:, 5, :], ALU.mult))
            own(v.tensor_scalar(stat[:, 4, :], stat[:, 4, :], -0.5, 1.5, ALU.mult, ALU.add))
            own(v.tensor_tensor(stat[:, 3, :], stat[:, 3, :], stat[:, 4, :], ALU.mult))
            own(v.tensor_copy(stat[:, 0, :], mv1[:, :, 0]))
            chunk(3, 1, own)

            own(v.memset(wtab, 0.0))
            for b in range(W - 1):
                own(v.scalar_tensor_tensor(wtab, pair_no, small(3)[:, b:b + 1], wtab, ALU.is_ge, ALU.add))
            v.tensor_copy(wtab_i[:, :], wtab).then_inc(s_wtab, 1)

            def node(k, own_k):
                if static_ge(k, 1):
                    dve.wait_ge(s_tp, k)
                gate(dve, s_gd)
                xk = xs[:, k, :] if isinstance(k, int) else xs[:, ds(k, 1), :].rearrange("p a d -> p (a d)")
                mk, rk = (stat[:, n, k:k + 1] if isinstance(k, int) else stat[:, n, ds(k, 1)] for n in (0, 3))
                v.tensor_scalar(xstage, xk, mk, rk, ALU.subtract, ALU.mult).then_inc(s_xst, 1)
                dve.wait_ge(s_xst, k + 1)
                own_k(v.tensor_tensor(xk, xk, xstage, ALU.add))
                own_k(v.tensor_tensor(xk, xk, ub2b, ALU.add))

            def seconds(k, par):
                pd1 = P12[:, k, 0, :] if isinstance(k, int) else P12[:, ds(k, 1), 0, :].rearrange("p a h -> p (a h)")
                pd2 = P12[:, k, 1, :] if isinstance(k, int) else P12[:, ds(k, 1), 1, :].rearrange("p a h -> p (a h)")
                dve.wait_ge(s_pq1, 2 * k + 1)
                v.tensor_tensor(pd2, ps[1][:, :], pd1, ALU.subtract).then_inc(s_pq2, 1)
                dve.wait_ge(s_pq1, 2 * k + 2)
                v.tensor_tensor(qst[:, par, H:2 * H], ps[2][:, :], qst[:, par, 0:H], ALU.subtract).then_inc(s_pq2, 1)

            for c in range(LEAD, EVEN):
                node(2 * (c - LEAD), own)
                chunk(c, c % 2, own)
                seconds(2 * (c - LEAD), 0)
                node(2 * (c - LEAD) + 1, own)
                seconds(2 * (c - LEAD) + 1, 1)
            loop_at[0] = made[0]
            with dve.Fori(EVEN // 2, W // 2) as i:
                for par in range(2):
                    loop_at[1] = 0
                    k = 2 * i + par
                    own_k = own_at(k)
                    node(k, own_k)
                    chunk(k, par, own_k)
                    seconds(k, par)
                    assert loop_at[1] == OWN
            made[0] = loop_at[0] + OWN * (W - 1 - EVEN)
            node(W - 1, own)
            chunk(W - 1, 0, own)
            seconds(W - 1, 0)
            dve.wait_ge(s_hist, W)
            v.tensor_copy(deg_s[:, :], ps[4][:, 0:W]).then_inc(s_deg, 1)
            dve.wait_ge(s_oh, 2 * W)
            dve.wait_ge(s_pq2, 2 * W)
            dve.wait_ge(s_chunk, W)
            v.memset(rec6.rearrange("p a b c -> p (a b c)"), 0.0)
            v.memset(r_h[:, :], 0.0).then_inc(s_hz, 1)
            dve.wait_ge(s_hz, 1)
            dve.wait_ge(n_f, 2 * NX + 1)
            own(v.tensor_reduce(sx[:, 12:13], fro[:, 0:NX], AX.X, ALU.add))
            own(v.tensor_reduce(sx[:, 13:14], fro[:, NX:2 * NX], AX.X, ALU.add))
            v.tensor_copy(sx[:, 14:15], fro[:, 2 * NX:2 * NX + 1]).then_inc(n_r, 1)
            dve.wait_ge(n_t, 1)
            v.tensor_copy(sx[:, 8:11], ps[6][:, 64:67]).then_inc(n_q, 1)

            def one_hot(j, t):
                v.tensor_scalar(oh[:, j, :], iota[:, :], recg[:, j // 4, j % 4, EA + 1:EA + 2], None,
                                ALU.is_equal).then_inc(e_oh, 1)

            def split(g, q):
                par = g % 2 if isinstance(g, int) else g_par[0]
                blocks = rec6[:, par]
                raw = recg[:, par, :, 0:EA]
                block = lambda n, m=1: blocks[:, :, n * EA:(n + m) * EA]
                if q:
                    dve.wait_ge(e_sp, 4 * g + q)
                elif static_ge(g, 2):
                    dve.wait_ge(e_tr, g - 1)
                if q == 0:
                    v.tensor_copy(block(0), raw).then_inc(e_sp, 1)
                if q == 1:
                    v.tensor_copy(block(1), block(0))
                    v.tensor_copy(block(2), block(0))
                    v.tensor_tensor(rest, raw, block(0), ALU.subtract).then_inc(e_sp, 1)
                if q == 2:
                    v.tensor_copy(block(3), rest).then_inc(e_sp, 1)
                if q == 3:
                    v.tensor_copy(block(4), block(3))
                    v.tensor_tensor(block(5), rest, block(3), ALU.subtract).then_inc(e_sp, 1)
            g_par = [0]

            def accumulate(p):
                wi = v.value_load(wtab_i[0:1, p:p + 1] if isinstance(p, int) else wtab_i[0:1, ds(p, 1)],
                                  min_val=0, max_val=W - 1)
                acc = Hacc[:, ds(wi, 1), :].rearrange("p a h -> p (a h)")
                return acc

            def edge_body(i, last=False):
                for j in range(8):
                    t = 8 * i + j
                    ja = j + 6
                    if not last or ja < 8:
                        if ja % 4 == 0:
                            dve.wait_ge(e_rec[(ja // 4) % 2], 16 * (i + 1 + ja // 8))
                        if static_ge(i, 1) or j >= 2:
                            dve.wait_ge(e_agg, t - 1)
                        one_hot(ja % 8, t + 6)
                    dve.wait_ge(e_h1, t + 1)
                    v.scalar_tensor_tensor(h2[:, j % 4, :], ps[j % 4][:, :], 0.0, h1[:, j % 4, :],
                                           ALU.max, ALU.subtract).then_inc(e_h2, 1)
                    if j % 2 == 0 and (static_ge(i, 1) or j >= 4):
                        p = 4 * i + j // 2 - 2
                        dve.wait_ge(e_agg, 2 * p + 2)
                        if static_ge(p, 1):
                            dve.wait_ge(e_acc, p)
                        acc = accumulate(p)
                        v.tensor_tensor(acc, acc, ps[4 + (j // 2) % 2][:, :], ALU.add).then_inc(e_acc, 1)
                    if not last:
                        if j % 4 == 0:
                            dve.wait_ge(e_rec[j // 4], 16 * (i + 2))
                        g_par[0] = j // 4
                        split(2 * i + 2 + j // 4, j % 4)
            dve.wait_ge(e_rec[0], 16)
            for j in range(4):
                one_hot(j, j)
            dve.wait_ge(e_rec[1], 16)
            for j in range(4, 6):
                one_hot(j, j)
            for g in range(2):
                for q in range(4):
                    split(g, q)
            edge_body(0)
            with dve.Fori(1, NT // 8 - 1) as i:
                edge_body(i)
            edge_body(NT // 8 - 1, last=True)
            for p in (PAIRS - 2, PAIRS - 1):
                dve.wait_ge(e_agg, 2 * p + 2)
                dve.wait_ge(e_acc, p)
                acc = accumulate(p)
                v.tensor_tensor(acc, acc, ps[4 + p % 2][:, :], ALU.add).then_inc(e_acc, 1)
            dve.wait_ge(e_acc, PAIRS)

            def scale(out_f, bound, inverse=None):
                own(v.tensor_scalar(sxi[:, 0:1], bound.bitcast(I32), 23, None, ALU.logical_shift_right))
                own(v.tensor_scalar(sxi[:, 1:2], sxi[:, 0:1], 90.0, 190.0, ALU.max, ALU.min))
                own(v.tensor_scalar(sxi[:, 2:3], sxi[:, 1:2], -1.0, 268.0, ALU.mult, ALU.add))
                own(v.tensor_scalar(out_f.bitcast(I32), sxi[:, 2:3], 23, None, ALU.logical_shift_left))
            def stage_sums(t, j, before_diag=lambda: None):
                if static_ge(t, 1):
                    dve.wait_ge(u_tr, t)
                src_t = Hacc[:, t, :] if isinstance(t, int) else Hacc[:, ds(t, 1), :].rearrange("p a h -> p (a h)")
                v.tensor_scalar(hst, src_t, finv, None, ALU.mult).then_inc(u_st, 1)
                before_diag()
                dt = deg_s[:, t:t + 1] if isinstance(t, int) else deg_s[:, ds(t, 1)]
                v.tensor_scalar(diag[:, j * 128:(j + 1) * 128], ident[:, :], dt, None, ALU.mult).then_inc(u_dg, 1)

            def x_t(t):
                return xs[:, t, :] if isinstance(t, int) else xs[:, ds(t, 1), :].rearrange("p a d -> p (a d)")

            def update_results(c, n, prv, own_c):
                if prv:
                    dve.wait_ge(z_sd, c)
                    r, q = zr[:, 2, 0:prv], zr[:, 3, 0:prv]
                    own_c(v.reciprocal(r, zr[:, 1, 0:prv]))
                    own_c(v.tensor_tensor(q, r, r, ALU.mult))
                    own_c(v.tensor_tensor(q, q, zr[:, 0, 0:prv], ALU.mult))
                    own_c(v.tensor_scalar(q, q, -0.5, 1.5, ALU.mult, ALU.add))
                    own_c(v.tensor_tensor(r, r, q, ALU.mult))
                def stage(j):
                    tz = 4 * c - 4 + j
                    if j >= 2:
                        dve.wait_ge(z_tr, tz - 1)
                        dve.wait_ge(z_2, tz)
                    elif j == 0 and static_ge(tz, 1):
                        dve.wait_ge(z_2, tz + 1)
                    zj = zst[:, j % 2, :]
                    own_c(v.scalar_tensor_tensor(zj, x_t(tz), mv[:, j, 0:1], gam, ALU.subtract, ALU.mult))
                    v.scalar_tensor_tensor(zj, zj, zr[:, 2, j:j + 1], bet, ALU.mult, ALU.add).then_inc(z_st, 1)
                for j in range(min(2, prv)):
                    stage(j)
                for j in range(max(n, prv)):
                    tz, t = 4 * c - 4 + j, 4 * c + j
                    if j < n:
                        dve.wait_ge(u_o, t + 1)
                        v.tensor_tensor(x_t(t), x_t(t), ps[5 + j % 2][:, 0:D], ALU.add).then_inc(u_x, 1)
                        dve.wait_ge(u_x, t + 1)
                        gate(dve, s_gd)
                        own_c(v.bn_stats(bns[:, 0:6], x_t(t)))
                        gate(dve, s_gd)
                        own_c(v.bn_aggr(mv[:, j, :], bns[:, 0:6]))
                    if j < prv:
                        dve.wait_ge(z_st, tz + 1)
                        dve.wait_ge(z_1, tz + 1)
                        a1 = z16[:, tz, 0:D] if isinstance(tz, int) else z16[:, ds(tz, 1), 0:D].rearrange("p a d -> p (a d)")
                        a2 = z16[:, tz, D:2 * D] if isinstance(tz, int) else z16[:, ds(tz, 1), D:2 * D].rearrange("p a d -> p (a d)")
                        v.scalar_tensor_tensor(a2, zst[:, j % 2, :], g_z, a1, ALU.mult, ALU.subtract).then_inc(z_2, 1)
                    if j + 2 < prv:
                        stage(j + 2)
                if n:
                    v.tensor_scalar(zr[:, 0, 0:n], mv[:, 0:n, 1], 1.0 + EPS, EPS * EPS, ALU.mult, ALU.add).then_inc(z_u, 1)

            OWNC = 5 + 4 + 2 * 4

            def update_chunk(c, par, n, nxt, prv):
                cbase, cn = made[0], [0]

                def own_c(ins):
                    ins.then_inc(dv, 1)
                    cn[0] += 1
                    at = cbase + cn[0] if isinstance(c, int) else OWNC * c + (loop_base - OWNC + cn[0])
                    dve.wait_ge(dv, at)
                for j in range(nxt):
                    stage_sums(4 * c + 4 + j, j, (lambda: dve.wait_ge(u_ag, 2 * c + 2)) if j == 0 else (lambda: None))
                update_results(c, n, prv, own_c)
                if isinstance(c, int):
                    made[0] += cn[0]
                else:
                    assert cn[0] == OWNC
            for j in range(4):
                stage_sums(j, j)
            dve.wait_ge(n_s, 1)
            dve.wait_ge(n_gb, 32)
            own(v.tensor_reduce(sx[:, 8:9], gam, AX.X, ALU.max, apply_absolute_value=True))
            own(v.tensor_reduce(sx[:, 9:10], bet, AX.X, ALU.max, apply_absolute_value=True))
            own(v.scalar_tensor_tensor(sx[:, 10:11], sx[:, 8:9], float(D) ** 0.5, sx[:, 9:10], ALU.mult, ALU.add))
            scale(g_z, sx[:, 10:11])
            scale(g_1, frs[:, 0:1])
            scale(g_2, frs[:, 1:2])
            own(v.tensor_tensor(sx[:, 11:12], sx[:, 8:9], sx[:, 9:10], ALU.add))
            own(v.scalar_tensor_tensor(sx[:, 11:12], sx[:, 11:12], float(D) ** 0.5, frs[:, 0:1], ALU.mult, ALU.mult))
            own(v.tensor_tensor(sx[:, 11:12], sx[:, 11:12], frs[:, 2:3], ALU.add))
            scale(g_h, sx[:, 11:12])
            own(v.tensor_tensor(sx[:, 12:13], g_z, g_1, ALU.mult))
            own(v.tensor_tensor(g_o, g_h, g_2, ALU.mult))
            own(v.reciprocal(un1, sx[:, 12:13]))
            own(v.reciprocal(un2, g_o))
            update_chunk(0, 0, 4, 4, 0)
            dve.sem_inc(z_2, 1)
            loop_base = made[0]
            pair_chunks(dve, update_chunk)
            made[0] = loop_base + OWNC * (NCH - 2)
            update_chunk(NCH - 1, (NCH - 1) % 2, 4, 1, 4)
            update_chunk(NCH, NCH % 2, 1, 0, 4)
            dve.wait_ge(z_u, NCH + 1)
            update_results(NCH + 1, 0, 1, own)
            dve.wait_ge(z_le, W + 1)
            own(v.tensor_tensor(lg[:, :, :], lg[:, :, :], brb[:, :].unsqueeze(1).broadcast_to([128, W, NX]), ALU.add))

            bc = lambda a: a.unsqueeze(2).broadcast_to([128, W, NX])
            rio = riota[:, :].unsqueeze(1).broadcast_to([128, W, NX])

            def pick(logits, value, hot, scratch, first):
                own(v.tensor_reduce(value, logits, AX.X, ALU.max))
                own(v.tensor_tensor(scratch, logits, bc(value), ALU.is_equal))
                own(v.tensor_tensor(scratch, scratch, rio, ALU.mult))
                own(v.tensor_reduce(first, scratch, AX.X, ALU.max))
                own(v.tensor_tensor(hot, rio, bc(first), ALU.is_equal))
            pick(lg[:, :, :], rs[:, 0, :], rt[:, 0], rt[:, 2], rs[:, 7, :])
            own(v.tensor_scalar(rt[:, 2], rt[:, 0], -1.0, 1.0, ALU.mult, ALU.add))
            own(v.tensor_tensor(rt[:, 2], rt[:, 2], lg[:, :, :], ALU.mult))
            own(v.scalar_tensor_tensor(rt[:, 3].rearrange("p a b -> p (a b)"), rt[:, 0].rearrange("p a b -> p (a b)"), -3.0e38,
                                       rt[:, 2].rearrange("p a b -> p (a b)"), ALU.mult, ALU.add))
            pick(rt[:, 3], rs[:, 1, :], rt[:, 1], rt[:, 2], rs[:, 7, :])
            v.tensor_tensor(rs[:, 2, :], rs[:, 1, :], rs[:, 0, :], ALU.subtract).then_inc(z_gap, 1)

            for k in range(2):
                own(v.tensor_copy(m2[:, :, k * W:(k + 1) * W], rt[:, k].rearrange("p w e -> p e w")))
            m2f, s2f = (q.rearrange("p e a -> p (e a)") for q in (m2, s2))
            own(v.tensor_tensor_scan(s2f, m2f, m2f, 0.0, ALU.add, ALU.max))
            own(v.tensor_copy(pr[:, 0, :], s2[:, :, 2 * W - 1]))
            own(v.tensor_copy(pr[:, 1, 0:1], pr[:, 0, 0:1]))
            v.tensor_tensor(pr[:, 1, 1:NX], pr[:, 0, 1:NX], pr[:, 0, 0:NX - 1], ALU.subtract).then_inc(r_cnt, 1)
            dve.wait_ge(z_ex, 1)
            own(v.tensor_scalar(rs[:, 4, :], rs[:, 3, :], 1.0, None, ALU.add))
            own(v.reciprocal(rs[:, 5, :], rs[:, 4, :]))
            own(v.tensor_tensor(rs[:, 6, :], rs[:, 5, :], rs[:, 3, :], ALU.mult))
            dve.wait_ge(r_tot, 1)
            own(v.tensor_scalar(sxi[:, 0:NX], ps[6][:, 0:NX], 127.0, None, ALU.add))
            own(v.tensor_scalar(sxi[:, 0:NX], sxi[:, 0:NX], 7, None, ALU.logical_shift_right))
            own(v.tensor_copy(pr[:, 2, :], sxi[:, 0:NX]))
            own(v.tensor_tensor_scan(pr[:, 3, :], pr[:, 2, :], pr[:, 2, :], 0.0, ALU.add, ALU.max))
            own(v.tensor_tensor(pr[:, 4, :], pr[:, 3, :], pr[:, 2, :], ALU.subtract))
            own(v.scalar_tensor_tensor(pr[:, 5, :], pr[:, 4, :], 128.0, ps[6][:, 32:32 + NX], ALU.mult, ALU.add))
            own(v.tensor_tensor(pr[:, 5, :], pr[:, 5, :], pr[:, 0, :], ALU.subtract))
            own(v.scalar_tensor_tensor(pr[:, 5, :], pr[:, 5, :], -1.0, pr[:, 1, :], ALU.add, ALU.add))
            own(v.tensor_tensor(s2, s2, pr[:, 5, :].unsqueeze(2).broadcast_to([128, NX, 2 * W]), ALU.add))
            own(v.tensor_tensor(s2, s2, m2, ALU.mult))
            own(v.tensor_reduce(slot_f, s2.rearrange("p e a -> p a e"), AX.X, ALU.add))
            own(v.tensor_copy(slot_i[:, :], slot_f))
            v.tensor_copy(carried[:, :, 0], place[:, :, :].rearrange("p k w -> p (k w)"))
            v.tensor_copy(carried[:, :, 1], rs[:, 5:7, :].rearrange("p k w -> p (k w)"))
            own(v.tensor_scalar(low_i[:, :], slot_i[:, :], 127, None, ALU.bitwise_and))
            own(v.tensor_scalar(slot_i[:, :], slot_i[:, :], 7, None, ALU.logical_shift_right))
            v.tensor_copy(part_f[:, 0, :], low_i[:, :])
            own(v.tensor_copy(part_f[:, 1, :], slot_i[:, :]))
            own(v.memset(etab[:, :], 0.0))
            for e in range(NX - 1):
                own(v.scalar_tensor_tensor(etab[:, :], tile_no[:, :], pr[:, 3, e:e + 1], etab[:, :], ALU.is_ge, ALU.add))
            assert NX == RING == 8
            by_round = etab[:, :].rearrange("p (i j) -> p i j", j=RING)
            own(v.tensor_copy(ep[:, :], by_round[:, :, 0]))
            for j in range(1, RING):
                own(v.scalar_tensor_tensor(ep[:, :], by_round[:, :, j], float(NX ** j), ep[:, :], ALU.mult, ALU.add))
            v.tensor_copy(ep_i[:, :], ep[:, :]).then_inc(r_et, 1)
            dve.wait_ge(r_et, 1)
            dve.wait_ge(b_in, 16)
            own(v.tensor_scalar(b2s[0:NX, :], b2s[0:NX, :], g_o[0:NX, :], None, ALU.mult))
            own(v.tensor_copy(b2p[0][0:NX, :], b2s[0:NX, :]))
            own(v.tensor_tensor(b2s[0:NX, :], b2s[0:NX, :], b2p[0][0:NX, :], ALU.subtract))
            own(v.tensor_copy(b2p[1][0:NX, :], b2s[0:NX, :]))
            v.tensor_tensor(b2p[2][0:NX, :], b2s[0:NX, :], b2p[1][0:NX, :], ALU.subtract).then_inc(b_p, 1)
            for n in range(2 * W):
                if n >= 4:
                    dve.wait_ge(r_put, n - 3)
                v.tensor_scalar(row_hot[:, n % 4, :], iota[:, :], part_f[:, 0, n:n + 1], None, ALU.is_equal)
                v.scalar_tensor_tensor(tile_val[:, n % 4, :].rearrange("p (a b) -> p a b", a=2),
                                       tile_no[:, 0:NTE].unsqueeze(1).broadcast_to([128, 2, NTE]), part_f[:, 1, n:n + 1],
                                       carried[:, n, :].unsqueeze(2).broadcast_to([128, 2, NTE]),
                                       ALU.is_equal, ALU.mult).then_inc(r_hot, 1)
            dve.wait_ge(r_put, 2 * W)
            found = ps[7][:, 0:NTE]
            own(v.scalar_tensor_tensor(pad_of, found, 0.5, padm[:, :], ALU.is_lt, ALU.mult))
            v.scalar_tensor_tensor(at_tile[:, :, 1], found, -1.0, pad_of, ALU.add, ALU.add)
            own(v.tensor_scalar(bare, found, -1.0, 0.0, ALU.add, ALU.max))
            own(v.tensor_scalar(at_tile[:, :, 0], bare, 1, None, ALU.logical_shift_right))
            own(v.tensor_copy(weight[:, :], ps[7][:, NTE:2 * NTE]))

            def indices(T, i, j):
                if static_ge(i, 1):
                    dve.wait_ge(x_sc[j], 16 * i)
                at_t = at_tile[:, T, :] if isinstance(T, int) else at_tile[:, ds(T, 1), :].rearrange("p a b -> p (a b)")
                v.tensor_scalar(at_ring[:, j, :], at_t, 0, None, ALU.add).then_inc(x_at, 1)
            for T in range(AHEAD):
                indices(T, 0, T)

            def rows_T(T, j):
                dve.wait_ge(x_tr, T + 1)
                if static_ge(T, 2):
                    dve.wait_ge(x_h, T - 1)
                v.tensor_copy(zT[:, j % 2].rearrange("p a b -> p (a b)"),
                              ps[j % 2][:, 0:D].bitcast(F16)).then_inc(x_te, 1)

            def split_and_weigh(T, i, j):
                if not (isinstance(T, int) and T + AHEAD >= NTE):
                    indices(T + AHEAD, i + (j + AHEAD) // RING, (j + AHEAD) % RING)
                if not (isinstance(T, int) and T + 2 >= NTE):
                    rows_T(T + 2, j)
                dve.wait_ge(x_g, T + 1)
                if static_ge(T, 2):
                    dve.wait_ge(x_o, T - 1)
                one, two = (hp[:, j % 2, s * KH:(s + 1) * KH].rearrange("p a b -> p (a b)") for s in range(2))
                v.tensor_scalar(one, h32[:, j % 2, :], g_h, None, ALU.mult).then_inc(x_h1, 1)
                dve.wait_ge(x_h1, T + 1)
                v.scalar_tensor_tensor(two, h32[:, j % 2, :], g_h, one, ALU.mult, ALU.subtract).then_inc(x_h2, 1)
                if static_ge(T, 1):
                    weigh(T - 1, i if j else i - 1, (j - 1) % RING)

            def weigh(T, i, j):
                dve.wait_ge(x_o, T + 1)
                if static_ge(T, RING) and static_ge(i, 1):
                    dve.wait_ge(x_sc[j], 16 * i)
                v.tensor_scalar(yo[:, j, :], ps[4 + j % 2][:, 0:D], weight[:, T:T + 1] if isinstance(T, int) else weight[:, ds(T, 1)], un2,
                                ALU.mult, ALU.mult).then_inc(x_y, 1)
            rows_T(0, 0)
            rows_T(1, 1)
            ring(dve, split_and_weigh)
            weigh(NTE - 1, (NTE - 1) // RING, (NTE - 1) % RING)

            for n in range(5):
                dve.wait_ge(y_ld[n], 16)
                part = xs[:, 5 * n:5 * n + 5, :]
                own(v.tensor_tensor(part, part, y_in[:, 5 * n:5 * n + 5, 0, :], ALU.add))
                v.tensor_tensor(part, part, y_in[:, 5 * n:5 * n + 5, 1, :], ALU.add).then_inc(y_ad, 1)

        @block.tensor
        def _(pe):
            mm = nc.tensor.matmul
            pe.wait_ge(s_cst, 18)
            pe.wait_ge(s_cnt, 1)
            cnt = sq_rows[0:EP, W:2 * W]
            mm(ps[6][:, 0:W], ones[0:EP, :], cnt, start=True, stop=True)
            mm(ps[6][0:EP, 32:32 + W], before[0:EP, 0:EP], cnt, start=True, stop=True).then_inc(s_tot, 1)

            def degrees(c):
                pe.wait_ge(s_oh, 2 * c + 2)
                for n in range(CH):
                    ins = mm(ps[4][:, 0:W], oh_lo[0:EP, n, :], oh_hi[0:EP, n, :], start=(isinstance(c, int) and c == 0 and n == 0),
                             stop=(isinstance(c, int) and c == W - 1 and n == CH - 1), skip_group_check=True)
                ins.then_inc(s_hist, 1)
            for c in range(LEAD):
                degrees(c)
            pe.wait_ge(s_f, 1)

            def node_tile(k, par):
                pe.wait_ge(s_xst, k + 1)
                if static_ge(k, 1):
                    pe.wait_ge(s_xT, 2 * k)
                for m in range(KD):
                    ins = nc.tensor.transpose(ps[0][:, m * 128:(m + 1) * 128], xstage[:, m * 128:(m + 1) * 128], ident[:, :])
                ins.then_inc(s_tp, 1)
                pe.wait_ge(s_xT, 2 * k + 1)
                for q in range(2):
                    if static_ge(k, 1):
                        pe.wait_ge(s_pq2, 2 * k - 1 + q)
                    for m in range(KD):
                        ins = mm(ps[1 + q][:, :], xTst[:, m, :], wAB[:, KD * q + m, :], start=(m == 0), stop=(q == 1 and m == KD - 1))
                    if q == 0:
                        ins = mm(ps[1][:, :], ones[0:1, :], b1row[0:1, :], start=False, stop=True)
                    ins.then_inc(s_pq, 1)

            for c in range(LEAD, EVEN):
                node_tile(2 * (c - LEAD), 0)
                degrees(c)
                node_tile(2 * (c - LEAD) + 1, 1)
            with pe.Fori(EVEN // 2, W // 2) as i:
                for par in range(2):
                    node_tile(2 * i + par, par)
                    degrees(2 * i + par)
            node_tile(W - 1, 0)
            degrees(W - 1)
            pe.wait_ge(n_r, 1)
            mm(ps[6][:, 64:67], ones[:, :], sx[:, 12:15], start=True, stop=True).then_inc(n_t, 1)

            def transposes(par):
                tb = ps[7][:, :].bitcast(BF16)
                for j in range(4):
                    nc.tensor.transpose(tb[:, j * 128:(j + 1) * 128], rec6[:, par, j, :], identb[:, :])
                for j in range(4):
                    ins = nc.tensor.transpose(tb[:, (4 + j) * 128:(5 + j) * 128], oh[:, 4 * par + j, :], identb[:, :])
                ins.then_inc(e_tr, 1)

            def group(g, par, first=False):
                pe.wait_ge(e_sp, 4 * g + 4)
                pe.wait_ge(e_oh, 4 * g + 4)
                if not first:
                    pe.wait_ge(e_te, g)
                transposes(par)

            def agg(i, j, first_pairs=False):
                t = 8 * i + j
                pe.wait_ge(e_h2, t + 1)
                if j % 2 == 0 and not first_pairs:
                    pe.wait_ge(e_acc, 4 * i + j // 2 - 1)
                bank = ps[4 + (j // 2) % 2]
                mm(bank[:, :], oh[:, j, :], h1[:, j % 4, :], start=(j % 2 == 0), stop=False)
                mm(bank[:, :], oh[:, j, :], h2[:, j % 4, :], start=False, stop=(j % 2 == 1)).then_inc(e_agg, 1)

            def edge_body(i, last=False):
                for j in range(8):
                    t = 8 * i + j
                    if j % 4 == 0:
                        pe.wait_ge(e_te, 2 * i + 1 + j // 4)
                    if static_ge(i, 1) or j >= 4:
                        pe.wait_ge(e_h2, t - 3)
                    if j % 2 == 0:
                        p = 4 * i + j // 2
                        wi = nc.tensor.value_load(wtab_i[0:1, p:p + 1] if isinstance(p, int) else wtab_i[0:1, ds(p, 1)],
                                                  min_val=0, max_val=W - 1)
                    bank = ps[j % 4][:, :]
                    ohT = trs[:, j // 4, (4 + j % 4) * 128:(5 + j % 4) * 128]
                    mm(bank, trs[0:KE, j // 4, (j % 4) * 128:(j % 4 + 1) * 128], C6[:, :], start=True, stop=False)
                    mm(bank, ohT, P12[:, ds(wi, 1), 0, :].rearrange("p a h -> p (a h)"), start=False, stop=False)
                    mm(bank, ohT, P12[:, ds(wi, 1), 1, :].rearrange("p a h -> p (a h)"), start=False, stop=False)
                    pe.wait_ge(e_q[j], 16 * (i + 1))
                    mm(bank, identb[:, :], qg[:, j, 0:H], start=False, stop=False)
                    mm(bank, identb[:, :], qg[:, j, H:2 * H], start=False, stop=True).then_inc(e_s, 1)
                    if j == 2:
                        group(2 * i + 1, 1)
                    if j == 6 and not last:
                        group(2 * i + 2, 0)
                    if j >= 2:
                        agg(i, j - 2, first_pairs=not static_ge(i, 1) and j - 2 < 4)
                    elif static_ge(i, 1):
                        agg(i - 1, j + 6, first_pairs=False)
            pe.wait_ge(s_wtab, 1)
            pe.wait_ge(s_c6, 96)
            pe.wait_ge(s_pq2, 2 * W)
            group(0, 0, first=True)
            edge_body(0)
            with pe.Fori(1, NT // 8 - 1) as i:
                edge_body(i)
            edge_body(NT // 8 - 1, last=True)
            agg(NT // 8 - 1, 6)
            agg(NT // 8 - 1, 7)

            pe.wait_ge(u_w, 48)
            pe.wait_ge(u_mb, 16)

            def transpose_sums(t):
                pe.wait_ge(u_st, t + 1)
                if static_ge(t, 1):
                    pe.wait_ge(u_ht, t)
                for m in range(KH):
                    ins = nc.tensor.transpose(ps[0][:, m * 128:(m + 1) * 128], hst[:, m * 128:(m + 1) * 128], ident[:, :])
                ins.then_inc(u_tr, 1)

            def z_transpose(t, j):
                pe.wait_ge(z_st, t + 1)
                if static_ge(t, 1):
                    pe.wait_ge(z_le, t + 1)
                for m in range(KD):
                    ins = nc.tensor.transpose(ps[7][:, m * 128:(m + 1) * 128], zst[:, j % 2, m * 128:(m + 1) * 128], ident[:, :])
                ins.then_inc(z_tr, 1)

            def z_logits(t):
                pe.wait_ge(z_te, t + 1)
                for m in range(KD):
                    ins = mm(ps[7][:, D:D + NX], zTst[:, m, :], Wrs[:, m, :], start=(m == 0), stop=(m == KD - 1))
                ins.then_inc(z_lg, 1)

            pe.sem_inc(z_lg, 1)

            def update_chunk(c, par, n, nxt, prv):
                cols = n * 128
                c0 = 512 * c
                nodes = lambda a: a[:, c0:c0 + cols] if isinstance(c, int) else a[:, ds(c0, cols)]
                pe.wait_ge(u_ht, 4 * c + n)
                pe.wait_ge(u_dg, 4 * c + n)
                for m in range(KD):
                    if static_ge(c, 1):
                        pe.wait_ge(u_ae, 2 * c - 1 + m)
                    for k in range(KH):
                        mm(ps[1 + m][:, 0:cols], mW2s[:, k, m * 128:(m + 1) * 128], HT[par][:, k, 0:cols], start=(k == 0), stop=False)
                    mm(ps[1 + m][:, 0:cols], mb2b[:, m * 128:(m + 1) * 128], diag[:, 0:cols], start=False, stop=True).then_inc(u_ag, 1)
                for m in range(KH):
                    if m < nxt:
                        transpose_sums(4 * c + 4 + m)
                    if static_ge(c, 1) or m >= 2:
                        pe.wait_ge(u_ue, 4 * c + m - 1)
                    for k in range(2 * KD):
                        if k == KD and m == 0:
                            pe.wait_ge(u_ae, 2 * c + 2)
                        rhs = nodes(xnT[:, k, :]) if k < KD else aggT[:, k - KD, 0:cols]
                        ins = mm(ps[3 + m % 2][:, 0:cols], uW1s[:, k, m * 128:(m + 1) * 128], rhs, start=(k == 0), stop=(k == 2 * KD - 1))
                    ins.then_inc(u_u, 1)
                for j in range(4):
                    if j < prv:
                        z_transpose(4 * c - 4 + j, j)
                    if j < n:
                        t = 4 * c + j
                        if j == 0:
                            pe.wait_ge(u_ue, 4 * c + 4)
                        if static_ge(c, 1) or j >= 2:
                            pe.wait_ge(u_x, t - 1)
                        for k in range(KH):
                            ins = mm(ps[5 + j % 2][:, 0:D], uT[:, k, j * 128:(j + 1) * 128], uW2s[:, k, :], start=(k == 0), stop=(k == KH - 1))
                        ins.then_inc(u_o, 1)
                    if j < prv:
                        z_logits(4 * c - 4 + j)
            for j in range(4):
                transpose_sums(j)
            update_chunk(0, 0, 4, 4, 0)
            pair_chunks(pe, update_chunk)
            update_chunk(NCH - 1, (NCH - 1) % 2, 4, 1, 4)
            update_chunk(NCH, NCH % 2, 1, 0, 4)
            z_transpose(W - 1, 0)
            z_logits(W - 1)

            pe.wait_ge(r_cnt, 1)
            pe.wait_ge(u_x, W)
            mm(ps[6][:, 0:NX], ones[:, :], pr[:, 1, :], start=True, stop=True)
            mm(ps[6][:, 32:32 + NX], before[:, :], pr[:, 1, :], start=True, stop=True).then_inc(r_tot, 1)

            for n in range(2 * W):
                pe.wait_ge(r_hot, n + 1)
                mm(ps[7][:, 0:2 * NTE], row_hot[:, n % 4, :], tile_val[:, n % 4, :], start=(n == 0), stop=(n == 2 * W - 1)).then_inc(r_put, 1)

            pe.wait_ge(r_et, 1)
            pe.wait_ge(w_b, 2 * NX)
            pe.wait_ge(b_r, 48)

            def rows_T(T, i, j):
                pe.wait_ge(x_in[j], 16 * i + 16)
                if static_ge(T, 2):
                    pe.wait_ge(x_te, T - 1)
                bank = ps[j % 2][:, 0:D].bitcast(F16)
                rows = zt[:, j, 0:D].bitcast(F16)
                for q in range(2 * KD):
                    ins = nc.tensor.transpose(bank[:, q * 128:(q + 1) * 128], rows[:, q * 128:(q + 1) * 128], identh[:, :])
                ins.then_inc(x_tr, 1)

            def first_product(T, j, e):
                pe.wait_ge(x_te, T + 1)
                if static_ge(T, 2):
                    pe.wait_ge(x_g, T - 1)
                for m in range(KH):
                    n = 0
                    for k in range(KD):
                        for sw, sz in ((0, 0), (0, 1), (1, 0)):
                            ins = mm(ps[2 + j % 2][:, m * 128:(m + 1) * 128],
                                     W1p[:, ds(e, 1), sw, k, m * 128:(m + 1) * 128].rearrange("p a b -> p (a b)"),
                                     zT[:, j % 2, sz * KD + k, :], start=(n == 0), stop=(n == 3 * KD - 1))
                            n += 1
                ins.then_inc(x_h, 1)

            def second_product(T, j, e):
                pe.wait_ge(x_h2, T + 1)
                if static_ge(T, 2):
                    pe.wait_ge(x_y, T - 1)
                bank = ps[4 + j % 2][:, 0:D]
                mm(bank, ones3[:, :], b2r[0:3, ds(e, 1), :].rearrange("p a d -> p (a d)"), start=True, stop=False)
                n = 0
                for k in range(KH):
                    for sh, sw in ((0, 0), (1, 0), (0, 1)):
                        n += 1
                        ins = mm(bank, hp[:, j % 2, sh * KH + k, :],
                                 W2p[:, ds(e, 1), sw, k, :].rearrange("p a d -> p (a d)"), start=False, stop=(n == 3 * KH))
                ins.then_inc(x_o, 1)

            def expert_tile(T, i, j):
                if not (isinstance(T, int) and T + 2 >= NTE):
                    rows_T(T + 2, i + (j + 2) // RING, (j + 2) % RING)
                if j == 0:
                    round_now[0] = round_experts(nc.tensor, i)
                    expert[0] = tile_expert(round_now[0], 0)
                if not (isinstance(T, int) and T + 1 >= NTE):
                    expert[j + 1] = (tile_expert(round_now[0], j + 1) if j + 1 < RING
                                     else tile_expert(round_experts(nc.tensor, i + 1), 0))
                    first_product(T + 1, j + 1, expert[j + 1])
                second_product(T, j, expert[j])
            rows_T(0, 0, 0)
            rows_T(1, 0, 1)
            first_product(0, 0, tile_expert(round_experts(nc.tensor, 0), 0))
            round_now = [None]
            expert = [None] * (RING + 1)
            ring(pe, expert_tile)


_INS = ['x', 'src', 'dst', 'edge_attr_16', 'L0_gnn_mW1', 'L0_gnn_mb1', 'L0_gnn_mW2', 'L0_gnn_mb2', 'L0_gnn_uW1',
        'L0_gnn_ub1', 'L0_gnn_uW2', 'L0_gnn_ub2', 'L0_ffn_gamma', 'L0_ffn_beta', 'L0_ffn_Wr', 'L0_ffn_br',
        'L0_ffn_W1', 'L0_ffn_b1', 'L0_ffn_W2', 'L0_ffn_b2']
_OUTS = [((3125, 256), 'float32')]


def kernel(**inputs):
    import numpy as _np
    import concourse.bacc as _bacc
    from concourse import mybir as _mybir
    from concourse.bass_utils import run_bass_kernel_spmd as _run

    nc = _bacc.Bacc("TRN2", target_bir_lowering=False, num_devices=1)
    arrays, args = {}, []
    for name in _INS:
        a = _np.ascontiguousarray(inputs[name])
        arrays[f"in_{name}_dram"] = a
        args.append(nc.dram_tensor(f"in_{name}_dram", a.shape, _mybir.dt.from_np(a.dtype), kind="ExternalInput").ap())
    for i, (shape, dtype) in enumerate(_OUTS):
        dt = _mybir.dt.from_np(_np.dtype(dtype))
        args.append(nc.dram_tensor(f"out_{i}_dram", shape, dt, kind="ExternalOutput").ap())
    build_kernel(nc, *args)
    r = _run(nc, [arrays], core_ids=[0])
    got = tuple(r.results[0][f"out_{i}_dram"] for i in range(len(_OUTS)))
    return got[0]
```
